# Optimizing a Trainium2 kernel written in Bass

```python
import numpy as np
import jax
import jax.numpy as jnp

def _softmax(x, axis=-1):
    return jax.nn.softmax(x, axis=axis)

def _gelu(x):
    return jax.nn.gelu(x, approximate=True)

def _silu(x):
    return jax.nn.silu(x)

def _sigmoid(x):
    return jax.nn.sigmoid(x)

def _layernorm(x, axis=-1, eps=1e-05):
    m = jnp.mean(x, axis=axis, keepdims=True)
    v = jnp.var(x, axis=axis, keepdims=True)
    return (x - m) / jnp.sqrt(v + eps)

def _scatter_add(tgt, idx, src, axis=0):
    return tgt.at[idx].add(src)

def _segment_sum(src, seg, n):
    return jax.ops.segment_sum(src, seg, n)
kernel_name = 'mk_hybrid_d1_jaxref_r8_3c020f'

def setup_inputs(seed: int=0):
    np.random.seed(seed)
    _w = jnp.asarray

    def _L0_attn_a_setup():
        import jax, jax.numpy as jnp
        import numpy as np
        D_MODEL = 128
        D_INNER = 256
        D_STATE = 16
        D_CONV = 4
        DT_RANK = 64
        N_EXPERTS = 8
        TOP_K = 2
        FFN = 512
        EPS = 1e-05

        def rmsnorm(x, w):
            return x * jax.lax.rsqrt(jnp.mean(x * x, axis=-1, keepdims=True) + EPS) * w

        def mamba_block(x, in_proj_w, conv_w, conv_b, x_proj_w, dt_proj_w, dt_proj_b, A_log, D_skip, out_proj_w):
            B, L, _ = x.shape
            xz = x @ in_proj_w
            xi, z = jnp.split(xz, 2, axis=-1)
            xc = jax.lax.conv_general_dilated(xi.transpose(0, 2, 1), conv_w, window_strides=(1,), padding=[(D_CONV - 1, 0)], feature_group_count=D_INNER, dimension_numbers=('NCH', 'OIH', 'NCH'))
            xi = jax.nn.silu(xc.transpose(0, 2, 1) + conv_b)
            dbc = xi @ x_proj_w
            delta = jax.nn.softplus(dbc[..., :DT_RANK] @ dt_proj_w + dt_proj_b)
            Bm = dbc[..., DT_RANK:DT_RANK + D_STATE]
            Cm = dbc[..., DT_RANK + D_STATE:]
            A = -jnp.exp(A_log)

            def step(h, inp):
                d_t, B_t, C_t, x_t = inp
                dA = jnp.exp(d_t[..., None] * A)
                h = dA * h + (d_t * x_t)[..., None] * B_t[:, None, :]
                y = jnp.einsum('ben,bn->be', h, C_t)
                return (h, y)
            h0 = jnp.zeros((B, D_INNER, D_STATE), dtype=x.dtype)
            xs = (delta.transpose(1, 0, 2), Bm.transpose(1, 0, 2), Cm.transpose(1, 0, 2), xi.transpose(1, 0, 2))
            _, ys = jax.lax.scan(step, h0, xs)
            y = ys.transpose(1, 0, 2) + D_skip * xi
            y = y * jax.nn.silu(z)
            return y @ out_proj_w

        def moe_block(x, router_w, Wg, Wu, Wd):
            B, L, D = x.shape
            hs = x.reshape(-1, D)
            router_logits = hs @ router_w
            rw = jax.nn.softmax(router_logits.astype(jnp.float32), axis=-1)
            top_w, sel = jax.lax.top_k(rw, TOP_K)
            top_w = top_w.astype(hs.dtype)
            out = jnp.zeros_like(hs)
            for e in range(N_EXPERTS):
                w_e = jnp.where(sel == e, top_w, 0.0).sum(axis=-1)
                ye = jax.nn.silu(hs @ Wg[e]) * (hs @ Wu[e]) @ Wd[e]
                out = out + w_e[:, None] * ye
            return (out.reshape(B, L, D), router_logits)
        key = jax.random.key(seed)
        ks = jax.random.split(key, 16)
        s = 0.02
        inp = {'hidden_states': jax.random.normal(ks[0], (2, 256, D_MODEL), jnp.float32), 'rms1_w': jnp.ones((D_MODEL,), jnp.float32), 'rms2_w': jnp.ones((D_MODEL,), jnp.float32), 'in_proj_w': jax.random.normal(ks[1], (D_MODEL, 2 * D_INNER), jnp.float32) * s, 'conv_w': jax.random.normal(ks[2], (D_INNER, 1, D_CONV), jnp.float32) * s, 'conv_b': jnp.zeros((D_INNER,), jnp.float32), 'x_proj_w': jax.random.normal(ks[3], (D_INNER, DT_RANK + 2 * D_STATE), jnp.float32) * s, 'dt_proj_w': jax.random.normal(ks[4], (DT_RANK, D_INNER), jnp.float32) * s, 'dt_proj_b': jnp.zeros((D_INNER,), jnp.float32), 'A_log': jnp.log(jnp.tile(jnp.arange(1, D_STATE + 1, dtype=jnp.float32), (D_INNER, 1))), 'D_skip': jnp.ones((D_INNER,), jnp.float32), 'out_proj_w': jax.random.normal(ks[5], (D_INNER, D_MODEL), jnp.float32) * s, 'router_w': jax.random.normal(ks[6], (D_MODEL, N_EXPERTS), jnp.float32) * s, 'Wg': jax.random.normal(ks[7], (N_EXPERTS, D_MODEL, FFN), jnp.float32) * s, 'Wu': jax.random.normal(ks[8], (N_EXPERTS, D_MODEL, FFN), jnp.float32) * s, 'Wd': jax.random.normal(ks[9], (N_EXPERTS, FFN, D_MODEL), jnp.float32) * s}
        return inp
    _L0_attn_a_in = _L0_attn_a_setup()

    def _L0_attn_b_setup():
        import jax, jax.numpy as jnp
        import numpy as np
        from math import sqrt
        N_HEAD = 16
        W_SCALE = 0.02

        def _reference_tuple_inner(x, W_dq, W_uq, W_dkv, W_uk, W_uv, W_o):
            B, T, C = x.shape
            nh = N_HEAD
            hs = C // nh
            n_kvl = W_dkv.shape[0]
            k_eff = (W_dq.T @ W_uq.T @ W_uk).reshape(nh, hs, n_kvl)
            v_eff = jnp.transpose((W_uv.T @ W_o.T).reshape(n_kvl, nh, hs), (1, 0, 2))
            c_kv = x @ W_dkv.T
            q = x @ W_dq.T @ W_uq.T
            q = q.reshape(B, T, nh, hs)
            q_lat = jnp.einsum('bqhd,hdl->bhql', q, k_eff)
            attn = jnp.einsum('bhql,bkl->bhqk', q_lat, c_kv) / sqrt(hs)
            causal = jnp.tril(jnp.ones((T, T), dtype=bool))
            attn = jnp.where(causal[None, None], attn, -jnp.inf)
            attn = jax.nn.softmax(attn, axis=-1)
            y_lat = jnp.einsum('bhqk,bkl->bhql', attn, c_kv)
            y = jnp.einsum('bhql,hld->bqhd', y_lat, v_eff).reshape(B, T, C)
            return (y, c_kv)
        key = jax.random.key(seed)
        ks = jax.random.split(key, 7)
        B, T, C = (2, 256, 128)
        QL, KVL = (64, 64)
        return {'x': jax.random.normal(ks[0], (B, T, C), dtype=jnp.float32), 'W_dq': jax.random.normal(ks[1], (QL, C), dtype=jnp.float32) * W_SCALE, 'W_uq': jax.random.normal(ks[2], (C, QL), dtype=jnp.float32) * W_SCALE, 'W_dkv': jax.random.normal(ks[3], (KVL, C), dtype=jnp.float32) * W_SCALE, 'W_uk': jax.random.normal(ks[4], (C, KVL), dtype=jnp.float32) * W_SCALE, 'W_uv': jax.random.normal(ks[5], (C, KVL), dtype=jnp.float32) * W_SCALE, 'W_o': jax.random.normal(ks[6], (C, C), dtype=jnp.float32) * W_SCALE}
    _L0_attn_b_in = _L0_attn_b_setup()

    def _L0_ffn_setup():
        import jax, jax.numpy as jnp
        import numpy as np
        DIM = 128
        HIDDEN = 384
        SCALE = 1.0 / 127.0

        def _dequant(w_int, dtype):
            return w_int.astype(dtype) * jnp.asarray(SCALE, dtype)
        key = jax.random.key(seed)
        k_x, k_g, k_u, k_d = jax.random.split(key, 4)
        x = jax.random.normal(k_x, (4, 256, DIM), dtype=jnp.float32)
        w_gate = jax.random.randint(k_g, (HIDDEN, DIM), -127, 128, dtype=jnp.int32)
        w_up = jax.random.randint(k_u, (HIDDEN, DIM), -127, 128, dtype=jnp.int32)
        w_down = jax.random.randint(k_d, (DIM, HIDDEN), -127, 128, dtype=jnp.int32)
        return {'x': x, 'w_gate': w_gate, 'w_up': w_up, 'w_down': w_down}
    _L0_ffn_in = _L0_ffn_setup()
    _d = {'L0_attn_a_hidden_states': _L0_attn_a_in['hidden_states'], 'L0_attn_a_rms1_w': _L0_attn_a_in['rms1_w'], 'L0_attn_a_rms2_w': _L0_attn_a_in['rms2_w'], 'L0_attn_a_in_proj_w': _L0_attn_a_in['in_proj_w'], 'L0_attn_a_conv_w': _L0_attn_a_in['conv_w'], 'L0_attn_a_conv_b': _L0_attn_a_in['conv_b'], 'L0_attn_a_x_proj_w': _L0_attn_a_in['x_proj_w'], 'L0_attn_a_dt_proj_w': _L0_attn_a_in['dt_proj_w'], 'L0_attn_a_dt_proj_b': _L0_attn_a_in['dt_proj_b'], 'L0_attn_a_A_log': _L0_attn_a_in['A_log'], 'L0_attn_a_D_skip': _L0_attn_a_in['D_skip'], 'L0_attn_a_out_proj_w': _L0_attn_a_in['out_proj_w'], 'L0_attn_a_router_w': _L0_attn_a_in['router_w'], 'L0_attn_a_Wg': _L0_attn_a_in['Wg'], 'L0_attn_a_Wu': _L0_attn_a_in['Wu'], 'L0_attn_a_Wd': _L0_attn_a_in['Wd'], 'L0_attn_b_W_dq': _L0_attn_b_in['W_dq'], 'L0_attn_b_W_uq': _L0_attn_b_in['W_uq'], 'L0_attn_b_W_dkv': _L0_attn_b_in['W_dkv'], 'L0_attn_b_W_uk': _L0_attn_b_in['W_uk'], 'L0_attn_b_W_uv': _L0_attn_b_in['W_uv'], 'L0_attn_b_W_o': _L0_attn_b_in['W_o'], 'L0_ffn_w_gate': _L0_ffn_in['w_gate'], 'L0_ffn_w_up': _L0_ffn_in['w_up'], 'L0_ffn_w_down': _L0_ffn_in['w_down']}
    _x0 = _d['L0_attn_a_hidden_states']
    _d['L0_attn_a_hidden_states'] = jax.random.normal(jax.random.fold_in(jax.random.key(seed), 1), (4, 512, 128), dtype=_x0.dtype)
    del _x0
    return _d

def reference(L0_attn_a_hidden_states, L0_attn_a_rms1_w, L0_attn_a_rms2_w, L0_attn_a_in_proj_w, L0_attn_a_conv_w, L0_attn_a_conv_b, L0_attn_a_x_proj_w, L0_attn_a_dt_proj_w, L0_attn_a_dt_proj_b, L0_attn_a_A_log, L0_attn_a_D_skip, L0_attn_a_out_proj_w, L0_attn_a_router_w, L0_attn_a_Wg, L0_attn_a_Wu, L0_attn_a_Wd, L0_attn_b_W_dq, L0_attn_b_W_uq, L0_attn_b_W_dkv, L0_attn_b_W_uk, L0_attn_b_W_uv, L0_attn_b_W_o, L0_ffn_w_gate, L0_ffn_w_up, L0_ffn_w_down):

    def _L0_attn_a_ref(hidden_states, rms1_w, rms2_w, in_proj_w, conv_w, conv_b, x_proj_w, dt_proj_w, dt_proj_b, A_log, D_skip, out_proj_w, router_w, Wg, Wu, Wd):
        import jax, jax.numpy as jnp
        import numpy as np
        D_MODEL = 128
        D_INNER = 256
        D_STATE = 16
        D_CONV = 4
        DT_RANK = 64
        N_EXPERTS = 8
        TOP_K = 2
        FFN = 512
        EPS = 1e-05

        def rmsnorm(x, w):
            return x * jax.lax.rsqrt(jnp.mean(x * x, axis=-1, keepdims=True) + EPS) * w

        def mamba_block(x, in_proj_w, conv_w, conv_b, x_proj_w, dt_proj_w, dt_proj_b, A_log, D_skip, out_proj_w):
            B, L, _ = x.shape
            xz = x @ in_proj_w
            xi, z = jnp.split(xz, 2, axis=-1)
            xc = jax.lax.conv_general_dilated(xi.transpose(0, 2, 1), conv_w, window_strides=(1,), padding=[(D_CONV - 1, 0)], feature_group_count=D_INNER, dimension_numbers=('NCH', 'OIH', 'NCH'))
            xi = jax.nn.silu(xc.transpose(0, 2, 1) + conv_b)
            dbc = xi @ x_proj_w
            delta = jax.nn.softplus(dbc[..., :DT_RANK] @ dt_proj_w + dt_proj_b)
            Bm = dbc[..., DT_RANK:DT_RANK + D_STATE]
            Cm = dbc[..., DT_RANK + D_STATE:]
            A = -jnp.exp(A_log)

            def step(h, inp):
                d_t, B_t, C_t, x_t = inp
                dA = jnp.exp(d_t[..., None] * A)
                h = dA * h + (d_t * x_t)[..., None] * B_t[:, None, :]
                y = jnp.einsum('ben,bn->be', h, C_t)
                return (h, y)
            h0 = jnp.zeros((B, D_INNER, D_STATE), dtype=x.dtype)
            xs = (delta.transpose(1, 0, 2), Bm.transpose(1, 0, 2), Cm.transpose(1, 0, 2), xi.transpose(1, 0, 2))
            _, ys = jax.lax.scan(step, h0, xs)
            y = ys.transpose(1, 0, 2) + D_skip * xi
            y = y * jax.nn.silu(z)
            return y @ out_proj_w

        def moe_block(x, router_w, Wg, Wu, Wd):
            B, L, D = x.shape
            hs = x.reshape(-1, D)
            router_logits = hs @ router_w
            rw = jax.nn.softmax(router_logits.astype(jnp.float32), axis=-1)
            top_w, sel = jax.lax.top_k(rw, TOP_K)
            top_w = top_w.astype(hs.dtype)
            out = jnp.zeros_like(hs)
            for e in range(N_EXPERTS):
                w_e = jnp.where(sel == e, top_w, 0.0).sum(axis=-1)
                ye = jax.nn.silu(hs @ Wg[e]) * (hs @ Wu[e]) @ Wd[e]
                out = out + w_e[:, None] * ye
            return (out.reshape(B, L, D), router_logits)
        residual = hidden_states
        h = rmsnorm(hidden_states, rms1_w)
        h = mamba_block(h, in_proj_w, conv_w, conv_b, x_proj_w, dt_proj_w, dt_proj_b, A_log, D_skip, out_proj_w)
        h = residual + h
        residual = h
        h = rmsnorm(h, rms2_w)
        h, router_logits = moe_block(h, router_w, Wg, Wu, Wd)
        h = residual + h
        return h

    def _L0_attn_b_ref(x, W_dq, W_uq, W_dkv, W_uk, W_uv, W_o):
        import jax, jax.numpy as jnp
        import numpy as np
        from math import sqrt
        N_HEAD = 16
        W_SCALE = 0.02

        def _reference_tuple_inner(x, W_dq, W_uq, W_dkv, W_uk, W_uv, W_o):
            B, T, C = x.shape
            nh = N_HEAD
            hs = C // nh
            n_kvl = W_dkv.shape[0]
            k_eff = (W_dq.T @ W_uq.T @ W_uk).reshape(nh, hs, n_kvl)
            v_eff = jnp.transpose((W_uv.T @ W_o.T).reshape(n_kvl, nh, hs), (1, 0, 2))
            c_kv = x @ W_dkv.T
            q = x @ W_dq.T @ W_uq.T
            q = q.reshape(B, T, nh, hs)
            q_lat = jnp.einsum('bqhd,hdl->bhql', q, k_eff)
            attn = jnp.einsum('bhql,bkl->bhqk', q_lat, c_kv) / sqrt(hs)
            causal = jnp.tril(jnp.ones((T, T), dtype=bool))
            attn = jnp.where(causal[None, None], attn, -jnp.inf)
            attn = jax.nn.softmax(attn, axis=-1)
            y_lat = jnp.einsum('bhqk,bkl->bhql', attn, c_kv)
            y = jnp.einsum('bhql,hld->bqhd', y_lat, v_eff).reshape(B, T, C)
            return (y, c_kv)
        return _reference_tuple_inner(x, W_dq, W_uq, W_dkv, W_uk, W_uv, W_o)[0]

    def _L0_ffn_ref(x, w_gate, w_up, w_down):
        import jax, jax.numpy as jnp
        import numpy as np
        DIM = 128
        HIDDEN = 384
        SCALE = 1.0 / 127.0

        def _dequant(w_int, dtype):
            return w_int.astype(dtype) * jnp.asarray(SCALE, dtype)
        wg = _dequant(w_gate, x.dtype)
        wu = _dequant(w_up, x.dtype)
        wd = _dequant(w_down, x.dtype)
        gate = jnp.einsum('bsd,hd->bsh', x, wg)
        up = jnp.einsum('bsd,hd->bsh', x, wu)
        h = jax.nn.silu(gate) * up
        return jnp.einsum('bsh,dh->bsd', h, wd)
    x = L0_attn_a_hidden_states
    x = x + _L0_attn_a_ref(_layernorm(x, axis=-1), L0_attn_a_rms1_w, L0_attn_a_rms2_w, L0_attn_a_in_proj_w, L0_attn_a_conv_w, L0_attn_a_conv_b, L0_attn_a_x_proj_w, L0_attn_a_dt_proj_w, L0_attn_a_dt_proj_b, L0_attn_a_A_log, L0_attn_a_D_skip, L0_attn_a_out_proj_w, L0_attn_a_router_w, L0_attn_a_Wg, L0_attn_a_Wu, L0_attn_a_Wd)
    x = x + _L0_ffn_ref(_layernorm(x, axis=-1), L0_ffn_w_gate, L0_ffn_w_up, L0_ffn_w_down)
    x = x + _L0_attn_b_ref(_layernorm(x, axis=-1), L0_attn_b_W_dq, L0_attn_b_W_uq, L0_attn_b_W_dkv, L0_attn_b_W_uk, L0_attn_b_W_uv, L0_attn_b_W_o)
    x = x + _L0_ffn_ref(_layernorm(x, axis=-1), L0_ffn_w_gate, L0_ffn_w_up, L0_ffn_w_down)
    return x

_drawn_inputs = setup_inputs


def setup_inputs(seed=0):
    import zlib

    import numpy as np

    out = dict(_drawn_inputs(seed))
    spreads = {'L0_attn_a_rms1_w': (1.0, 0.6),
     'L0_attn_a_rms2_w': (1.0, 0.6),
     'L0_attn_a_conv_b': (0.0, 0.8),
     'L0_attn_a_dt_proj_b': (0.0, 0.8),
     'L0_attn_a_D_skip': (1.0, 0.6)}
    factors = {'L0_attn_a_in_proj_w': 8.0,
     'L0_attn_a_conv_w': 8.0,
     'L0_attn_a_x_proj_w': 8.0,
     'L0_attn_a_dt_proj_w': 8.0,
     'L0_attn_a_A_log': 8.0,
     'L0_attn_a_out_proj_w': 8.0,
     'L0_attn_a_router_w': 8.0,
     'L0_attn_a_Wg': 8.0,
     'L0_attn_a_Wu': 8.0,
     'L0_attn_a_Wd': 8.0,
     'L0_attn_b_W_dq': 35.261,
     'L0_attn_b_W_uq': 34.811,
     'L0_attn_b_W_dkv': 36.417,
     'L0_attn_b_W_uk': 35.139,
     'L0_attn_b_W_uv': 34.668,
     'L0_attn_b_W_o': 34.664}
    for name, (base, spread) in spreads.items():
        noise = np.random.default_rng([zlib.crc32(name.encode()), seed]).standard_normal(out[name].shape)
        drawn = base * np.exp(spread * noise) if base else spread * noise
        out[name] = jnp.asarray(drawn.astype(out[name].dtype))
    for name, factor in factors.items():
        out[name] = (out[name] * factor).astype(out[name].dtype)
    return out
```

```python
from contextlib import ExitStack

import concourse.bass as bass
from concourse import mybir

F32 = mybir.dt.float32
BF16 = mybir.dt.bfloat16
I32 = mybir.dt.int32
U32 = mybir.dt.uint32
ALU = mybir.AluOpType
ACT = mybir.ActivationFunctionType
AX = mybir.AxisListType.X

P = 128
EPS = 1e-5
NEG = -1.0e38


class Chain:

    def __init__(self, eng, sem):
        self.eng, self.sem, self.n = eng, sem, 0

    def link(self, ins):
        self.n += 1
        ins.then_inc(self.sem, 1)
        self.eng.wait_ge(self.sem, self.n)


def build(nc, x_in, rms1_w, rms2_w, in_proj_w, conv_w, conv_b, x_proj_w, dt_proj_w, dt_proj_b,
          A_log, D_skip, out_proj_w, router_w, Wg, Wu, Wd, W_dq, W_uq, W_dkv, W_uk, W_uv, W_o,
          w_gate, w_up, w_down, out):
    NB, L, D = x_in.shape
    NT = NB * L // P
    TB = L // P
    DI = in_proj_w.shape[1] // 2
    CT = DI // P
    NS = A_log.shape[1]
    DC = conv_w.shape[2]
    RK = dt_proj_w.shape[0]
    NE, _, FF = Wg.shape
    FT = FF // P
    HID = w_gate.shape[0]
    HT = HID // P
    QL, KVL = W_dq.shape[0], W_dkv.shape[0]
    NH, HS = 16, D // 16
    HG = 4
    HB = 2
    HL = HB * L
    QS = float(HS) ** -0.5
    DQ = 1.0 / 127.0
    assert D == P and L == 512 and CT == 2 and FT == 4 and NH == HG * 4

    xd = x_in.rearrange("b (j p) d -> b p j d", p=P)
    od = out.rearrange("b (j p) d -> b p j d", p=P)

    ctx = ExitStack()
    with ctx:
        def sb(name, shape, dt=F32):
            return ctx.enter_context(nc.sbuf_tensor(name, shape, dt))

        def sem(name):
            return ctx.enter_context(nc.semaphore(name))

        ps = ctx.enter_context(nc.psum_tensor("ps", [P, 8, 512], F32))

        def bank(k, n=1):
            return ps[:, k, :] if n == 1 else ps[:, k:k + n, :]

        x = sb("x", [P, NT, D])
        r = sb("r", [P, NT, D])
        nb = sb("nb", [P, 2, TB, D])
        xT = sb("xT", [P, 2, L])
        stats = sb("stats", [P, NT, 6])
        mv = sb("mv", [P, NT, 2])
        small = sb("small", [P, 4, NT])
        ident = sb("ident", [P, P])
        cmask = sb("cmask", [P, L])
        identb = sb("identb", [P, P], BF16)
        kmask = sb("kmask", [P, P], BF16)
        neghalf = sb("neghalf", [P, NT])
        moew = sb("moew", [P, 2, 3, FF])
        wgT = sb("wgT", [P, HID])
        wuT = sb("wuT", [P, HID])
        wdT = sb("wdT", [P, HT, D])
        wqm = sb("wqm", [P, HG, D])
        mT = sb("mT", [P, D])
        vx = sb("vx", [P, D])
        hmask = sb("hmask", [P, HG])
        hone = sb("hone", [P, HG])
        w1c = sb("w1c", [P, 1])
        w2c = sb("w2c", [P, 1])
        rw = sb("rw", [P, NE])
        wtok = sb("wtok", [P, NT, NE])
        iota8 = sb("iota8", [P, NE])
        wqq = sb("wqq", [P, D])
        junk_r = sb("junk_r", [P, 2 * TB])
        rmax = sb("rmax", [P, 2 * TB, 8])
        ridx = sb("ridx", [P, 2 * TB, 8], U32)
        req = sb("req", [P, 2, 2 * TB, NE])

        ARENA = 35 * 1024
        arena = sb("arena", [P, ARENA])
        at = [0]

        def carve(shape, dt=F32):
            n = 1
            for s in shape:
                n *= s
            words = n if dt != BF16 else n // 2
            a = arena[:, at[0]:at[0] + words]
            at[0] += words
            assert at[0] <= ARENA, at[0]
            if dt != F32:
                a = a.bitcast(dt)
            names = " ".join(f"a{i}" for i in range(len(shape)))
            if len(shape) == 1:
                return a
            return a.rearrange(f"p ({names}) -> p {names}", **{f"a{i}": s for i, s in enumerate(shape)})

        ipw = carve([2 * DI])
        xpw = carve([CT, RK])
        bcw = carve([CT, 3, 2 * NS])
        dtw = carve([DI])
        opw = carve([CT, D])
        convw = carve([CT, DC])
        convb = carve([CT])
        dtb = carve([CT])
        dsk = carve([CT])
        aneg = carve([CT, NS])
        convd = carve([CT, DC, P])
        dskd = carve([CT, P])
        sel = carve([2 * NS, P], BF16)
        selr = carve([2 * NS])
        h2T = carve([NB, L])
        moe_from = at[0]
        xip = carve([HB, CT, L + 4])
        xc = carve([CT, HL])
        zs = carve([CT, HL])
        delta = carve([CT, HL])
        dx = carve([CT, HL])
        dts = carve([HB, L])
        bc3 = carve([HL], BF16)
        scan_from = at[0]
        v = carve([HB, CT, L])
        u = carve([HB, CT, L])
        bcr = carve([HB, L])
        bcm = carve([HB, L], BF16)
        v_to = at[0]
        at[0] = scan_from
        bs = carve([2, HL])
        dA = carve([2, CT, HL])
        dBx = carve([2, CT, HL])
        hst = carve([CT, HL])
        hC = carve([CT, HL])
        assert v_to <= at[0]
        at[0] = scan_from
        wint = carve([3, HID], I32)
        wflt = carve([3, HID])
        adq, auq, adkv, auk, auv, ao = (carve([P]) for _ in range(6))
        auqT, aoT, aqqT, akT, av = (carve([P]) for _ in range(5))
        at[0] = moe_from
        sg = carve([2, L])
        hh = carve([2, FT, L])
        at[0] = 0
        fsg = carve([2, L])
        fhh = carve([2, HT, L])
        at[0] = 0
        qm = carve([HG, L])
        qa = carve([2, HG, L])
        km = carve([2, HG, L])
        vv = carve([2, TB, NH, 32])
        pt = carve([2, HG, L])
        ot = carve([HG, L])
        zm = carve([TB, HG, P])
        junk = carve([2, L])
        rs = carve([TB, NH])
        yn = carve([TB, D])

        s_x = [sem(f"x_loaded{b}") for b in range(NB)]
        s_w = sem("mamba_weights_loaded")
        s_aw = sem("attn_ffn_weights_loaded")
        s_out = sem("out_stored")
        s_dch = sem("dve_chain")
        s_ach = sem("act_chain")
        s_pch = sem("pool_chain")
        s_const = sem("constants_ready")
        s_dconst = sem("dve_constants_ready")
        s_wflt = sem("ffn_weights_float")
        s_wp = sem("weight_prep_matmul")
        s_wpc = sem("weight_prep_copied")
        s_var = sem("variance_ready")
        s_rstd = sem("rstd_ready")
        s_nb = sem("tokens_normalised")
        s_tr = sem("transposed")
        s_xT = sem("xT_ready")
        s_ip = sem("in_proj_done")
        s_xi = sem("xi_ready")
        s_zs = sem("z_ready")
        s_cv = sem("conv_done")
        s_xc = sem("xc_ready")
        s_pj = sem("x_proj_done")
        s_dts = sem("dt_ready")
        s_bc3 = sem("bc_split_ready")
        s_dtp = sem("dt_proj_done")
        s_v = sem("softplus_input_ready")
        s_aexp = sem("exp_A_ready")
        s_vv0 = sem("attn_buffers_cleared")
        s_rs = sem("reciprocal_sum_ready")
        s_u = sem("softplus_log_ready")
        s_dl = sem("delta_ready")
        s_dx = sem("dx_ready")
        s_bps = sem("b_broadcast_done")
        s_cps = sem("c_broadcast_done")
        s_bs = sem("b_copied")
        s_da = sem("dA_ready")
        s_dbx = sem("dBx_ready")
        s_scan = sem("scan_done")
        s_hc = sem("hC_ready")
        s_ys = sem("y_summed")
        s_yg = sem("y_gated")
        s_op = sem("out_proj_done")
        s_r = sem("residual_ready")
        s_h2 = sem("h2_ready")
        s_tr2 = sem("h2_transposed")
        s_h2T = sem("h2T_ready")
        s_rt = sem("router_done")
        s_rx = sem("router_shifted")
        s_re = sem("router_exp")
        s_wt = sem("router_weights_ready")
        s_mw = [sem(f"expert_loaded{k}") for k in range(2)]
        s_g = sem("gate_done")
        s_u2 = sem("up_done")
        s_sg = sem("silu_done")
        s_hm = sem("hidden_ready")
        s_dn = sem("down_done")
        s_acc = sem("expert_added")
        s_fx = sem("ffn_input_ready")
        s_fn = sem("ffn_normalised")
        s_ft = sem("ffn_transposed")
        s_fxT = sem("ffn_xT_ready")
        s_fg = sem("ffn_gate_done")
        s_fu = sem("ffn_up_done")
        s_fs = sem("ffn_silu_done")
        s_fh = sem("ffn_hidden_ready")
        s_fd = sem("ffn_down_done")
        s_fa = sem("ffn_added")
        s_an = sem("attn_normalised")
        s_at = sem("attn_transposed")
        s_axT = sem("attn_xT_ready")
        s_aq = sem("attn_q_done")
        s_ak = sem("attn_k_done")
        s_av = sem("attn_v_done")
        s_qm = sem("q_masked")
        s_km = sem("k_masked")
        s_vv = sem("v_ready")
        s_s1 = sem("scores_q_major")
        s_mx = sem("row_max_ready")
        s_zq = sem("q_with_max_done")
        s_qa = sem("q_with_max_ready")
        s_s2 = sem("scores_k_major")
        s_ex = sem("exp_done")
        s_pv = sem("pv_done")
        s_ot = sem("o_copied")
        s_ott = sem("o_transposed")
        s_ya = sem("attn_added")

        block = ctx.enter_context(nc.Block())

        def wait(eng, s, n):
            if not isinstance(n, int) or n > 0:
                eng.wait_ge(s, n)

        def tiles(b):
            return slice(TB * b, TB * b + TB)

        def small_r(h):
            return wtok[:, 2 * TB * h:2 * TB * h + 2 * TB, :]

        loads = [(w1c[:, :], rms1_w.rearrange("(p o) -> p o", o=1)),
                 (w2c[:, :], rms2_w.rearrange("(p o) -> p o", o=1)),
                 (ipw[:, :], in_proj_w), (dtw[0:RK, :], dt_proj_w), (rw[:, :], router_w),
                 (convw[:, :, :], conv_w.rearrange("(e p) o k -> p e (o k)", p=P)),
                 (aneg[:, :, :], A_log.rearrange("(e p) n -> p e n", p=P)),
                 (opw[:, :, :], out_proj_w.rearrange("(e p) d -> p e d", p=P))]
        for e in range(CT):
            rows = x_proj_w[e * P:e * P + P, :]
            loads += [(dst[:, e:e + 1], src[e * P:e * P + P].rearrange("(p o) -> p o", o=1))
                      for dst, src in ((convb, conv_b), (dtb, dt_proj_b), (dsk, D_skip))]
            loads.append((xpw[:, e, :], rows[:, 0:RK]))
            loads += [(bcw[:, e, q, :], rows[:, RK:RK + 2 * NS]) for q in range(3)]

        def turn(rows, cols=P):
            turn.n += 1
            return ps[0:rows, (turn.n - 1) % 8, 0:cols]

        turn.n = 0
        prep = []
        for src, dst in ((0, wgT), (1, wuT), (2, None)):
            for t in range(HT):
                cs = slice(t * P, t * P + P)
                prep.append((turn(P), wflt[:, src, cs], ident[:], True,
                             wdT[:, t, :] if dst is None else dst[:, cs], 0))
        n0 = len(prep)
        prep += [(turn(QL), auq[:, 0:QL], ident[:], True, auqT[0:QL, :], 0),
                 (turn(P), ao[:, :], ident[:], True, aoT[:, :], 0),
                 (turn(P), adq[0:QL, :], auqT[0:QL, :], False, wqq[:], n0 + 1),
                 (turn(P), auqT[0:QL, :], adq[0:QL, :], False, aqqT[:, :], n0 + 1),
                 (turn(KVL), auk[:, 0:KVL], aqqT[:, :], False, akT[0:KVL, :], n0 + 4),
                 (turn(KVL), auv[:, 0:KVL], aoT[:, :], False, av[0:KVL, :], n0 + 2),
                 (turn(P), adkv[0:KVL, :], akT[0:KVL, :], False, mT[:], n0 + 5),
                 (turn(P), adkv[0:KVL, :], av[0:KVL, :], False, vx[:], n0 + 6)]
        NPREP = len(prep)

        @block.sync
        def _(sp):
            sp.sem_inc(s_dbx, 4)
            sp.sem_inc(s_scan, 4)
            sp.sem_inc(s_ys, 2)
            sp.sem_inc(s_hc, 2)
            sp.sem_inc(s_hm, 2)
            sp.sem_inc(s_dn, 8)
            sp.sem_inc(s_acc, 2)
            for b in range(NB):
                sp.dma_start(x[:, tiles(b), :], xd[b]).then_inc(s_x[b], 16)
            for dst, src in (
                (wint[:, 0, :].rearrange("p (t d) -> p t d", t=HT), w_gate.rearrange("(t p) d -> p t d", p=P)),
                (wint[:, 1, :].rearrange("p (t d) -> p t d", t=HT), w_up.rearrange("(t p) d -> p t d", p=P)),
                (wint[:, 2, :], w_down),
                (adq[0:QL, :], W_dq), (auq[:, 0:QL], W_uq), (adkv[0:KVL, :], W_dkv),
                (auk[:, 0:KVL], W_uk), (auv[:, 0:KVL], W_uv), (ao[:, :], W_o),
            ):
                sp.dma_start(dst, src).then_inc(s_aw, 16)
            with sp.Fori(0, NE // 2) as pair:
                e0 = pair * 2
                for k in range(2):
                    sp.wait_ge(s_dn, e0 * 4 + 4 * (k + 1))
                    e = e0 + k
                    for i, w in enumerate((Wg, Wu)):
                        sp.dma_start(moew[:, k, i, :],
                                     w[bass.ds(e, 1), :, :].rearrange("e p f -> (e p) f")).then_inc(s_mw[k], 16)
                    sp.dma_start(moew[:, k, 2, :].rearrange("p (t d) -> p t d", t=FT),
                                 Wd[bass.ds(e, 1), :, :].rearrange("e (t p) d -> p (e t) d", p=P)).then_inc(s_mw[k], 16)
            for b in range(NB):
                sp.wait_ge(s_fa, NB + b + 1)
                sp.dma_start(od[b], x[:, tiles(b), :]).then_inc(s_out, 16)
            sp.wait_ge(s_out, 16 * NB)

        @block.gpsimd
        def _(pool):
            G = nc.gpsimd
            ch = Chain(pool, s_pch)
            G.memset(ident[:], 0.0)
            G.memset(selr[:, :], 0.0)
            G.memset(cmask[:], 0.0)
            G.memset(kmask[:], 0.0)
            G.memset(hmask[:], 0.0)
            G.memset(hone[:], 0.0)
            ch.link(G.memset(neghalf[:], -0.5))
            G.affine_select(out=ident[:], in_=ident[:], compare_op=ALU.not_equal, fill=1.0, base=0,
                            pattern=[[-1, P]], channel_multiplier=1).then_inc(s_const, 1)
            G.affine_select(out=cmask[:, L - P:L], in_=cmask[:, L - P:L], compare_op=ALU.is_ge, fill=NEG,
                            base=0, pattern=[[-1, P]], channel_multiplier=1)
            G.affine_select(out=kmask[:], in_=kmask[:], compare_op=ALU.is_ge, fill=NEG,
                            base=0, pattern=[[1, P]], channel_multiplier=-1)
            G.iota(iota8[:], pattern=[[1, NE]], base=0, channel_multiplier=0,
                   allow_small_or_imprecise_dtypes=True)
            for q in range(3):
                ch.link(G.affine_select(out=selr[:, :], in_=selr[:, :], compare_op=ALU.not_equal, fill=1.0,
                                        base=-2 * NS * q, pattern=[[-1, 2 * NS]], channel_multiplier=1))
            for g in range(4):
                sl = slice(32 * g, 32 * g + 32)
                ch.link(G.memset(hmask[sl, :], 1.0))
                ch.link(G.affine_select(out=hmask[sl, :], in_=hmask[sl, :], compare_op=ALU.is_ge, fill=0.0,
                                        base=0, pattern=[[-HS, HG]], channel_multiplier=1))
                ch.link(G.affine_select(out=hmask[sl, :], in_=hmask[sl, :], compare_op=ALU.is_ge, fill=0.0,
                                        base=HS - 1, pattern=[[HS, HG]], channel_multiplier=-1))
                ch.link(G.affine_select(out=hone[sl, 0:HG - 1], in_=hone[sl, 0:HG - 1], compare_op=ALU.not_equal,
                                        fill=1.0, base=-HS, pattern=[[-HS, HG - 1]], channel_multiplier=1))
                ch.link(G.affine_select(out=hone[sl, HG - 1:HG], in_=hone[sl, HG - 1:HG],
                                        compare_op=ALU.not_equal, fill=1.0, base=0,
                                        pattern=[[-HS, 1]], channel_multiplier=1))
            pool.sem_inc(s_const, 1)

            def powers(n, col, width, src=1):
                pool.wait_ge(s_var, n)
                G.tensor_tensor(small[:, 2, col:col + width], small[:, src, col:col + width],
                                neghalf[:, col:col + width], ALU.pow).then_inc(s_rstd, 1)

            for h in range(HB):
                for c in range(HB):
                    b = HB * h + c
                    powers(5 * h + 2 * c + 1, TB * b, TB)
                    powers(5 * h + 2 * c + 2, TB * b, TB)
                for c in range(HB):
                    pool.wait_ge(s_dl, HB * h + c + 1)
                    G.tensor_tensor(dx[:, :, c * L:c * L + L], delta[:, :, c * L:c * L + L],
                                    xc[:, :, c * L:c * L + L], ALU.mult).then_inc(s_dx, 1)
                pool.wait_ge(s_dx, HB * h + HB)
                with pool.Fori(0, NS // 2) as pair:
                    n0 = pair * 2
                    for k in range(2):
                        n = n0 + (h * NS + k)
                        pool.wait_ge(s_bs, n + 1)
                        for e in range(CT):
                            pool.wait_ge(s_scan, 2 * n + e + 1)
                            G.tensor_tensor(dBx[:, k, e, :], dx[:, e, :], bs[:, k, :],
                                            ALU.mult).then_inc(s_dbx, 1)
                powers(5 * h + 5, 2 * TB * h, 2 * TB)
            for p in range(3):
                for b in range(NB):
                    powers(5 * HB + NB * p + b + 1, TB * b, TB)

        @block.scalar
        def _(act):
            S = nc.scalar
            ch = Chain(act, s_ach)
            for dst, src in loads:
                act.dma_start(dst, src).then_inc(s_w, 16)
            S.preload_act_table(ACT.Exp)
            act.wait_ge(s_w, 16 * len(loads))
            S.activation(aneg[:, :, :], aneg[:, :, :], ACT.Exp).then_inc(s_aexp, 1)

            act.wait_ge(s_aw, 16 * 9)
            S.copy(wflt[:, :, :], wint[:, :, :]).then_inc(s_wflt, 1)

            for h in range(HB):
                for c in range(HB):
                    b = HB * h + c
                    act.wait_ge(s_tr, b + 1)
                    S.activation(xT[:, c, :], bank(c), ACT.Copy, scale=w1c[:, 0:1]).then_inc(s_xT, 1)
                for c in range(HB):
                    b = HB * h + c
                    banks = ((2, 3, 4, 5), (6, 7, 0, 1))[c]
                    for e in range(CT):
                        act.wait_ge(s_ip, 4 * b + e + 1)
                        S.copy(xip[:, c, e, 4:4 + L], bank(banks[e])).then_inc(s_xi, 1)
                    for e in range(CT):
                        act.wait_ge(s_ip, 4 * b + 2 + e + 1)
                        S.activation(zs[:, e, c * L:c * L + L], bank(banks[2 + e]), ACT.Silu).then_inc(s_zs, 1)
                for c in range(HB):
                    b = HB * h + c
                    for e in range(CT):
                        act.wait_ge(s_cv, 2 * b + e + 1)
                        S.activation(xc[:, e, c * L:c * L + L], bank((2, 6)[c] + e), ACT.Silu,
                                     bias=convb[:, e:e + 1]).then_inc(s_xc, 1)
                for c in range(HB):
                    b = HB * h + c
                    act.wait_ge(s_pj, 2 * b + 1)
                    S.copy(dts[0:RK, c, :], ps[0:RK, (4, 0)[c], :]).then_inc(s_dts, 1)
                S.preload_act_table_set("natural_log_exp_and_others")
                for c in range(HB):
                    b = HB * h + c
                    act.wait_ge(s_v, b + 1)
                    ch.link(S.activation(u[:, c, :, :], u[:, c, :, :], ACT.Exp))
                    S.activation(u[:, c, :, :], u[:, c, :, :], ACT.Ln, bias=1.0).then_inc(s_u, 1)
                act.wait_ge(s_dl, HB * h + HB)
                act.wait_ge(s_dx, HB * h + HB)
                with act.Fori(0, NS // 2) as pair:
                    n0 = pair * 2
                    for k in range(2):
                        n = n0 + (h * NS + k)
                        act.wait_ge(s_bps, n + 1)
                        act.wait_ge(s_dbx, 2 * n + 2)
                        S.copy(bs[:, k, :].rearrange("p (c l) -> p c l", c=HB), bank(6, 2)).then_inc(s_bs, 1)
                        for e in range(CT):
                            act.wait_ge(s_scan, 2 * n + e + 1)
                            S.activation(dA[:, k, e, :].rearrange("p (c l) -> p c l", c=HB)[:, :, 1:L],
                                         delta[:, e, :].rearrange("p (c l) -> p c l", c=HB)[:, :, 1:L],
                                         ACT.Exp, scale=aneg[:, e, bass.ds(n0 + k, 1)]).then_inc(s_da, 1)
                for c in range(HB):
                    b = HB * h + c
                    act.wait_ge(s_tr2, b + 1)
                    S.activation(h2T[:, b, :], bank(6 + c), ACT.Copy, scale=w2c[:, 0:1]).then_inc(s_h2T, 1)
                act.wait_ge(s_rx, h + 1)
                S.activation(small_r(h), small_r(h), ACT.Exp).then_inc(s_re, 1)

            act.wait_ge(s_wt, HB)
            S.preload_act_table(ACT.Silu)
            with act.Fori(0, NE // 2) as pair:
                e0 = pair * 2
                for j in range(2 * NB):
                    for f in range(FT):
                        m = e0 * (NB * FT) + (j * FT + f)
                        act.wait_ge(s_g, m + 1)
                        act.wait_ge(s_hm, m + 1)
                        S.activation(sg[:, f % 2, :], bank(f % 2), ACT.Silu).then_inc(s_sg, 1)

            def ffn(p):
                for b in range(NB):
                    q = p * NB + b
                    act.wait_ge(s_ft, q + 1)
                    S.copy(xT[:, b % 2, :], bank(6 + b % 2)).then_inc(s_fxT, 1)
                    for f in range(HT):
                        m = q * HT + f
                        act.wait_ge(s_fg, m + 1)
                        wait(act, s_fh, m - 1)
                        S.activation(fsg[:, m % 2, :], bank(m % 2), ACT.Silu, scale=DQ).then_inc(s_fs, 1)

            ffn(0)

            def project(b):
                act.wait_ge(s_at, b + 1)
                S.copy(xT[:, b % 2, :], bank(7)).then_inc(s_axT, 1)
                act.wait_ge(s_aq, b + 1)
                for i in range(HG):
                    S.activation(qm[:, i, :], bank(7), ACT.Copy, scale=hmask[:, i:i + 1]).then_inc(s_qm, 1)
                act.wait_ge(s_ak, b + 1)
                for i in range(HG):
                    S.activation(km[:, b % 2, i, :], bank(7), ACT.Identity, scale=hmask[:, i:i + 1],
                                 bias=hone[:, i:i + 1]).then_inc(s_km, 1)
                act.wait_ge(s_av, b + 1)
                S.copy(vv[:, b % 2, :, :, 0:HS], bank(7).rearrange("p (t h d) -> p t h d", t=TB, d=HS)).then_inc(s_vv, 1)

            def with_max(b):
                for i in range(HG):
                    act.wait_ge(s_zq, HG * b + i + 1)
                    S.copy(qa[:, b % 2, i, :], bank(7)).then_inc(s_qa, 1)

            def exps(b, i):
                for kt in range(TB):
                    m = (b * HG + i) * TB + kt
                    if m >= 2:
                        act.wait_ge(s_pv, m - 1)
                    for g in range(4):
                        act.wait_ge(s_s2, 4 * m + g + 1)
                        S.activation(pt[:, kt % 2, g, kt * P:L], ps[:, g, kt * P:L], ACT.Exp).then_inc(s_ex, 1)
                act.wait_ge(s_pv, (b * HG + i + 1) * TB)
                wait(act, s_ott, b * TB if i == 0 else 0)
                S.copy(ot[:, i, :], bank(6)).then_inc(s_ot, 1)

            act.wait_ge(s_fa, NB)
            project(0)
            with_max(0)
            for b in range(NB):
                if b + 1 < NB:
                    project(b + 1)
                for i in range(HG):
                    exps(b, i)
                if b + 1 < NB:
                    with_max(b + 1)
            ffn(1)

        @block.vector
        def _(dve):
            V = nc.vector
            ch = Chain(dve, s_dch)
            count = {"var": 0}

            def moments(src, b, n=TB):
                t0 = TB * b
                for j in range(n):
                    last = V.bn_stats(stats[:, t0 + j, :], src[:, t0 + j, :])
                ch.link(last)
                for j in range(n):
                    last = V.bn_aggr(mv[:, t0 + j, :], stats[:, t0 + j, :])
                ch.link(last)

            def power(n):
                count["var"] += 1
                n.then_inc(s_var, 1)
                dve.wait_ge(s_rstd, count["var"])

            def normalise(dst, src, t, rcol):
                return V.tensor_scalar(dst, src, mv[:, t, 0:1], rcol, ALU.subtract, ALU.mult)

            for c in range(HB):
                V.memset(xip[:, c, :, 0:4], 0.0)
            dve.wait_ge(s_const, 2)
            dve.wait_ge(s_w, 16 * len(loads))
            dve.wait_ge(s_aexp, 1)
            V.tensor_scalar(aneg[:, :, :], aneg[:, :, :], -1.0, None, ALU.mult)
            V.tensor_copy(identb[:], ident[:])
            V.tensor_copy(sel[:, :, :], selr[:, :].unsqueeze(2).to_broadcast([P, 2 * NS, P]))
            for e in range(CT):
                for k in range(DC):
                    V.tensor_scalar(convd[:, e, k, :], ident[:], convw[:, e, k:k + 1], None, ALU.mult)
                last = V.tensor_scalar(dskd[:, e, :], ident[:], dsk[:, e:e + 1], None, ALU.mult)
            last.then_inc(s_dconst, 1)
            for n, (src, _, _, _, dst, _) in enumerate(prep):
                dve.wait_ge(s_wp, n + 1)
                if n == NPREP - 2:
                    V.tensor_scalar(dst, src, QS, None, ALU.mult).then_inc(s_wpc, 1)
                else:
                    V.tensor_copy(dst, src).then_inc(s_wpc, 1)
            V.memset(wqm[:, :, :], 0.0).then_inc(s_wpc, 1)
            dve.wait_ge(s_wpc, NPREP + 1)
            for i in range(HG):
                V.tensor_copy(wqm[:, i, :].rearrange("p (g w) -> p g w", w=32)[:, :, HS * i:HS * i + HS],
                              wqq[:].rearrange("p (g w) -> p g w", w=32)[:, :, HS * i:HS * i + HS]
                              ).then_inc(s_wpc, 1)

            for h in range(HB):
                for c in range(HB):
                    b = HB * h + c
                    sl = slice(TB * b, TB * b + TB)
                    dve.wait_ge(s_x[b], 16)
                    moments(x, b)
                    power(V.tensor_scalar(small[:, 1, sl], mv[:, sl, 1], EPS, None, ALU.add))
                    for j in range(TB):
                        t = TB * b + j
                        last = normalise(r[:, t, :], x[:, t, :], t, small[:, 2, t:t + 1])
                    ch.link(last)
                    ch.link(V.tensor_tensor(small[:, 3, sl], small[:, 2, sl], small[:, 2, sl], ALU.mult))
                    ch.link(V.tensor_tensor(small[:, 3, sl], small[:, 3, sl], mv[:, sl, 1], ALU.mult))
                    power(V.tensor_scalar(small[:, 1, sl], small[:, 3, sl], EPS, None, ALU.add))
                    if h:
                        dve.wait_ge(s_tr2, b - 1)
                    for j in range(TB):
                        t = TB * b + j
                        last = V.tensor_scalar(nb[:, c, j, :], r[:, t, :], small[:, 2, t:t + 1], None, ALU.mult)
                    last.then_inc(s_nb, 1)
                for c in range(HB):
                    b = HB * h + c
                    cs = slice(c * L, c * L + L)
                    src = ps[0:96, (5, 1)[c], :]
                    dve.wait_ge(s_pj, 2 * b + 2)
                    ch.link(V.tensor_copy(bc3[0:96, cs], src))
                    ch.link(V.tensor_tensor(bcr[0:96, c, :], src, bc3[0:96, cs], ALU.subtract))
                    ch.link(V.tensor_copy(bcm[0:96, c, :], bcr[0:96, c, :]))
                    V.tensor_copy(bc3[32:64, cs], bcm[32:64, c, :])
                    V.tensor_tensor(bc3[64:96, cs], bcr[64:96, c, :], bcm[64:96, c, :],
                                    ALU.subtract).then_inc(s_bc3, 1)
                for c in range(HB):
                    b = HB * h + c
                    for e in range(CT):
                        dve.wait_ge(s_dtp, 2 * b + e + 1)
                        last = V.tensor_scalar(v[:, c, e, :], bank((2, 6)[c] + e), dtb[:, e:e + 1], None, ALU.add)
                    ch.link(last)
                    V.scalar_tensor_tensor(u[:, c, :, :], v[:, c, :, :], -1.0, v[:, c, :, :],
                                           ALU.mult, ALU.min).then_inc(s_v, 1)
                for c in range(HB):
                    b = HB * h + c
                    dve.wait_ge(s_u, b + 1)
                    V.scalar_tensor_tensor(delta[:, :, c * L:c * L + L], v[:, c, :, :], 0.0, u[:, c, :, :],
                                           ALU.max, ALU.add).then_inc(s_dl, 1)
                dve.wait_ge(s_dl, HB * h + HB)
                for k in range(2):
                    last = V.memset(dA[:, k, :, :].rearrange("p e (c l) -> p (e c) l", c=HB)[:, :, 0:1], 0.0)
                ch.link(last)
                with dve.Fori(0, NS // 2) as pair:
                    n0 = pair * 2
                    for k in range(2):
                        n = n0 + (h * NS + k)
                        for e in range(CT):
                            dve.wait_ge(s_da, 2 * n + e + 1)
                            dve.wait_ge(s_dbx, 2 * n + e + 5)
                            dve.wait_ge(s_hc, 2 * n + e + 1)
                            V.tensor_tensor_scan(hst[:, e, :], dA[:, k, e, :], dBx[:, k, e, :], 0.0,
                                                 ALU.mult, ALU.add).then_inc(s_scan, 1)
                        dve.wait_ge(s_cps, n + 1)
                        for e in range(CT):
                            dve.wait_ge(s_scan, 2 * n + e + 5)
                            dve.wait_ge(s_ys, 2 * n + e + 1)
                            V.tensor_tensor(hC[:, e, :].rearrange("p (c l) -> p c l", c=HB),
                                            hst[:, e, :].rearrange("p (c l) -> p c l", c=HB),
                                            bank(4, 2), ALU.mult).then_inc(s_hc, 1)
                for e in range(CT):
                    dve.wait_ge(s_ys, 2 * NS * (h + 1) + e + 1)
                    V.tensor_tensor(zs[:, e, :].rearrange("p (c l) -> p c l", c=HB), bank(2 * e, 2),
                                    zs[:, e, :].rearrange("p (c l) -> p c l", c=HB), ALU.mult).then_inc(s_yg, 1)
                for c in range(HB):
                    b = HB * h + c
                    dve.wait_ge(s_op, b + 1)
                    V.tensor_tensor(r[:, tiles(b), :], bank(4 + c).rearrange("p (j d) -> p j d", j=TB),
                                    r[:, tiles(b), :], ALU.add).then_inc(s_r, 1)
                dve.wait_ge(s_r, HB * h + HB)
                sl = slice(2 * TB * h, 2 * TB * h + 2 * TB)
                moments(r, HB * h, 2 * TB)
                ch.link(V.tensor_tensor(small[:, 3, sl], mv[:, sl, 0], mv[:, sl, 0], ALU.mult))
                ch.link(V.tensor_tensor(small[:, 3, sl], small[:, 3, sl], mv[:, sl, 1], ALU.add))
                power(V.tensor_scalar(small[:, 1, sl], small[:, 3, sl], EPS, None, ALU.add))
                for c in range(HB):
                    for j in range(TB):
                        t = TB * (HB * h + c) + j
                        last = V.tensor_scalar(nb[:, c, j, :], r[:, t, :], small[:, 2, t:t + 1], None, ALU.mult)
                    last.then_inc(s_h2, 1)
                NTH = 2 * TB
                lg = ps[:, 4, 0:NTH * NE].rearrange("p (t e) -> p t e", e=NE)
                sc = small_r(h)
                m8 = junk_r[:, 0:NTH]
                dve.wait_ge(s_rt, h + 1)
                ch.link(V.tensor_reduce(m8, lg, AX, ALU.max))
                V.tensor_tensor(sc, lg, m8.unsqueeze(2).to_broadcast([P, NTH, NE]), ALU.subtract).then_inc(s_rx, 1)
                dve.wait_ge(s_re, h + 1)
                ch.link(V.tensor_reduce(m8, sc, AX, ALU.add))
                ch.link(V.reciprocal(m8, m8))
                ch.link(V.tensor_tensor(sc, sc, m8.unsqueeze(2).to_broadcast([P, NTH, NE]), ALU.mult))
                for t in range(NTH):
                    last = V.max(rmax[:, t, :], sc[:, t, :])
                ch.link(last)
                for t in range(NTH):
                    last = V.max_index(ridx[:, t, :], rmax[:, t, :], sc[:, t, :])
                ch.link(last)
                ch.link(V.tensor_copy(rmax[:, :, 0:2], ridx[:, :, 0:2]))
                io = iota8[:, :].unsqueeze(1).to_broadcast([P, NTH, NE])
                V.tensor_tensor(req[:, 0], io, rmax[:, :, 0:1].to_broadcast([P, NTH, NE]), ALU.is_equal)
                ch.link(V.tensor_tensor(req[:, 1], io, rmax[:, :, 1:2].to_broadcast([P, NTH, NE]), ALU.is_equal))
                ch.link(V.tensor_tensor(req[:, 0], req[:, 0], req[:, 1], ALU.add))
                V.tensor_tensor(sc, sc, req[:, 0], ALU.mult).then_inc(s_wt, 1)

            dve.wait_ge(s_wt, HB)
            with dve.Fori(0, NE // 2) as pair:
                e0 = pair * 2
                def hidden(j, f):
                    m = e0 * (NB * FT) + (j * FT + f)
                    dve.wait_ge(s_sg, m + 1)
                    dve.wait_ge(s_u2, m + 1)
                    if f == 0:
                        dve.wait_ge(s_dn, e0 * NB + j + 7)
                    V.tensor_tensor(hh[:, j % 2, f, :], sg[:, f % 2, :], bank(2 + f % 2), ALU.mult).then_inc(s_hm, 1)

                def add(j):
                    b = j % NB
                    dve.wait_ge(s_dn, e0 * NB + j + 9)
                    for t in range(TB):
                        last = V.scalar_tensor_tensor(r[:, TB * b + t, :], ps[:, 4 + j % 2, t * P:t * P + P],
                                                      wtok[:, TB * b + t, bass.ds(e0 + j // NB, 1)],
                                                      r[:, TB * b + t, :], ALU.mult, ALU.add)
                    last.then_inc(s_acc, 1)

                for j in range(2 * NB):
                    for f in range(FT):
                        hidden(j, f)
                        if f == 1 and j:
                            add(j - 1)
                add(2 * NB - 1)
            dve.wait_ge(s_acc, 2 + NE * NB)

            ln_n = [0]

            def layernorm(b, k, done):
                sl = slice(TB * b, TB * b + TB)
                moments(x, b)
                power(V.tensor_scalar(small[:, 1, sl], mv[:, sl, 1], EPS, None, ALU.add))
                for j in range(TB):
                    t = TB * b + j
                    last = normalise(nb[:, k, j, :], x[:, t, :], t, small[:, 2, t:t + 1])
                last.then_inc(done, 1)

            def ffn(p):
                def head(b):
                    if p == 0:
                        ch.link(V.tensor_tensor(x[:, tiles(b), :], x[:, tiles(b), :], r[:, tiles(b), :], ALU.add))
                    else:
                        dve.wait_ge(s_ya, TB * (b + 1))
                    wait(dve, s_ft, p * NB + b - 1)
                    layernorm(b, b % 2, s_fn)

                def hid(b, f):
                    m = (p * NB + b) * HT + f
                    dve.wait_ge(s_fs, m + 1)
                    dve.wait_ge(s_fu, m + 1)
                    if f == 0:
                        wait(dve, s_fd, p * NB + b - 1)
                    V.tensor_tensor(fhh[:, b % 2, f, :], fsg[:, m % 2, :], bank(2 + m % 2), ALU.mult).then_inc(s_fh, 1)

                def add(b):
                    q = p * NB + b
                    dve.wait_ge(s_fd, q + 1)
                    V.scalar_tensor_tensor(x[:, tiles(b), :], bank(4 + b % 2).rearrange("p (j d) -> p j d", j=TB),
                                           DQ * DQ, x[:, tiles(b), :], ALU.mult, ALU.add).then_inc(s_fa, 1)

                head(0)
                for b in range(NB):
                    if b + 1 < NB:
                        head(b + 1)
                    for f in range(HT):
                        hid(b, f)
                        if f == 1 and b:
                            add(b - 1)
                add(NB - 1)

            ffn(0)

            dve.wait_ge(s_fa, NB)
            V.memset(vv[:, :, :, :, :], 0.0)
            ch.link(V.memset(zm[:, :, :, :], 0.0))
            for k in range(2):
                last = V.memset(vv[:, k, :, :, HS:HS + 1], 1.0)
            last.then_inc(s_vv0, 1)

            def norm(b):
                wait(dve, s_at, b - 1)
                layernorm(b, b % 2, s_an)

            def maxima(b, i):
                for qt in range(TB):
                    for g in range(4):
                        m = ((b * HG + i) * TB + qt) * 4 + g
                        w = (qt + 1) * P
                        dve.wait_ge(s_s1, m + 1)
                        if b and i == 0 and qt == 0 and g == 0:
                            dve.wait_ge(s_zq, HG * b)
                        col = 32 * g + HS * ((i + 1) % HG)
                        wait(dve, s_mx, m - 1)
                        V.tensor_tensor_reduce(out=junk[:, m % 2, 0:w], in0=ps[:, 4 + m % 2, 0:w], in1=cmask[:, L - w:L],
                                               scale=-1.0, scalar=3.0e38, op0=ALU.add, op1=ALU.min,
                                               accum_out=zm[:, qt, i, col:col + 1]).then_inc(s_mx, 1)

            def finish(b):
                for qt in range(TB):
                    dve.wait_ge(s_ott, b * TB + qt + 1)
                    o4 = bank(7).rearrange("p (i g w) -> p i g w", i=HG, g=4)
                    V.reciprocal(rs[:, qt, :].rearrange("p (i g) -> p i g", i=HG), o4[:, :, :, HS]).then_inc(s_rs, 1)
                    dve.wait_ge(s_rs, b * TB + qt + 1)
                    yv = yn[:, qt, :].rearrange("p (g i d) -> p i g d", g=4, i=HG)
                    for i in range(HG):
                        last = V.tensor_tensor(
                            yv[:, i, :, :], o4[:, i, :, 0:HS],
                            rs[:, qt, HG * i:HG * i + HG].unsqueeze(2).to_broadcast([P, 4, HS]), ALU.mult)
                    ch.link(last)
                    V.tensor_tensor(x[:, TB * b + qt, :], x[:, TB * b + qt, :], yn[:, qt, :], ALU.add).then_inc(s_ya, 1)

            norm(0)
            for i in range(HG):
                maxima(0, i)
            for b in range(NB):
                if b + 1 < NB:
                    norm(b + 1)
                for i in range(HG):
                    if b + 1 < NB:
                        maxima(b + 1, i)
                finish(b)
            ffn(1)

        @block.tensor
        def _(pe):
            T = nc.tensor

            def mm(o, l, rr, start=True, stop=True):
                return T.matmul(o, l, rr, start=start, stop=stop)

            pe.wait_ge(s_const, 2)
            pe.wait_ge(s_wflt, 1)
            pe.wait_ge(s_aw, 16 * 9)
            for n, (o, l, rr, turned, _, need) in enumerate(prep):
                wait(pe, s_wpc, max(need, n - 7))
                (T.transpose(o, l, rr) if turned else mm(o, l, rr)).then_inc(s_wp, 1)
            pe.wait_ge(s_wpc, NPREP + 1 + HG)
            pe.wait_ge(s_dconst, 1)

            for h in range(HB):
                if h:
                    pe.wait_ge(s_rx, h)
                for c in range(HB):
                    b = HB * h + c
                    pe.wait_ge(s_nb, b + 1)
                    for j in range(TB):
                        last = T.transpose(ps[:, c, j * P:j * P + P], nb[:, c, j, :], ident[:])
                    last.then_inc(s_tr, 1)
                pe.wait_ge(s_xT, HB * h + HB)
                for c in range(HB):
                    banks = ((2, 3, 4, 5), (6, 7, 0, 1))[c]
                    for m in range(4):
                        mm(bank(banks[m]), ipw[:, m * P:m * P + P], xT[:, c, :]).then_inc(s_ip, 1)
                for c in range(HB):
                    b = HB * h + c
                    pe.wait_ge(s_xi, 2 * b + 2)
                    for e in range(CT):
                        for k in range(DC):
                            last = mm(bank((2, 6)[c] + e), convd[:, e, k, :], xip[:, c, e, 1 + k:1 + k + L],
                                      start=(k == 0), stop=(k == DC - 1))
                        last.then_inc(s_cv, 1)
                for c in range(HB):
                    b = HB * h + c
                    pe.wait_ge(s_zs, 2 * b + 2)
                    pe.wait_ge(s_xc, 2 * b + 2)
                    d_bank, bc_bank = ((4, 5), (0, 1))[c]
                    for e in range(CT):
                        last = mm(ps[0:RK, d_bank, :], xpw[:, e, :], xc[:, e, c * L:c * L + L],
                                  start=(e == 0), stop=(e == CT - 1))
                    last.then_inc(s_pj, 1)
                    for e in range(CT):
                        last = mm(ps[0:96, bc_bank, :], bcw[:, e, :, :].rearrange("p q n -> p (q n)"),
                                  xc[:, e, c * L:c * L + L], start=(e == 0), stop=(e == CT - 1))
                    last.then_inc(s_pj, 1)
                for c in range(HB):
                    b = HB * h + c
                    pe.wait_ge(s_dts, b + 1)
                    for e in range(CT):
                        mm(bank((2, 6)[c] + e), dtw[0:RK, e * P:e * P + P], dts[0:RK, c, :]).then_inc(s_dtp, 1)
                pe.wait_ge(s_v, HB * h + HB)
                pe.wait_ge(s_bc3, HB * h + HB)
                for e in range(CT):
                    for c in range(HB):
                        mm(bank(2 * e + c), dskd[:, e, :], xc[:, e, c * L:c * L + L], stop=False)

                def broadcast(bk, row, done):
                    for c in range(HB):
                        last = mm(bank(bk + c), sel[0:96, row, :], bc3[0:96, c * L:c * L + L])
                    last.then_inc(done, 1)

                def ysum(e, stop):
                    for c in range(HB):
                        last = mm(bank(2 * e + c), ident[:], hC[:, e, c * L:c * L + L], start=False, stop=stop)
                    last.then_inc(s_ys, 1)

                broadcast(6, 0, s_bps)
                broadcast(4, NS, s_cps)
                with pe.Fori(1, NS, 1) as n:
                    gn = n + h * NS
                    pe.wait_ge(s_bs, gn)
                    for c in range(HB):
                        last = mm(bank(6 + c), sel[0:96, bass.ds(n, 1), :].rearrange("p o q -> p (o q)"),
                                  bc3[0:96, c * L:c * L + L])
                    last.then_inc(s_bps, 1)
                    pe.wait_ge(s_hc, 2 * gn + 1)
                    ysum(0, False)
                    pe.wait_ge(s_hc, 2 * gn + 2)
                    for c in range(HB):
                        last = mm(bank(4 + c), sel[0:96, bass.ds(n + NS, 1), :].rearrange("p o q -> p (o q)"),
                                  bc3[0:96, c * L:c * L + L])
                    last.then_inc(s_cps, 1)
                    ysum(1, False)
                for e in range(CT):
                    pe.wait_ge(s_hc, 2 * NS * (h + 1) + 1 + e)
                    ysum(e, True)
                pe.wait_ge(s_yg, 2 * h + 2)
                for c in range(HB):
                    for j in range(TB):
                        for e in range(CT):
                            last = mm(ps[:, 4 + c, j * P:j * P + P], zs[:, e, c * L + j * P:c * L + j * P + P],
                                      opw[:, e, :], start=(e == 0), stop=(e == CT - 1))
                    last.then_inc(s_op, 1)
                for c in range(HB):
                    b = HB * h + c
                    pe.wait_ge(s_h2, b + 1)
                    for j in range(TB):
                        last = T.transpose(ps[:, 6 + c, j * P:j * P + P], nb[:, c, j, :], ident[:])
                    last.then_inc(s_tr2, 1)
                for c in range(HB):
                    b = HB * h + c
                    pe.wait_ge(s_h2T, b + 1)
                    for j in range(TB):
                        t = c * TB + j
                        last = mm(ps[:, 4, t * NE:t * NE + NE], h2T[:, b, j * P:j * P + P], rw[:])
                last.then_inc(s_rt, 1)

            pe.wait_ge(s_rx, HB)
            with pe.Fori(0, NE // 2) as pair:
                e0 = pair * 2
                def gate_up(j, f):
                    k, b = j // NB, j % NB
                    m = e0 * (NB * FT) + (j * FT + f)
                    pe.wait_ge(s_hm, m + 1)
                    mm(bank(f % 2), moew[:, k, 0, f * P:f * P + P], h2T[:, b, :]).then_inc(s_g, 1)
                    mm(bank(2 + f % 2), moew[:, k, 1, f * P:f * P + P], h2T[:, b, :]).then_inc(s_u2, 1)

                def down(j):
                    k = j // NB
                    pe.wait_ge(s_hm, e0 * (NB * FT) + (j * FT + FT + 2))
                    pe.wait_ge(s_acc, e0 * NB + j + 1)
                    for t in range(TB):
                        for f in range(FT):
                            last = mm(ps[:, 4 + j % 2, t * P:t * P + P], hh[:, j % 2, f, t * P:t * P + P],
                                      moew[:, k, 2, f * P:f * P + P], start=(f == 0), stop=(f == FT - 1))
                    last.then_inc(s_dn, 1)

                for j in range(2 * NB):
                    if j % NB == 0:
                        pe.wait_ge(s_mw[j // NB], e0 * 24 + 48)
                    for f in range(FT):
                        gate_up(j, f)
                        if f == 0 and j:
                            down(j - 1)
                down(2 * NB - 1)
            pe.wait_ge(s_acc, 2 + NE * NB)

            def ffn(p):
                def head(b):
                    q = p * NB + b
                    pe.wait_ge(s_fn, q + 1)
                    wait(pe, s_fxT, q - 1)
                    for j in range(TB):
                        last = T.transpose(ps[:, 6 + b % 2, j * P:j * P + P], nb[:, b % 2, j, :], ident[:])
                    last.then_inc(s_ft, 1)

                def gate_up(b, f):
                    m = (p * NB + b) * HT + f
                    wait(pe, s_fh, m - 1)
                    mm(bank(m % 2), wgT[:, f * P:f * P + P], xT[:, b % 2, :]).then_inc(s_fg, 1)
                    mm(bank(2 + m % 2), wuT[:, f * P:f * P + P], xT[:, b % 2, :]).then_inc(s_fu, 1)

                def down(b):
                    q = p * NB + b
                    pe.wait_ge(s_fh, q * HT + HT)
                    wait(pe, s_fa, q - 1)
                    for t in range(TB):
                        for f in range(HT):
                            last = mm(ps[:, 4 + b % 2, t * P:t * P + P], fhh[:, b % 2, f, t * P:t * P + P],
                                      wdT[:, f, :], start=(f == 0), stop=(f == HT - 1))
                    last.then_inc(s_fd, 1)

                head(0)
                for b in range(NB):
                    if b + 1 < NB:
                        head(b + 1)
                    pe.wait_ge(s_fxT, p * NB + b + 1)
                    for f in range(HT):
                        gate_up(b, f)
                        if f == 0 and b:
                            down(b - 1)
                down(NB - 1)

            ffn(0)

            pe.wait_ge(s_fa, NB)

            def project(b):
                pe.wait_ge(s_an, b + 1)
                wait(pe, s_qa, HG * b)
                wait(pe, s_ya, TB * (b - 1))
                for j in range(TB):
                    last = T.transpose(ps[:, 7, j * P:j * P + P], nb[:, b % 2, j, :], ident[:])
                last.then_inc(s_at, 1)
                pe.wait_ge(s_axT, b + 1)
                mm(bank(7), wqq[:], xT[:, b % 2, :]).then_inc(s_aq, 1)
                pe.wait_ge(s_qm, HG * b + HG)
                mm(bank(7), mT[:], xT[:, b % 2, :]).then_inc(s_ak, 1)
                pe.wait_ge(s_km, HG * b + HG)
                for j in range(TB):
                    last = mm(ps[:, 7, j * P:j * P + P], xT[:, b % 2, j * P:j * P + P], vx[:])
                last.then_inc(s_av, 1)

            def query_major(b, i):
                for qt in range(TB):
                    for g in range(4):
                        m = ((b * HG + i) * TB + qt) * 4 + g
                        gs = slice(32 * g, 32 * g + 32)
                        wait(pe, s_mx, m - 1)
                        mm(ps[:, 4 + m % 2, 0:(qt + 1) * P], qm[gs, i, qt * P:qt * P + P],
                           km[gs, b % 2, i, 0:(qt + 1) * P]).then_inc(s_s1, 1)

            def with_max(b):
                pe.wait_ge(s_mx, (b + 1) * HG * TB * 4)
                pe.wait_ge(s_vv, b + 1)
                for i in range(HG):
                    wait(pe, s_qa, HG * b + i)
                    mm(bank(7), wqm[:, i, :], xT[:, b % 2, :], stop=False)
                    for qt in range(TB):
                        last = mm(ps[:, 7, qt * P:qt * P + P], zm[:, qt, i, :], ident[:], start=False,
                                  stop=(qt == TB - 1))
                    last.then_inc(s_zq, 1)

            def key_major(b, i):
                def scores(kt):
                    m = (b * HG + i) * TB + kt
                    for g in range(4):
                        gs = slice(32 * g, 32 * g + 32)
                        wait(pe, s_ex, 4 * (m - 1) + g + 1)
                        mm(ps[:, g, kt * P:L], km[gs, b % 2, i, kt * P:kt * P + P],
                           qa[gs, b % 2, i, kt * P:L], stop=False)
                    for g in range(4):
                        mm(ps[:, g, kt * P:kt * P + P], identb[:], kmask[:], start=False).then_inc(s_s2, 1)

                def values(kt):
                    m = (b * HG + i) * TB + kt
                    pe.wait_ge(s_ex, 4 * (m + 1))
                    if kt == 0:
                        wait(pe, s_ot, b * HG + i)
                    for g in range(4):
                        last = mm(ps[32 * g:32 * g + 32, 6, kt * P:L], vv[:, b % 2, kt, HG * g + i, :],
                                  pt[:, kt % 2, g, kt * P:L], start=(kt == 0), stop=(kt == TB - 1))
                    last.then_inc(s_pv, 1)

                scores(0)
                for kt in range(TB):
                    if kt + 1 < TB:
                        scores(kt + 1)
                    values(kt)

            def finish(b):
                pe.wait_ge(s_ot, HG * (b + 1))
                for qt in range(TB):
                    wait(pe, s_ya, b * TB + qt)
                    if qt == 0:
                        wait(pe, s_vv, min(b + 2, NB))
                    for i in range(HG):
                        last = T.transpose(ps[:, 7, i * P:i * P + P], ot[:, i, qt * P:qt * P + P], ident[:])
                    last.then_inc(s_ott, 1)

            pe.wait_ge(s_vv0, 1)
            project(0)
            for i in range(HG):
                query_major(0, i)
            with_max(0)
            for b in range(NB):
                if b + 1 < NB:
                    project(b + 1)
                pe.wait_ge(s_qa, HG * (b + 1))
                for i in range(HG):
                    if b + 1 < NB:
                        query_major(b + 1, i)
                    key_major(b, i)
                finish(b)
                if b + 1 < NB:
                    pe.wait_ge(s_ya, TB * (b + 1))
                    with_max(b + 1)
            ffn(1)


_INS = ["hidden_states", "rms1_w", "rms2_w", "in_proj_w", "conv_w", "conv_b", "x_proj_w", "dt_proj_w",
        "dt_proj_b", "A_log", "D_skip", "out_proj_w", "router_w", "Wg", "Wu", "Wd"]
_INS = ["L0_attn_a_" + n for n in _INS] + ["L0_attn_b_" + n for n in
                                           ("W_dq", "W_uq", "W_dkv", "W_uk", "W_uv", "W_o")]
_INS += ["L0_ffn_" + n for n in ("w_gate", "w_up", "w_down")]
_SHAPE = (4, 512, 128)


def kernel(**inputs):
    import numpy as _np
    import concourse.bacc as _bacc
    from concourse import mybir as _mybir
    from concourse.bass_utils import run_bass_kernel_spmd as _run

    nc = _bacc.Bacc("TRN2", target_bir_lowering=False, num_devices=1)
    arrays, args = {}, []
    for name in _INS:
        a = _np.ascontiguousarray(inputs[name])
        arrays[f"in_{name}"] = a
        args.append(nc.dram_tensor(f"in_{name}", a.shape, _mybir.dt.from_np(a.dtype), kind="ExternalInput").ap())
    out = nc.dram_tensor("out_0", _SHAPE, _mybir.dt.float32, kind="ExternalOutput").ap()
    build(nc, *args, out)
    r = _run(nc, [arrays], core_ids=[0])
    return r.results[0]["out_0"]
```

```python
from contextlib import ExitStack

import concourse.bass as bass
from concourse import mybir

F32 = mybir.dt.float32
BF16 = mybir.dt.bfloat16
I32 = mybir.dt.int32
U32 = mybir.dt.uint32
ALU = mybir.AluOpType
ACT = mybir.ActivationFunctionType
AX = mybir.AxisListType.X

P = 128
EPS = 1e-5
NEG = -1.0e38


class Chain:

    def __init__(self, eng, sem):
        self.eng, self.sem, self.n = eng, sem, 0

    def link(self, ins):
        self.n += 1
        ins.then_inc(self.sem, 1)
        self.eng.wait_ge(self.sem, self.n)


def build(nc, x_in, rms1_w, rms2_w, in_proj_w, conv_w, conv_b, x_proj_w, dt_proj_w, dt_proj_b,
          A_log, D_skip, out_proj_w, router_w, Wg, Wu, Wd, W_dq, W_uq, W_dkv, W_uk, W_uv, W_o,
          w_gate, w_up, w_down, out):
    NB, L, D = x_in.shape
    NT = NB * L // P
    TB = L // P
    DI = in_proj_w.shape[1] // 2
    CT = DI // P
    NS = A_log.shape[1]
    DC = conv_w.shape[2]
    RK = dt_proj_w.shape[0]
    NE, _, FF = Wg.shape
    FT = FF // P
    HID = w_gate.shape[0]
    HT = HID // P
    QL, KVL = W_dq.shape[0], W_dkv.shape[0]
    NH, HS = 16, D // 16
    HG = 4
    HB = 2
    HL = HB * L
    QS = float(HS) ** -0.5
    DQ = 1.0 / 127.0
    assert HT == 3 and FF == L and D == P and L == 512 and CT == 2 and FT == 4 and NH == HG * 4

    xd = x_in.rearrange("b (j p) d -> b p j d", p=P)
    od = out.rearrange("b (j p) d -> b p j d", p=P)

    ctx = ExitStack()
    with ctx:
        def sb(name, shape, dt=F32):
            return ctx.enter_context(nc.sbuf_tensor(name, shape, dt))

        def sem(name):
            return ctx.enter_context(nc.semaphore(name))

        ps = ctx.enter_context(nc.psum_tensor("ps", [P, 8, 512], F32))

        def bank(k, n=1):
            return ps[:, k, :] if n == 1 else ps[:, k:k + n, :]

        x = sb("x", [P, NT, D])
        r = sb("r", [P, NT, D])
        nb = sb("nb", [P, 2, TB, D])
        xT = sb("xT", [P, 2, L])
        stats = sb("stats", [P, NT, 6])
        mv = sb("mv", [P, NT, 2])
        small = sb("small", [P, 4, NT])
        ident = sb("ident", [P, P])
        cmask = sb("cmask", [P, L])
        identb = sb("identb", [P, P], BF16)
        kmask = sb("kmask", [P, P], BF16)
        neghalf = sb("neghalf", [P, NT])
        moew = sb("moew", [P, 2, 3, FF])
        wgT = sb("wgT", [P, HID])
        wuT = sb("wuT", [P, HID])
        wdT = sb("wdT", [P, HT, D])
        mT = sb("mT", [P, D])
        vx = sb("vx", [P, D])
        w1c = sb("w1c", [P, 1])
        w2c = sb("w2c", [P, 1])
        rw = sb("rw", [P, NE])
        wtok = sb("wtok", [P, NT, NE])
        iota8 = sb("iota8", [P, NE])
        wqq = sb("wqq", [P, D])
        junk_r = sb("junk_r", [P, 2 * TB])
        rmax = sb("rmax", [P, 2 * TB, 8])
        ridx = sb("ridx", [P, 2 * TB, 8], U32)
        req = sb("req", [P, 2, 2 * TB, NE])

        ARENA = 38 * 1024
        arena = sb("arena", [P, ARENA])
        at = [0]

        def carve(shape, dt=F32):
            n = 1
            for s in shape:
                n *= s
            words = n if dt != BF16 else n // 2
            a = arena[:, at[0]:at[0] + words]
            at[0] += words
            assert at[0] <= ARENA, at[0]
            if dt != F32:
                a = a.bitcast(dt)
            names = " ".join(f"a{i}" for i in range(len(shape)))
            if len(shape) == 1:
                return a
            return a.rearrange(f"p ({names}) -> p {names}", **{f"a{i}": s for i, s in enumerate(shape)})

        ipw = carve([2 * DI])
        xpw = carve([CT, RK])
        bcw = carve([CT, 3, 2 * NS])
        dtw = carve([DI])
        opw = carve([CT, D])
        convw = carve([CT, DC])
        convb = carve([CT])
        dtb = carve([CT])
        dsk = carve([CT])
        aneg = carve([CT, NS])
        convd = carve([CT, DC, P])
        dskd = carve([CT, P])
        sel = carve([2 * NS, P], BF16)
        selr = carve([2 * NS])
        h2T = carve([NB, L])
        moe_from = at[0]
        xip = carve([HB, CT, L + 4])
        xc = carve([CT, HL])
        zs = carve([CT, HL])
        delta = carve([CT, HL])
        dx = carve([CT, HL])
        dts = carve([HB, L])
        bc3 = carve([HL], BF16)
        scan_from = at[0]
        v = carve([HB, CT, L])
        u = carve([HB, CT, L])
        bcr = carve([HB, L])
        bcm = carve([HB, L], BF16)
        v_to = at[0]
        at[0] = scan_from
        bs = carve([2, HL])
        dA = carve([2, CT, HL])
        dBx = carve([2, CT, HL])
        hst = carve([CT, HL])
        hC = carve([2, CT, HL])
        assert v_to <= at[0]
        at[0] = scan_from
        wint = carve([3, HID], I32)
        wflt = carve([3, HID])
        adq, auq, adkv, auk, auv, ao = (carve([P]) for _ in range(6))
        auqT, aoT, aqqT, akT, av = (carve([P]) for _ in range(5))
        at[0] = moe_from
        sg = carve([2, L])
        hh = carve([2, FT, L])
        moe_to = at[0]
        at[0] = 0
        QR = 7 * HS
        MR = QR + 3
        qq = carve([NB, NH // 2, L], BF16)
        pt = carve([2, 4, L])
        assert at[0] >= moe_to
        kk = carve([NB, NH // 2, L], BF16)
        vv = carve([NB, TB, NH, 32])
        ot = carve([4, L])
        qp = carve([2, 3, L], BF16)
        qr = carve([2, L])
        nm = carve([2, TB, 2, NH // 2])
        nr = carve([2, TB, 2, NH // 2])
        m3 = carve([2, TB, 2, 3, NH // 2], BF16)
        mrow = carve([2, L], BF16)
        onesr = carve([L], BF16)
        junk = carve([2, L])
        rs = carve([TB, NH])
        yn = carve([TB, D])
        fsg = carve([2, L])
        fhh = moew[:, :, :, :]

        s_x = [sem(f"x_loaded{b}") for b in range(NB)]
        s_w = sem("mamba_weights_loaded")
        s_aw = sem("attn_ffn_weights_loaded")
        s_out = sem("out_stored")
        s_dch = sem("dve_chain")
        s_ach = sem("act_chain")
        s_pch = sem("pool_chain")
        s_const = sem("constants_ready")
        s_dconst = sem("dve_constants_ready")
        s_wflt = sem("ffn_weights_float")
        s_wp = sem("weight_prep_matmul")
        s_wpc = sem("weight_prep_copied")
        s_var = sem("variance_ready")
        s_rstd = sem("rstd_ready")
        s_nb = sem("tokens_normalised")
        s_tr = sem("transposed")
        s_xT = sem("xT_ready")
        s_ip = sem("in_proj_done")
        s_xi = sem("xi_ready")
        s_zs = sem("z_ready")
        s_cv = sem("conv_done")
        s_xc = sem("xc_ready")
        s_pj = sem("x_proj_done")
        s_dts = sem("dt_ready")
        s_bc3 = sem("bc_split_ready")
        s_dtp = sem("dt_proj_done")
        s_v = sem("softplus_input_ready")
        s_aexp = sem("exp_A_ready")
        s_ones = sem("ones_placed")
        s_vv0 = sem("attn_buffers_cleared")
        s_rs = sem("reciprocal_sum_ready")
        s_u = sem("softplus_log_ready")
        s_dl = sem("delta_ready")
        s_dx = sem("dx_ready")
        s_bps = sem("b_broadcast_done")
        s_cps = sem("c_broadcast_done")
        s_bs = sem("b_copied")
        s_da = sem("dA_ready")
        s_dbx = sem("dBx_ready")
        s_scan = sem("scan_done")
        s_hc = sem("hC_ready")
        s_ys = sem("y_summed")
        s_yg = sem("y_gated")
        s_op = sem("out_proj_done")
        s_r = sem("residual_ready")
        s_h2 = sem("h2_ready")
        s_tr2 = sem("h2_transposed")
        s_h2T = sem("h2T_ready")
        s_rt = sem("router_done")
        s_rx = sem("router_shifted")
        s_re = sem("router_exp")
        s_wt = sem("router_weights_ready")
        s_mw = [sem(f"expert_loaded{k}") for k in range(2)]
        s_g = sem("gate_done")
        s_u2 = sem("up_done")
        s_sg = sem("silu_done")
        s_hm = sem("hidden_ready")
        s_dn = sem("down_done")
        s_acc = sem("expert_added")
        s_fx = sem("ffn_input_ready")
        s_fn = sem("ffn_normalised")
        s_ft = sem("ffn_transposed")
        s_fxT = sem("ffn_xT_ready")
        s_fg = sem("ffn_gate_done")
        s_fu = sem("ffn_up_done")
        s_fs = sem("ffn_silu_done")
        s_fh = sem("ffn_hidden_ready")
        s_fd = sem("ffn_down_done")
        s_fa = sem("ffn_added")
        s_an = sem("attn_normalised")
        s_at = sem("attn_transposed")
        s_axT = sem("attn_xT_ready")
        s_aq = sem("attn_qk_done")
        s_av = sem("attn_v_done")
        s_qh = sem("first_part_ready")
        s_qr = sem("rest_ready")
        s_qp = sem("parts_ready")
        s_qk = [[sem(f"{w}_rows_placed{b}") for w in "qk"] for b in range(NB)]
        s_vv = sem("v_ready")
        s_s1 = sem("scores_q_major")
        s_mx = sem("row_max_ready")
        s_m3 = sem("max_parts_ready")
        s_mt = sem("max_transposed")
        s_mr = sem("max_rows_ready")
        s_mp = [sem(f"max_rows_placed{b}") for b in range(NB)]
        s_s2 = sem("scores_k_major")
        s_ex = sem("exp_done")
        s_pv = sem("pv_done")
        s_ot = sem("o_copied")
        s_ott = sem("o_transposed")
        s_ya = sem("attn_added")

        block = ctx.enter_context(nc.Block())

        def wait(eng, s, n):
            if not isinstance(n, int) or n > 0:
                eng.wait_ge(s, n)

        def tiles(b):
            return slice(TB * b, TB * b + TB)

        max_rows = bank(7).bitcast(BF16)[0:3 * NH, 0:L]

        def small_r(h):
            return wtok[:, 2 * TB * h:2 * TB * h + 2 * TB, :]

        loads = [(w1c[:, :], rms1_w.rearrange("(p o) -> p o", o=1)),
                 (w2c[:, :], rms2_w.rearrange("(p o) -> p o", o=1)),
                 (ipw[:, :], in_proj_w), (dtw[0:RK, :], dt_proj_w), (rw[:, :], router_w),
                 (convw[:, :, :], conv_w.rearrange("(e p) o k -> p e (o k)", p=P)),
                 (aneg[:, :, :], A_log.rearrange("(e p) n -> p e n", p=P)),
                 (opw[:, :, :], out_proj_w.rearrange("(e p) d -> p e d", p=P))]
        for e in range(CT):
            rows = x_proj_w[e * P:e * P + P, :]
            loads += [(dst[:, e:e + 1], src[e * P:e * P + P].rearrange("(p o) -> p o", o=1))
                      for dst, src in ((convb, conv_b), (dtb, dt_proj_b), (dsk, D_skip))]
            loads.append((xpw[:, e, :], rows[:, 0:RK]))
            loads += [(bcw[:, e, q, :], rows[:, RK:RK + 2 * NS]) for q in range(3)]

        def turn(rows, cols=P):
            turn.n += 1
            return ps[0:rows, (turn.n - 1) % 8, 0:cols]

        turn.n = 0
        prep = []
        for src, dst in ((0, wgT), (1, wuT), (2, None)):
            for t in range(HT):
                cs = slice(t * P, t * P + P)
                prep.append((turn(P), wflt[:, src, cs], ident[:], True,
                             wdT[:, t, :] if dst is None else dst[:, cs], 0))
        n0 = len(prep)
        prep += [(turn(QL), auq[:, 0:QL], ident[:], True, auqT[0:QL, :], 0),
                 (turn(P), ao[:, :], ident[:], True, aoT[:, :], 0),
                 (turn(P), adq[0:QL, :], auqT[0:QL, :], False, wqq[:], n0 + 1),
                 (turn(P), auqT[0:QL, :], adq[0:QL, :], False, aqqT[:, :], n0 + 1),
                 (turn(KVL), auk[:, 0:KVL], aqqT[:, :], False, akT[0:KVL, :], n0 + 4),
                 (turn(KVL), auv[:, 0:KVL], aoT[:, :], False, av[0:KVL, :], n0 + 2),
                 (turn(P), adkv[0:KVL, :], akT[0:KVL, :], False, mT[:], n0 + 5),
                 (turn(P), adkv[0:KVL, :], av[0:KVL, :], False, vx[:], n0 + 6)]
        NPREP = len(prep)

        PAIRS, UNITS, LAG = NH // 2, (NH // 4) * TB, 3
        steps, later = [("vals", 0)], []
        for a in range(NB * PAIRS + PAIRS + LAG):
            b, j = divmod(a, PAIRS)
            if j == 0 and b + 1 < NB:
                later += [("norm", b + 1), ("turn", b + 1), ("qk", b + 1, 0), ("qk", b + 1, 1), ("vals", b + 1)]
            for i in range(2):
                c = 2 * (a - PAIRS - LAG) + i
                for q in range(2):
                    if b < NB:
                        steps.append(("maxima", b, j, (0, 3, 1, 2)[2 * i + q]))
                    if 0 <= c < NB * UNITS:
                        steps.append(("scores", c, q))
                if 0 < c <= NB * UNITS:
                    steps.append(("values", c - 1))
                    if c % UNITS == 0:
                        later = [("finish", c // UNITS - 1, qt) for qt in range(TB)] + later
                if later:
                    steps.append(later.pop(0))
            if b < NB and j == PAIRS - 1:
                steps.append(("split_max", b))
                later.insert(0, ("place_max", b))
        steps += [("values", NB * UNITS - 1)] + later + [("finish", NB - 1, qt) for qt in range(TB)]
        early = {(2, 2): ("norm", 0), (3, 0): ("turn", 0), (3, 1): ("qk", 0, 0), (3, 2): ("qk", 0, 1)}

        def attend(parts, events=None):
            for name, *args in steps if events is None else events:
                if name in parts:
                    parts[name](*args)

        @block.sync
        def _(sp):
            sp.sem_inc(s_dbx, 4)
            sp.sem_inc(s_scan, 4)
            sp.sem_inc(s_ys, 4)
            sp.sem_inc(s_hc, 2)
            sp.sem_inc(s_hm, 2)
            sp.sem_inc(s_dn, 8)
            sp.sem_inc(s_acc, 2)
            for b in range(NB):
                sp.dma_start(x[:, tiles(b), :], xd[b]).then_inc(s_x[b], 16)
            for dst, src in (
                (wint[:, 0, :].rearrange("p (t d) -> p t d", t=HT), w_gate.rearrange("(t p) d -> p t d", p=P)),
                (wint[:, 1, :].rearrange("p (t d) -> p t d", t=HT), w_up.rearrange("(t p) d -> p t d", p=P)),
                (wint[:, 2, :], w_down),
                (adq[0:QL, :], W_dq), (auq[:, 0:QL], W_uq), (adkv[0:KVL, :], W_dkv),
                (auk[:, 0:KVL], W_uk), (auv[:, 0:KVL], W_uv), (ao[:, :], W_o),
            ):
                sp.dma_start(dst, src).then_inc(s_aw, 16)
            with sp.Fori(0, NE // 2) as pair:
                e0 = pair * 2
                for k in range(2):
                    sp.wait_ge(s_dn, e0 * 4 + 4 * (k + 1))
                    e = e0 + k
                    for i, w in enumerate((Wg, Wu)):
                        sp.dma_start(moew[:, k, i, :],
                                     w[bass.ds(e, 1), :, :].rearrange("e p f -> (e p) f")).then_inc(s_mw[k], 16)
                    sp.dma_start(moew[:, k, 2, :].rearrange("p (t d) -> p t d", t=FT),
                                 Wd[bass.ds(e, 1), :, :].rearrange("e (t p) d -> p (e t) d", p=P)).then_inc(s_mw[k], 16)
            sp.wait_ge(s_vv0, 2)
            for b in range(NB):
                for r in range(2):
                    sp.dma_start(kk[64 * r + QR:64 * r + MR, b, :, :],
                                 onesr[0:3, :].unsqueeze(1).to_broadcast([3, PAIRS, L])).then_inc(s_ones, 16)

            def place_qk(b, w):
                dst, parts = ((qq, (0, 0, 1, 0, 2, 1, 1)), (kk, (0, 1, 0, 2, 0, 1, 2)))[w]
                sp.wait_ge(s_qp, 2 * (2 * b + w) + 2)
                for n, part in enumerate(parts):
                    for r in range(2):
                        sp.dma_start(dst[64 * r + HS * n:64 * r + HS * n + HS, b, :, :],
                                     qp[64 * r:64 * r + 64, w, part, :]).then_inc(s_qk[b][w], 16)

            def place_max(b):
                sp.wait_ge(s_mr, b + 1)
                for r in range(2):
                    sp.dma_start(qq[64 * r + QR:64 * r + MR, b, :, :],
                                 mrow[3 * PAIRS * r:3 * PAIRS * (r + 1), b % 2, :]).then_inc(s_mp[b], 16)

            place_qk(0, 0)
            place_qk(0, 1)
            attend(dict(qk=place_qk, place_max=place_max))
            for b in range(NB):
                sp.wait_ge(s_fa, NB + b + 1)
                sp.dma_start(od[b], x[:, tiles(b), :]).then_inc(s_out, 16)
            sp.wait_ge(s_out, 16 * NB)

        @block.gpsimd
        def _(pool):
            G = nc.gpsimd
            ch = Chain(pool, s_pch)
            G.memset(ident[:], 0.0)
            G.memset(selr[:, :], 0.0)
            G.memset(cmask[:], 0.0)
            G.memset(kmask[:], 0.0)
            ch.link(G.memset(neghalf[:], -0.5))
            G.affine_select(out=ident[:], in_=ident[:], compare_op=ALU.not_equal, fill=1.0, base=0,
                            pattern=[[-1, P]], channel_multiplier=1).then_inc(s_const, 1)
            G.affine_select(out=cmask[:, L - P:L], in_=cmask[:, L - P:L], compare_op=ALU.is_ge, fill=NEG,
                            base=0, pattern=[[-1, P]], channel_multiplier=1)
            G.affine_select(out=kmask[:], in_=kmask[:], compare_op=ALU.is_ge, fill=NEG,
                            base=0, pattern=[[1, P]], channel_multiplier=-1)
            G.iota(iota8[:], pattern=[[1, NE]], base=0, channel_multiplier=0,
                   allow_small_or_imprecise_dtypes=True)
            for q in range(3):
                ch.link(G.affine_select(out=selr[:, :], in_=selr[:, :], compare_op=ALU.not_equal, fill=1.0,
                                        base=-2 * NS * q, pattern=[[-1, 2 * NS]], channel_multiplier=1))
            pool.sem_inc(s_const, 1)

            def powers(n, col, width, src=1):
                pool.wait_ge(s_var, n)
                G.tensor_tensor(small[:, 2, col:col + width], small[:, src, col:col + width],
                                neghalf[:, col:col + width], ALU.pow).then_inc(s_rstd, 1)

            for h in range(HB):
                for c in range(HB):
                    b = HB * h + c
                    powers(5 * h + 2 * c + 1, TB * b, TB)
                    powers(5 * h + 2 * c + 2, TB * b, TB)
                for c in range(HB):
                    pool.wait_ge(s_dl, HB * h + c + 1)
                    G.tensor_tensor(dx[:, :, c * L:c * L + L], delta[:, :, c * L:c * L + L],
                                    xc[:, :, c * L:c * L + L], ALU.mult).then_inc(s_dx, 1)
                pool.wait_ge(s_dx, HB * h + HB)
                with pool.Fori(0, NS // 2) as pair:
                    n0 = pair * 2
                    for k in range(2):
                        n = n0 + (h * NS + k)
                        pool.wait_ge(s_bs, n + 1)
                        for e in range(CT):
                            pool.wait_ge(s_scan, 2 * n + e + 1)
                            G.tensor_tensor(dBx[:, k, e, :], dx[:, e, :], bs[:, k, :],
                                            ALU.mult).then_inc(s_dbx, 1)
                powers(5 * h + 5, 2 * TB * h, 2 * TB)

            pool.wait_ge(s_op, NB)
            ch.link(G.memset(vv[:, :, :, :, :].rearrange("p b t h w -> p (b t h) w"), 0.0))
            G.memset(vv[:, :, :, :, :].rearrange("p b t h w -> p (b t h) w")[:, :, HS:HS + 1],
                     1.0).then_inc(s_vv0, 1)
            G.memset(onesr[:, :], 1.0).then_inc(s_vv0, 1)

            def ffn_powers(p):
                for b in range(NB):
                    powers(5 * HB + NB * p + b + 1, TB * b, TB)

            ffn_powers(0)

            def norm(b):
                powers(5 * HB + NB + b + 1, TB * b, TB)

            def split_qk(b, w):
                n = 2 * b + w
                pool.wait_ge(s_qr, n + 1)
                if b:
                    pool.wait_ge(s_qk[b - 1][w], 16 * 14)
                G.tensor_copy(qp[:, w, 1, :], qr[:, w, :]).then_inc(s_qp, 1)
                pool.wait_ge(s_qp, 2 * n + 1)
                G.tensor_tensor(qp[:, w, 2, :], qr[:, w, :], qp[:, w, 1, :], ALU.subtract).then_inc(s_qp, 1)

            def split_max(b):
                k = b % 2
                pool.wait_ge(s_mx, (b + 1) * NH * TB)
                wait(pool, s_mt, b - 1)
                src, rest = nm[:, k, :, :, :], nr[:, k, :, :, :]
                first, second, third = (m3[:, k, :, :, c, :] for c in range(3))
                ch.link(G.tensor_copy(first, src))
                ch.link(G.tensor_tensor(rest, src, first, ALU.subtract))
                ch.link(G.tensor_copy(second, rest))
                G.tensor_tensor(third, rest, second, ALU.subtract).then_inc(s_m3, 1)

            norm(0)
            split_qk(0, 0)
            split_qk(0, 1)
            attend(dict(norm=norm, qk=split_qk, split_max=split_max))
            ffn_powers(2)

        @block.scalar
        def _(act):
            S = nc.scalar
            ch = Chain(act, s_ach)
            for dst, src in loads:
                act.dma_start(dst, src).then_inc(s_w, 16)
            S.preload_act_table(ACT.Exp)
            act.wait_ge(s_w, 16 * len(loads))
            S.activation(aneg[:, :, :], aneg[:, :, :], ACT.Exp).then_inc(s_aexp, 1)

            act.wait_ge(s_aw, 16 * 9)
            S.copy(wflt[:, :, :], wint[:, :, :]).then_inc(s_wflt, 1)

            for h in range(HB):
                for c in range(HB):
                    b = HB * h + c
                    act.wait_ge(s_tr, b + 1)
                    S.activation(xT[:, c, :], bank(c), ACT.Copy, scale=w1c[:, 0:1]).then_inc(s_xT, 1)
                for c in range(HB):
                    b = HB * h + c
                    banks = ((2, 3, 4, 5), (6, 7, 0, 1))[c]
                    for e in range(CT):
                        act.wait_ge(s_ip, 4 * b + e + 1)
                        S.copy(xip[:, c, e, 4:4 + L], bank(banks[e])).then_inc(s_xi, 1)
                    for e in range(CT):
                        act.wait_ge(s_ip, 4 * b + 2 + e + 1)
                        S.activation(zs[:, e, c * L:c * L + L], bank(banks[2 + e]), ACT.Silu).then_inc(s_zs, 1)
                for c in range(HB):
                    b = HB * h + c
                    for e in range(CT):
                        act.wait_ge(s_cv, 2 * b + e + 1)
                        S.activation(xc[:, e, c * L:c * L + L], bank((2, 6)[c] + e), ACT.Silu,
                                     bias=convb[:, e:e + 1]).then_inc(s_xc, 1)
                for c in range(HB):
                    b = HB * h + c
                    act.wait_ge(s_pj, 2 * b + 1)
                    S.copy(dts[0:RK, c, :], ps[0:RK, (4, 0)[c], :]).then_inc(s_dts, 1)
                S.preload_act_table_set("natural_log_exp_and_others")
                for c in range(HB):
                    b = HB * h + c
                    act.wait_ge(s_v, b + 1)
                    ch.link(S.activation(u[:, c, :, :], u[:, c, :, :], ACT.Exp))
                    S.activation(u[:, c, :, :], u[:, c, :, :], ACT.Ln, bias=1.0).then_inc(s_u, 1)
                act.wait_ge(s_dl, HB * h + HB)
                act.wait_ge(s_dx, HB * h + HB)
                with act.Fori(0, NS // 2) as pair:
                    n0 = pair * 2
                    for k in range(2):
                        n = n0 + (h * NS + k)
                        act.wait_ge(s_bps, n + 1)
                        act.wait_ge(s_dbx, 2 * n + 2)
                        S.copy(bs[:, k, :].rearrange("p (c l) -> p c l", c=HB), bank(6, 2)).then_inc(s_bs, 1)
                        for e in range(CT):
                            act.wait_ge(s_scan, 2 * n + e + 1)
                            S.activation(dA[:, k, e, :].rearrange("p (c l) -> p c l", c=HB)[:, :, 1:L],
                                         delta[:, e, :].rearrange("p (c l) -> p c l", c=HB)[:, :, 1:L],
                                         ACT.Exp, scale=aneg[:, e, bass.ds(n0 + k, 1)]).then_inc(s_da, 1)
                for c in range(HB):
                    b = HB * h + c
                    act.wait_ge(s_tr2, b + 1)
                    S.activation(h2T[:, b, :], bank(6 + c), ACT.Copy, scale=w2c[:, 0:1]).then_inc(s_h2T, 1)
                act.wait_ge(s_rx, h + 1)
                S.activation(small_r(h), small_r(h), ACT.Exp).then_inc(s_re, 1)

            act.wait_ge(s_wt, HB)
            S.preload_act_table(ACT.Silu)
            with act.Fori(0, NE // 2) as pair:
                e0 = pair * 2
                for j in range(2 * NB):
                    for f in range(FT):
                        m = e0 * (NB * FT) + (j * FT + f)
                        act.wait_ge(s_g, m + 1)
                        act.wait_ge(s_hm, m + 1)
                        S.activation(sg[:, f % 2, :], bank(f % 2), ACT.Silu).then_inc(s_sg, 1)

            def turn(b):
                act.wait_ge(s_at, b + 1)
                if b < 2:
                    act.wait_ge(s_fu, HT * (b + 3))
                S.copy(xT[:, b % 2, :], bank(7)).then_inc(s_axT, 1)

            def first_part(b, w):
                act.wait_ge(s_aq, 2 * b + w + 1)
                if b:
                    act.wait_ge(s_qk[b - 1][w], 16 * 14)
                S.copy(qp[:, w, 0, :], bank(7)).then_inc(s_qh, 1)

            def vals(b):
                act.wait_ge(s_av, b + 1)
                S.copy(vv[:, b, :, :, 0:HS], bank(7).rearrange("p (t h d) -> p t h d", t=TB, d=HS)).then_inc(s_vv, 1)

            def place_max(b):
                act.wait_ge(s_mt, b + 1)
                if b >= 2:
                    act.wait_ge(s_mp[b - 2], 32)
                S.copy(mrow[0:3 * NH, b % 2, :], max_rows).then_inc(s_mr, 1)

            def exps(c, q):
                kt = c % TB
                if q == 0:
                    wait(act, s_pv, c - 1)
                act.wait_ge(s_s2, 2 * c + q + 1)
                S.activation(pt[:, c % 2, 2 * q:2 * q + 2, kt * P:L], ps[:, 2 * q:2 * q + 2, kt * P:L],
                             ACT.Exp).then_inc(s_ex, 1)

            def outputs(c):
                if c % TB == TB - 1:
                    b, n = c // UNITS, c // TB
                    act.wait_ge(s_pv, c + 1)
                    wait(act, s_ott, b * TB)
                    S.copy(ot[:, n % 4, :], bank(6)).then_inc(s_ot, 1)

            parts = dict(turn=turn, qk=first_part, vals=vals, place_max=place_max, scores=exps, values=outputs)

            def ffn(p):
                for b in range(NB):
                    q = p * NB + b
                    act.wait_ge(s_ft, q + 1)
                    S.copy(xT[:, b % 2, :], bank(6 + b % 2)).then_inc(s_fxT, 1)
                    for f in range(HT):
                        m = q * HT + f
                        act.wait_ge(s_fg, m + 1)
                        wait(act, s_fh, m - 1)
                        S.activation(fsg[:, m % 2, :], bank(m % 2), ACT.Silu, scale=DQ).then_inc(s_fs, 1)
                        if p == 0 and (b, f) in early:
                            attend(parts, [early[b, f]])

            ffn(0)

            S.preload_act_table(ACT.Exp)
            act.wait_ge(s_vv0, 2)
            attend(parts)
            ffn(1)

        @block.vector
        def _(dve):
            V = nc.vector
            ch = Chain(dve, s_dch)
            count = {"var": 0}

            def moments(src, b, n=TB):
                t0 = TB * b
                for j in range(n):
                    last = V.bn_stats(stats[:, t0 + j, :], src[:, t0 + j, :])
                ch.link(last)
                for j in range(n):
                    last = V.bn_aggr(mv[:, t0 + j, :], stats[:, t0 + j, :])
                ch.link(last)

            def power(n):
                count["var"] += 1
                n.then_inc(s_var, 1)
                dve.wait_ge(s_rstd, count["var"])

            def normalise(dst, src, t, rcol):
                return V.tensor_scalar(dst, src, mv[:, t, 0:1], rcol, ALU.subtract, ALU.mult)

            for c in range(HB):
                V.memset(xip[:, c, :, 0:4], 0.0)
            dve.wait_ge(s_const, 2)
            dve.wait_ge(s_w, 16 * len(loads))
            dve.wait_ge(s_aexp, 1)
            V.tensor_scalar(aneg[:, :, :], aneg[:, :, :], -1.0, None, ALU.mult)
            V.tensor_copy(identb[:], ident[:])
            V.tensor_copy(sel[:, :, :], selr[:, :].unsqueeze(2).to_broadcast([P, 2 * NS, P]))
            for e in range(CT):
                for k in range(DC):
                    V.tensor_scalar(convd[:, e, k, :], ident[:], convw[:, e, k:k + 1], None, ALU.mult)
                last = V.tensor_scalar(dskd[:, e, :], ident[:], dsk[:, e:e + 1], None, ALU.mult)
            last.then_inc(s_dconst, 1)
            for n, (src, _, _, _, dst, _) in enumerate(prep):
                dve.wait_ge(s_wp, n + 1)
                if n in (NPREP - 2, NPREP - 6):
                    V.tensor_scalar(dst.rearrange("p (r d j) -> p j r d", r=2, d=HS),
                                    src.rearrange("p (j r d) -> p j r d", r=2, d=HS),
                                    QS if n == NPREP - 2 else 1.0,
                                    None, ALU.mult).then_inc(s_wpc, 1)
                else:
                    V.tensor_copy(dst, src).then_inc(s_wpc, 1)

            for h in range(HB):
                for c in range(HB):
                    b = HB * h + c
                    sl = slice(TB * b, TB * b + TB)
                    dve.wait_ge(s_x[b], 16)
                    moments(x, b)
                    power(V.tensor_scalar(small[:, 1, sl], mv[:, sl, 1], EPS, None, ALU.add))
                    for j in range(TB):
                        t = TB * b + j
                        last = normalise(r[:, t, :], x[:, t, :], t, small[:, 2, t:t + 1])
                    ch.link(last)
                    ch.link(V.tensor_tensor(small[:, 3, sl], small[:, 2, sl], small[:, 2, sl], ALU.mult))
                    ch.link(V.tensor_tensor(small[:, 3, sl], small[:, 3, sl], mv[:, sl, 1], ALU.mult))
                    power(V.tensor_scalar(small[:, 1, sl], small[:, 3, sl], EPS, None, ALU.add))
                    if h:
                        dve.wait_ge(s_tr2, b - 1)
                    for j in range(TB):
                        t = TB * b + j
                        last = V.tensor_scalar(nb[:, c, j, :], r[:, t, :], small[:, 2, t:t + 1], None, ALU.mult)
                    last.then_inc(s_nb, 1)
                for c in range(HB):
                    b = HB * h + c
                    cs = slice(c * L, c * L + L)
                    src = ps[0:96, (5, 1)[c], :]
                    dve.wait_ge(s_pj, 2 * b + 2)
                    ch.link(V.tensor_copy(bc3[0:96, cs], src))
                    ch.link(V.tensor_tensor(bcr[0:96, c, :], src, bc3[0:96, cs], ALU.subtract))
                    ch.link(V.tensor_copy(bcm[0:96, c, :], bcr[0:96, c, :]))
                    V.tensor_copy(bc3[32:64, cs], bcm[32:64, c, :])
                    V.tensor_tensor(bc3[64:96, cs], bcr[64:96, c, :], bcm[64:96, c, :],
                                    ALU.subtract).then_inc(s_bc3, 1)
                for c in range(HB):
                    b = HB * h + c
                    for e in range(CT):
                        dve.wait_ge(s_dtp, 2 * b + e + 1)
                        last = V.tensor_scalar(v[:, c, e, :], bank((2, 6)[c] + e), dtb[:, e:e + 1], None, ALU.add)
                    ch.link(last)
                    V.scalar_tensor_tensor(u[:, c, :, :], v[:, c, :, :], -1.0, v[:, c, :, :],
                                           ALU.mult, ALU.min).then_inc(s_v, 1)
                for c in range(HB):
                    b = HB * h + c
                    dve.wait_ge(s_u, b + 1)
                    V.scalar_tensor_tensor(delta[:, :, c * L:c * L + L], v[:, c, :, :], 0.0, u[:, c, :, :],
                                           ALU.max, ALU.add).then_inc(s_dl, 1)
                dve.wait_ge(s_dl, HB * h + HB)
                for k in range(2):
                    last = V.memset(dA[:, k, :, :].rearrange("p e (c l) -> p (e c) l", c=HB)[:, :, 0:1], 0.0)
                ch.link(last)
                with dve.Fori(0, NS // 2) as pair:
                    n0 = pair * 2
                    for k in range(2):
                        n = n0 + (h * NS + k)
                        for e in range(CT):
                            dve.wait_ge(s_da, 2 * n + e + 1)
                            dve.wait_ge(s_dbx, 2 * n + e + 5)
                            dve.wait_ge(s_hc, 2 * n + e + 1)
                            V.tensor_tensor_scan(hst[:, e, :], dA[:, k, e, :], dBx[:, k, e, :], 0.0,
                                                 ALU.mult, ALU.add).then_inc(s_scan, 1)
                        dve.wait_ge(s_cps, n + 1)
                        for e in range(CT):
                            dve.wait_ge(s_scan, 2 * n + e + 5)
                            dve.wait_ge(s_ys, 2 * n + e + 1)
                            V.tensor_tensor(hC[:, k, e, :].rearrange("p (c l) -> p c l", c=HB),
                                            hst[:, e, :].rearrange("p (c l) -> p c l", c=HB),
                                            bank(4, 2), ALU.mult).then_inc(s_hc, 1)
                for e in range(CT):
                    dve.wait_ge(s_ys, 2 * NS * (h + 1) + e + 3)
                    V.tensor_tensor(zs[:, e, :].rearrange("p (c l) -> p c l", c=HB), bank(2 * e, 2),
                                    zs[:, e, :].rearrange("p (c l) -> p c l", c=HB), ALU.mult).then_inc(s_yg, 1)
                for c in range(HB):
                    b = HB * h + c
                    dve.wait_ge(s_op, b + 1)
                    V.tensor_tensor(r[:, tiles(b), :], bank(4 + c).rearrange("p (j d) -> p j d", j=TB),
                                    r[:, tiles(b), :], ALU.add).then_inc(s_r, 1)
                dve.wait_ge(s_r, HB * h + HB)
                sl = slice(2 * TB * h, 2 * TB * h + 2 * TB)
                moments(r, HB * h, 2 * TB)
                ch.link(V.tensor_tensor(small[:, 3, sl], mv[:, sl, 0], mv[:, sl, 0], ALU.mult))
                ch.link(V.tensor_tensor(small[:, 3, sl], small[:, 3, sl], mv[:, sl, 1], ALU.add))
                power(V.tensor_scalar(small[:, 1, sl], small[:, 3, sl], EPS, None, ALU.add))
                for c in range(HB):
                    for j in range(TB):
                        t = TB * (HB * h + c) + j
                        last = V.tensor_scalar(nb[:, c, j, :], r[:, t, :], small[:, 2, t:t + 1], None, ALU.mult)
                    last.then_inc(s_h2, 1)
                NTH = 2 * TB
                lg = ps[:, 4, 0:NTH * NE].rearrange("p (t e) -> p t e", e=NE)
                sc = small_r(h)
                m8 = junk_r[:, 0:NTH]
                dve.wait_ge(s_rt, h + 1)
                ch.link(V.tensor_reduce(m8, lg, AX, ALU.max))
                V.tensor_tensor(sc, lg, m8.unsqueeze(2).to_broadcast([P, NTH, NE]), ALU.subtract).then_inc(s_rx, 1)
                dve.wait_ge(s_re, h + 1)
                ch.link(V.tensor_reduce(m8, sc, AX, ALU.add))
                ch.link(V.reciprocal(m8, m8))
                ch.link(V.tensor_tensor(sc, sc, m8.unsqueeze(2).to_broadcast([P, NTH, NE]), ALU.mult))
                for t in range(NTH):
                    last = V.max(rmax[:, t, :], sc[:, t, :])
                ch.link(last)
                for t in range(NTH):
                    last = V.max_index(ridx[:, t, :], rmax[:, t, :], sc[:, t, :])
                ch.link(last)
                ch.link(V.tensor_copy(rmax[:, :, 0:2], ridx[:, :, 0:2]))
                io = iota8[:, :].unsqueeze(1).to_broadcast([P, NTH, NE])
                V.tensor_tensor(req[:, 0], io, rmax[:, :, 0:1].to_broadcast([P, NTH, NE]), ALU.is_equal)
                ch.link(V.tensor_tensor(req[:, 1], io, rmax[:, :, 1:2].to_broadcast([P, NTH, NE]), ALU.is_equal))
                ch.link(V.tensor_tensor(req[:, 0], req[:, 0], req[:, 1], ALU.add))
                V.tensor_tensor(sc, sc, req[:, 0], ALU.mult).then_inc(s_wt, 1)

            dve.wait_ge(s_wt, HB)
            with dve.Fori(0, NE // 2) as pair:
                e0 = pair * 2
                def hidden(j, f):
                    m = e0 * (NB * FT) + (j * FT + f)
                    dve.wait_ge(s_sg, m + 1)
                    dve.wait_ge(s_u2, m + 1)
                    if f == 0:
                        dve.wait_ge(s_dn, e0 * NB + j + 7)
                    V.tensor_tensor(hh[:, j % 2, f, :], sg[:, f % 2, :], bank(2 + f % 2), ALU.mult).then_inc(s_hm, 1)

                def add(j):
                    b = j % NB
                    dve.wait_ge(s_dn, e0 * NB + j + 9)
                    for t in range(TB):
                        last = V.scalar_tensor_tensor(r[:, TB * b + t, :], ps[:, 4 + j % 2, t * P:t * P + P],
                                                      wtok[:, TB * b + t, bass.ds(e0 + j // NB, 1)],
                                                      r[:, TB * b + t, :], ALU.mult, ALU.add)
                    last.then_inc(s_acc, 1)

                for j in range(2 * NB):
                    for f in range(FT):
                        hidden(j, f)
                        if f == 1 and j:
                            add(j - 1)
                add(2 * NB - 1)
            dve.wait_ge(s_acc, 2 + NE * NB)

            ln_n = [0]

            def layernorm(b, k, done):
                sl = slice(TB * b, TB * b + TB)
                moments(x, b)
                power(V.tensor_scalar(small[:, 1, sl], mv[:, sl, 1], EPS, None, ALU.add))
                for j in range(TB):
                    t = TB * b + j
                    last = normalise(nb[:, k, j, :], x[:, t, :], t, small[:, 2, t:t + 1])
                last.then_inc(done, 1)

            def norm(b):
                if b < 2:
                    dve.wait_ge(s_ft, b + 3)
                    dve.wait_ge(s_fa, b + 1)
                else:
                    dve.wait_ge(s_at, b - 1)
                layernorm(b, b % 2, s_an)

            def rest_part(b, w):
                dve.wait_ge(s_qh, 2 * b + w + 1)
                wait(dve, s_qp, 2 * (2 * b + w - 2) + 2)
                V.tensor_tensor(qr[:, w, :], bank(7), qp[:, w, 0, :], ALU.subtract).then_inc(s_qr, 1)

            nmax = [0]

            def maxima(b, j, qt):
                w = (qt + 1) * P
                for r in range(2):
                    m = nmax[0]
                    nmax[0] += 1
                    dve.wait_ge(s_s1, m + 1)
                    if b >= 2 and m % (2 * PAIRS * TB) == 0:
                        dve.wait_ge(s_m3, b - 1)
                    wait(dve, s_mx, m - 1)
                    V.tensor_tensor_reduce(out=junk[:, m % 2, 0:w], in0=ps[:, 4 + m % 2, 0:w],
                                           in1=cmask[:, L - w:L], scale=-1.0, scalar=3.0e38,
                                           op0=ALU.add, op1=ALU.min,
                                           accum_out=nm[:, b % 2, qt, r, j:j + 1]).then_inc(s_mx, 1)

            def finish(b, qt):
                n = b * TB + qt + 1
                dve.wait_ge(s_ott, n)
                o = bank(7).rearrange("p (h w) -> p h w", w=32)
                V.reciprocal(rs[:, qt, :], o[:, :, HS]).then_inc(s_rs, 1)
                dve.wait_ge(s_rs, n)
                ch.link(V.tensor_tensor(yn[:, qt, :].rearrange("p (h d) -> p h d", d=HS), o[:, :, 0:HS],
                                        rs[:, qt, :].unsqueeze(2).to_broadcast([P, NH, HS]), ALU.mult))
                V.tensor_tensor(x[:, TB * b + qt, :], x[:, TB * b + qt, :], yn[:, qt, :], ALU.add).then_inc(s_ya, 1)

            parts = dict(norm=norm, qk=rest_part, maxima=maxima, finish=finish)

            def ffn(p):
                def head(b):
                    if p == 0:
                        ch.link(V.tensor_tensor(x[:, tiles(b), :], x[:, tiles(b), :], r[:, tiles(b), :], ALU.add))
                    else:
                        dve.wait_ge(s_ya, TB * (b + 1))
                    wait(dve, s_ft, p * NB + b - 1)
                    layernorm(b, b % 2, s_fn)

                def hid(b, f):
                    m = (p * NB + b) * HT + f
                    dve.wait_ge(s_fs, m + 1)
                    dve.wait_ge(s_fu, m + 1)
                    if f == 0:
                        wait(dve, s_fd, p * NB + b - 1)
                    V.tensor_tensor(fhh[:, b % 2, f, :], fsg[:, m % 2, :], bank(2 + m % 2), ALU.mult).then_inc(s_fh, 1)

                def add(b):
                    q = p * NB + b
                    dve.wait_ge(s_fd, q + 1)
                    V.scalar_tensor_tensor(x[:, tiles(b), :], bank(4 + b % 2).rearrange("p (j d) -> p j d", j=TB),
                                           DQ * DQ, x[:, tiles(b), :], ALU.mult, ALU.add).then_inc(s_fa, 1)

                head(0)
                for b in range(NB):
                    if b + 1 < NB:
                        head(b + 1)
                    for f in range(HT):
                        hid(b, f)
                        if f == 1 and b:
                            add(b - 1)
                        if p == 0 and (b, f) in early:
                            attend(parts, [early[b, f]])
                add(NB - 1)

            ffn(0)

            dve.wait_ge(s_fa, NB)
            attend(parts)
            ffn(1)

        @block.tensor
        def _(pe):
            T = nc.tensor

            def mm(o, l, rr, start=True, stop=True):
                return T.matmul(o, l, rr, start=start, stop=stop)

            pe.wait_ge(s_const, 2)
            pe.wait_ge(s_wflt, 1)
            pe.wait_ge(s_aw, 16 * 9)
            for n, (o, l, rr, turned, _, need) in enumerate(prep):
                wait(pe, s_wpc, max(need, n - 7))
                (T.transpose(o, l, rr) if turned else mm(o, l, rr)).then_inc(s_wp, 1)
            pe.wait_ge(s_wpc, NPREP)
            pe.wait_ge(s_dconst, 1)

            for h in range(HB):
                if h:
                    pe.wait_ge(s_rx, h)
                for c in range(HB):
                    b = HB * h + c
                    pe.wait_ge(s_nb, b + 1)
                    for j in range(TB):
                        last = T.transpose(ps[:, c, j * P:j * P + P], nb[:, c, j, :], ident[:])
                    last.then_inc(s_tr, 1)
                pe.wait_ge(s_xT, HB * h + HB)
                for c in range(HB):
                    banks = ((2, 3, 4, 5), (6, 7, 0, 1))[c]
                    for m in range(4):
                        mm(bank(banks[m]), ipw[:, m * P:m * P + P], xT[:, c, :]).then_inc(s_ip, 1)
                for c in range(HB):
                    b = HB * h + c
                    pe.wait_ge(s_xi, 2 * b + 2)
                    for e in range(CT):
                        for k in range(DC):
                            last = mm(bank((2, 6)[c] + e), convd[:, e, k, :], xip[:, c, e, 1 + k:1 + k + L],
                                      start=(k == 0), stop=(k == DC - 1))
                        last.then_inc(s_cv, 1)
                for c in range(HB):
                    b = HB * h + c
                    pe.wait_ge(s_zs, 2 * b + 2)
                    pe.wait_ge(s_xc, 2 * b + 2)
                    d_bank, bc_bank = ((4, 5), (0, 1))[c]
                    for e in range(CT):
                        last = mm(ps[0:RK, d_bank, :], xpw[:, e, :], xc[:, e, c * L:c * L + L],
                                  start=(e == 0), stop=(e == CT - 1))
                    last.then_inc(s_pj, 1)
                    for e in range(CT):
                        last = mm(ps[0:96, bc_bank, :], bcw[:, e, :, :].rearrange("p q n -> p (q n)"),
                                  xc[:, e, c * L:c * L + L], start=(e == 0), stop=(e == CT - 1))
                    last.then_inc(s_pj, 1)
                for c in range(HB):
                    b = HB * h + c
                    pe.wait_ge(s_dts, b + 1)
                    for e in range(CT):
                        mm(bank((2, 6)[c] + e), dtw[0:RK, e * P:e * P + P], dts[0:RK, c, :]).then_inc(s_dtp, 1)
                pe.wait_ge(s_v, HB * h + HB)
                pe.wait_ge(s_bc3, HB * h + HB)
                for e in range(CT):
                    for c in range(HB):
                        mm(bank(2 * e + c), dskd[:, e, :], xc[:, e, c * L:c * L + L], stop=False)

                def ysum(k, e, stop):
                    for c in range(HB):
                        last = mm(bank(2 * e + c), ident[:], hC[:, k, e, c * L:c * L + L], start=False, stop=stop)
                    last.then_inc(s_ys, 1)

                def row(n):
                    return sel[0:96, bass.ds(n, 1), :].rearrange("p o q -> p (o q)")

                def spread_b(n):
                    pe.wait_ge(s_bs, n + h * NS)
                    for c in range(HB):
                        last = mm(bank(6 + c), row(n), bc3[0:96, c * L:c * L + L])
                    last.then_inc(s_bps, 1)

                def state(n, k):
                    gn = n + h * NS
                    pe.wait_ge(s_hc, 2 * gn + 2)
                    for c in range(HB):
                        last = mm(bank(4 + c), row(n + NS), bc3[0:96, c * L:c * L + L])
                    last.then_inc(s_cps, 1)
                    for e in range(CT):
                        ysum(1 - k, e, False)

                for bk, r0, done in ((6, 0, s_bps), (4, NS, s_cps)):
                    for c in range(HB):
                        last = mm(bank(bk + c), sel[0:96, r0, :], bc3[0:96, c * L:c * L + L])
                    last.then_inc(done, 1)
                spread_b(1)
                spread_b(2)
                state(1, 1)
                with pe.Fori(1, NS // 2 - 1) as pair:
                    for k in range(2):
                        spread_b(pair * 2 + k + 1)
                        state(pair * 2 + k, k)
                spread_b(NS - 1)
                state(NS - 2, 0)
                state(NS - 1, 1)
                pe.wait_ge(s_hc, 2 * NS * (h + 1) + 2)
                for e in range(CT):
                    ysum(1, e, True)
                pe.wait_ge(s_yg, 2 * h + 2)
                for c in range(HB):
                    for j in range(TB):
                        for e in range(CT):
                            last = mm(ps[:, 4 + c, j * P:j * P + P], zs[:, e, c * L + j * P:c * L + j * P + P],
                                      opw[:, e, :], start=(e == 0), stop=(e == CT - 1))
                    last.then_inc(s_op, 1)
                for c in range(HB):
                    b = HB * h + c
                    pe.wait_ge(s_h2, b + 1)
                    for j in range(TB):
                        last = T.transpose(ps[:, 6 + c, j * P:j * P + P], nb[:, c, j, :], ident[:])
                    last.then_inc(s_tr2, 1)
                for c in range(HB):
                    b = HB * h + c
                    pe.wait_ge(s_h2T, b + 1)
                    for j in range(TB):
                        t = c * TB + j
                        last = mm(ps[:, 4, t * NE:t * NE + NE], h2T[:, b, j * P:j * P + P], rw[:])
                last.then_inc(s_rt, 1)

            pe.wait_ge(s_rx, HB)
            with pe.Fori(0, NE // 2) as pair:
                e0 = pair * 2
                def gate_up(j, f):
                    k, b = j // NB, j % NB
                    m = e0 * (NB * FT) + (j * FT + f)
                    pe.wait_ge(s_hm, m + 1)
                    mm(bank(f % 2), moew[:, k, 0, f * P:f * P + P], h2T[:, b, :]).then_inc(s_g, 1)
                    mm(bank(2 + f % 2), moew[:, k, 1, f * P:f * P + P], h2T[:, b, :]).then_inc(s_u2, 1)

                def down(j):
                    k = j // NB
                    pe.wait_ge(s_hm, e0 * (NB * FT) + (j * FT + FT + 2))
                    pe.wait_ge(s_acc, e0 * NB + j + 1)
                    for t in range(TB):
                        for f in range(FT):
                            last = mm(ps[:, 4 + j % 2, t * P:t * P + P], hh[:, j % 2, f, t * P:t * P + P],
                                      moew[:, k, 2, f * P:f * P + P], start=(f == 0), stop=(f == FT - 1))
                    last.then_inc(s_dn, 1)

                for j in range(2 * NB):
                    if j % NB == 0:
                        pe.wait_ge(s_mw[j // NB], e0 * 24 + 48)
                    for f in range(FT):
                        gate_up(j, f)
                        if f == 0 and j:
                            down(j - 1)
                down(2 * NB - 1)
            pe.wait_ge(s_acc, 2 + NE * NB)

            bank7_read = [[(s_fxT, NB)]]

            def bank7(reader, count):
                for s, n in bank7_read[0]:
                    pe.wait_ge(s, n)
                bank7_read[0] = list(zip(reader, count))

            def turn(b):
                pe.wait_ge(s_an, b + 1)
                bank7((s_axT,), (b + 1,))
                for j in range(TB):
                    last = T.transpose(ps[:, 7, j * P:j * P + P], nb[:, b % 2, j, :], ident[:])
                last.then_inc(s_at, 1)

            def qk(b, w):
                bank7((s_qh, s_qr), (2 * b + w + 1,) * 2)
                pe.wait_ge(s_axT, b + 1)
                mm(bank(7), (wqq, mT)[w][:], xT[:, b % 2, :]).then_inc(s_aq, 1)

            def vals(b):
                bank7((s_vv,), (b + 1,))
                for j in range(TB):
                    last = mm(ps[:, 7, j * P:j * P + P], xT[:, b % 2, j * P:j * P + P], vx[:])
                last.then_inc(s_av, 1)

            nmax = [0]

            def maxima(b, j, qt):
                if nmax[0] % (2 * PAIRS * TB) == 0:
                    for w in range(2):
                        pe.wait_ge(s_qk[b][w], 16 * 14)
                for r in range(2):
                    m = nmax[0]
                    nmax[0] += 1
                    rows = slice(64 * r, 64 * r + QR)
                    wait(pe, s_mx, m - 1)
                    mm(ps[:, 4 + m % 2, 0:(qt + 1) * P], qq[rows, b, j, qt * P:qt * P + P],
                       kk[rows, b, j, 0:(qt + 1) * P]).then_inc(s_s1, 1)

            def place_max(b):
                pe.wait_ge(s_m3, b + 1)
                bank7((s_mr,), (b + 1,))
                for qt in range(TB):
                    last = T.transpose(max_rows[:, qt * P:qt * P + P],
                                       m3[:, b % 2, qt, :, :, :].rearrange("p r c j -> p (r c j)"), identb[:])
                last.then_inc(s_mt, 1)

            def scores(c, q):
                b, u, kt = c // UNITS, c // TB % 4, c % TB
                if c % UNITS == 0 and q == 0:
                    pe.wait_ge(s_mp[b], 32)
                wait(pe, s_ex, 2 * (c - 1) + q + 1)
                for r in range(2):
                    rows = slice(64 * r, 64 * r + MR)
                    mm(ps[:, 2 * q + r, kt * P:L], kk[rows, b, 2 * u + q, kt * P:kt * P + P],
                       qq[rows, b, 2 * u + q, kt * P:L], stop=False)
                for r in range(2):
                    last = mm(ps[:, 2 * q + r, kt * P:kt * P + P], identb[:], kmask[:], start=False)
                last.then_inc(s_s2, 1)

            def values(c):
                b, u, kt = c // UNITS, c // TB % 4, c % TB
                pe.wait_ge(s_ex, 2 * c + 2)
                if kt == 0:
                    wait(pe, s_ot, c // TB)
                for g in range(4):
                    last = mm(ps[32 * g:32 * g + 32, 6, kt * P:L], vv[:, b, kt, 4 * u + g, :],
                              pt[:, c % 2, g, kt * P:L], start=(kt == 0), stop=(kt == TB - 1))
                last.then_inc(s_pv, 1)

            def finish(b, qt):
                pe.wait_ge(s_ot, 4 * (b + 1))
                bank7((s_ya,), (b * TB + qt + 1,))
                for u in range(4):
                    last = T.transpose(ps[:, 7, u * P:u * P + P], ot[:, u, qt * P:qt * P + P], ident[:])
                last.then_inc(s_ott, 1)

            parts = dict(turn=turn, qk=qk, vals=vals, maxima=maxima, place_max=place_max, scores=scores,
                         values=values, finish=finish)

            def ffn(p):
                def head(b):
                    q = p * NB + b
                    pe.wait_ge(s_fn, q + 1)
                    wait(pe, s_fxT, q - 1)
                    for j in range(TB):
                        last = T.transpose(ps[:, 6 + b % 2, j * P:j * P + P], nb[:, b % 2, j, :], ident[:])
                    last.then_inc(s_ft, 1)

                def gate_up(b, f):
                    m = (p * NB + b) * HT + f
                    wait(pe, s_fh, m - 1)
                    mm(bank(m % 2), wgT[:, f * P:f * P + P], xT[:, b % 2, :]).then_inc(s_fg, 1)
                    mm(bank(2 + m % 2), wuT[:, f * P:f * P + P], xT[:, b % 2, :]).then_inc(s_fu, 1)

                def down(b):
                    q = p * NB + b
                    pe.wait_ge(s_fh, q * HT + HT)
                    wait(pe, s_fa, q - 1)
                    for t in range(TB):
                        for f in range(HT):
                            last = mm(ps[:, 4 + b % 2, t * P:t * P + P], fhh[:, b % 2, f, t * P:t * P + P],
                                      wdT[:, f, :], start=(f == 0), stop=(f == HT - 1))
                    last.then_inc(s_fd, 1)

                head(0)
                for b in range(NB):
                    if b + 1 < NB:
                        head(b + 1)
                    pe.wait_ge(s_fxT, p * NB + b + 1)
                    for f in range(HT):
                        gate_up(b, f)
                        if f == 0 and b:
                            down(b - 1)
                        if p == 0 and (b, f) in early:
                            attend(parts, [early[b, f]])
                down(NB - 1)

            ffn(0)

            pe.wait_ge(s_fa, NB)
            pe.wait_ge(s_vv0, 2)
            pe.wait_ge(s_ones, 16 * 2 * NB)
            attend(parts)
            ffn(1)


_INS = ["hidden_states", "rms1_w", "rms2_w", "in_proj_w", "conv_w", "conv_b", "x_proj_w", "dt_proj_w",
        "dt_proj_b", "A_log", "D_skip", "out_proj_w", "router_w", "Wg", "Wu", "Wd"]
_INS = ["L0_attn_a_" + n for n in _INS] + ["L0_attn_b_" + n for n in
                                           ("W_dq", "W_uq", "W_dkv", "W_uk", "W_uv", "W_o")]
_INS += ["L0_ffn_" + n for n in ("w_gate", "w_up", "w_down")]
_SHAPE = (4, 512, 128)


def kernel(**inputs):
    import numpy as _np
    import concourse.bacc as _bacc
    from concourse import mybir as _mybir
    from concourse.bass_utils import run_bass_kernel_spmd as _run

    nc = _bacc.Bacc("TRN2", target_bir_lowering=False, num_devices=1)
    arrays, args = {}, []
    for name in _INS:
        a = _np.ascontiguousarray(inputs[name])
        arrays[f"in_{name}"] = a
        args.append(nc.dram_tensor(f"in_{name}", a.shape, _mybir.dt.from_np(a.dtype), kind="ExternalInput").ap())
    out = nc.dram_tensor("out_0", _SHAPE, _mybir.dt.float32, kind="ExternalOutput").ap()
    build(nc, *args, out)
    r = _run(nc, [arrays], core_ids=[0])
    return r.results[0]["out_0"]
```

```python
from contextlib import ExitStack

import concourse.bass as bass
from concourse import mybir

F32 = mybir.dt.float32
BF16 = mybir.dt.bfloat16
F32R = mybir.dt.float32r
I32 = mybir.dt.int32
U32 = mybir.dt.uint32
ALU = mybir.AluOpType
ACT = mybir.ActivationFunctionType
AX = mybir.AxisListType.X

P = 128
EPS = 1e-5
NEG = -1.0e38


class Chain:

    def __init__(self, eng, sem):
        self.eng, self.sem, self.n = eng, sem, 0

    def link(self, ins):
        self.n += 1
        ins.then_inc(self.sem, 1)
        self.eng.wait_ge(self.sem, self.n)


def build(nc, x_in, rms1_w, rms2_w, in_proj_w, conv_w, conv_b, x_proj_w, dt_proj_w, dt_proj_b,
          A_log, D_skip, out_proj_w, router_w, Wg, Wu, Wd, W_dq, W_uq, W_dkv, W_uk, W_uv, W_o,
          w_gate, w_up, w_down, out):
    NB, L, D = x_in.shape
    NT = NB * L // P
    TB = L // P
    DI = in_proj_w.shape[1] // 2
    CT = DI // P
    NS = A_log.shape[1]
    DC = conv_w.shape[2]
    RK = dt_proj_w.shape[0]
    NE, _, FF = Wg.shape
    FT = FF // P
    HID = w_gate.shape[0]
    HT = HID // P
    QL, KVL = W_dq.shape[0], W_dkv.shape[0]
    NH, HS = 16, D // 16
    HG = 4
    HB = 2
    HL = HB * L
    QS = float(HS) ** -0.5
    DQ = 1.0 / 127.0
    assert HT == 3 and FF == L and D == P and L == 512 and CT == 2 and FT == 4 and NH == HG * 4

    xd = x_in.rearrange("b (j p) d -> b p j d", p=P)
    od = out.rearrange("b (j p) d -> b p j d", p=P)

    ctx = ExitStack()
    with ctx:
        def sb(name, shape, dt=F32):
            return ctx.enter_context(nc.sbuf_tensor(name, shape, dt))

        def sem(name):
            return ctx.enter_context(nc.semaphore(name))

        ps = ctx.enter_context(nc.psum_tensor("ps", [P, 8, 512], F32))

        def bank(k, n=1):
            return ps[:, k, :] if n == 1 else ps[:, k:k + n, :]

        x = sb("x", [P, NT, D])
        r = sb("r", [P, NT, D])
        nb = sb("nb", [P, 2, TB, D])
        xT = sb("xT", [P, 2, L])
        stats = sb("stats", [P, NT, 6])
        mv = sb("mv", [P, NT, 2])
        small = sb("small", [P, 4, NT])
        ident = sb("ident", [P, P])
        cmask = sb("cmask", [P, L])
        identb = sb("identb", [P, P], BF16)
        kmask = sb("kmask", [P, P], BF16)
        neghalf = sb("neghalf", [P, NT])
        moew = sb("moew", [P, 2, 3, FF])
        wgT = sb("wgT", [P, HID])
        wuT = sb("wuT", [P, HID])
        wdT = sb("wdT", [P, HT, D])
        mT = sb("mT", [P, D])
        vx = sb("vx", [P, D])
        w1c = sb("w1c", [P, 1])
        w2c = sb("w2c", [P, 1])
        rw = sb("rw", [P, NE])
        wtok = sb("wtok", [P, NT, NE])
        iota8 = sb("iota8", [P, NE])
        wqq = sb("wqq", [P, D])
        m8 = sb("m8", [P, NT])

        ARENA = 32 * 1024
        arena = sb("arena", [P, ARENA])
        at = [0]
        LATE = 4 * CT * HL
        with nc.sbuf_tensor("late", [P, LATE], F32) as late:
            pass
        w_hi = sb("w_hi", [P, 2, 2, FF], F32R)
        w_lo = sb("w_lo", [P, 2, 2, FF], F32R)
        x_hi = sb("x_hi", [P, NB, L], F32R)
        x_lo = sb("x_lo", [P, NB, L], F32R)

        def late_carve(first, shape):
            n = 1
            for d in shape:
                n *= d
            names = " ".join(f"a{i}" for i in range(len(shape)))
            return late[:, first:first + n].rearrange(f"p ({names}) -> p {names}",
                                                      **{f"a{i}": d for i, d in enumerate(shape)})

        def carve(shape, dt=F32):
            n = 1
            for s in shape:
                n *= s
            words = n if dt != BF16 else n // 2
            a = arena[:, at[0]:at[0] + words]
            at[0] += words
            assert at[0] <= ARENA, at[0]
            if dt != F32:
                a = a.bitcast(dt)
            names = " ".join(f"a{i}" for i in range(len(shape)))
            if len(shape) == 1:
                return a
            return a.rearrange(f"p ({names}) -> p {names}", **{f"a{i}": s for i, s in enumerate(shape)})

        ipw = carve([2 * DI])
        xpw = carve([CT, RK + 2 * NS])
        dtw = carve([DI])
        opw = carve([CT, D])
        convw = carve([CT, DC])
        convb = carve([CT])
        dtb = carve([CT])
        dsk = carve([CT])
        aneg = carve([CT, NS])
        convd = carve([DC, P])
        dskd = carve([CT, P])
        sel = carve([2 * NS, P], BF16)
        selr = carve([2 * NS])
        h2T = carve([NB, L])
        moe_from = at[0]
        xip = carve([HB, CT, L + 4])
        xc = carve([CT, HL])
        zs = carve([CT, HL])
        delta = carve([CT, HL])
        dx = carve([CT, HL])
        dts = carve([HB, L])
        bc3 = carve([HL], BF16)
        scan_from = at[0]
        v = carve([HB, CT, L])
        u = carve([HB, CT, L])
        bcr = carve([HB, L])
        bcp = carve([HB, 2, L], BF16)
        v_to = at[0]
        at[0] = scan_from
        dA = late_carve(0, [2, CT, HL])
        dBx = late_carve(LATE // 2, [2, CT, HL])
        hst = carve([CT, HL])
        hC = carve([2, CT, HL])
        at[0] = max(at[0], v_to)
        wint = carve([3, HID], I32)
        wflt = carve([3, HID])
        adq, auq, adkv, auk, auv, ao = (carve([P]) for _ in range(6))
        auqT, aoT, aqqT, akT, av = (carve([P]) for _ in range(5))
        bs = carve([2, HL])
        at[0] = scan_from
        rmax = carve([NT, 8])
        ridx = carve([NT, 8], U32)
        req = carve([2, NT, NE])
        at[0] = moe_from
        sg = carve([2, L])
        hh = carve([2, FT, L])
        moe_to = at[0]
        at[0] = 0
        QR = 7 * HS
        MR = QR + 3
        SL = 3
        onesr = carve([L], BF16)
        zeror = carve([L], BF16)
        assert at[0] <= 2 * DI
        qq = carve([SL, NH // 2, L], BF16)
        pt = late_carve(0, [2, 4, L])
        ot = late_carve(8 * L, [4, L])
        qr = late_carve(12 * L, [2, L])
        nm = carve([2, TB, 2, NH // 2])
        nr = carve([2, TB, 2, NH // 2])
        m3 = carve([2, 2, TB, 2, 3, NH // 4], BF16)
        assert at[0] >= moe_from
        qp = carve([2, 3, L], BF16)
        mrow = carve([2, L], BF16)
        junk = late_carve(14 * L, [2, L])
        assert 16 * L <= LATE
        rs = carve([TB, NH])
        yn = carve([TB, D])
        fsg = carve([2, L])
        xA = carve([L])
        xE = carve([L])
        at[0] = max(at[0], moe_to)
        kz = carve([SL, 2, NH // 2, L], BF16)
        vv = carve([NB, TB, NH, 32])
        fhh = moew

        s_x = [sem(f"x_loaded{b}") for b in range(NB)]
        s_w = sem("mamba_weights_loaded")
        s_aw = sem("attn_ffn_weights_loaded")
        s_out = sem("out_stored")
        s_dch = sem("dve_chain")
        s_ach = sem("act_chain")
        s_pch = sem("pool_chain")
        s_const = sem("constants_ready")
        s_dconst = sem("dve_constants_ready")
        s_wflt = sem("ffn_weights_float")
        s_wp = sem("weight_prep_matmul")
        s_wpc = sem("weight_prep_copied")
        s_var = sem("variance_ready")
        s_rstd = sem("rstd_ready")
        s_nb = sem("tokens_normalised")
        s_tr = sem("transposed")
        s_xT = sem("xT_ready")
        s_ip = sem("in_proj_done")
        s_xi = sem("xi_ready")
        s_zs = sem("z_ready")
        s_cv = sem("conv_done")
        s_cd = sem("conv_on_dve_done")
        s_cc = sem("conv_on_dve_step")
        s_xc = sem("xc_ready")
        s_pj = sem("x_proj_done")
        s_dts = sem("dt_ready")
        s_bc3 = sem("bc_split_ready")
        s_dtp = sem("dt_proj_done")
        s_v = sem("softplus_input_ready")
        s_aexp = sem("exp_A_ready")
        s_ones = sem("ones_placed")
        s_pad = sem("attn_padding_ready")
        s_rs = sem("reciprocal_sum_ready")
        s_u = sem("softplus_log_ready")
        s_dl = sem("delta_ready")
        s_dx = sem("dx_ready")
        s_bps = sem("b_broadcast_done")
        s_cps = sem("c_broadcast_done")
        s_bs = sem("b_copied")
        s_da = sem("dA_ready")
        s_dbx = sem("dBx_ready")
        s_scan = sem("scan_done")
        s_hc = sem("hC_ready")
        s_ys = sem("y_summed")
        s_yg = sem("y_gated")
        s_op = sem("out_proj_done")
        s_r = sem("residual_ready")
        s_h2 = sem("h2_ready")
        s_tr2 = sem("h2_transposed")
        s_h2T = sem("h2T_ready")
        s_rt = sem("router_done")
        s_rx = sem("router_logits_copied")
        s_rs2 = sem("router_shifted")
        s_re = sem("router_exp")
        s_wt = sem("router_weights_ready")
        s_mw = [sem(f"expert_loaded{k}") for k in range(2)]
        s_g = sem("gate_done")
        s_u2 = sem("up_done")
        s_sg = sem("silu_done")
        s_wh = sem("expert_rounded")
        s_ws = sem("expert_split")
        s_hs = sem("moe_input_split")
        s_hm = sem("hidden_ready")
        s_dn = sem("down_done")
        s_acc = sem("expert_added")
        s_fn = sem("ffn_normalised")
        s_ft = sem("ffn_transposed")
        s_fxT = sem("ffn_xT_ready")
        s_fg = sem("ffn_gate_done")
        s_fu = sem("ffn_up_done")
        s_fs = sem("ffn_silu_done")
        s_fh = sem("ffn_hidden_ready")
        s_fd = sem("ffn_down_done")
        s_fa = sem("ffn_added")
        s_an = sem("attn_normalised")
        s_at = sem("attn_transposed")
        s_axT = sem("attn_xT_ready")
        s_aq = sem("attn_qk_done")
        s_av = sem("attn_v_done")
        s_qh = sem("first_part_ready")
        s_qr = sem("rest_ready")
        s_qp = sem("parts_ready")
        s_qk = [[sem(f"{w}_rows_placed{b}") for w in "qk"] for b in range(NB)]
        s_qz = [sem(f"q_zeros_placed{b}") for b in range(NB)]
        s_vv = sem("v_ready")
        s_s1 = sem("scores_q_major")
        s_mx = sem("row_max_ready")
        s_m3 = sem("max_parts_ready")
        s_mt = sem("max_transposed")
        s_mr = sem("max_rows_ready")
        s_mp = [[sem(f"max_rows_placed{b}_{q}") for q in range(2)] for b in range(NB)]
        s_s2 = sem("scores_k_major")
        s_ex = sem("exp_done")
        s_pv = sem("pv_done")
        s_ot = sem("o_copied")
        s_ott = sem("o_transposed")
        s_yn = sem("attn_divided")
        s_ya = sem("attn_added")

        block = ctx.enter_context(nc.Block())

        def wait(eng, s, n):
            if not isinstance(n, int) or n > 0:
                eng.wait_ge(s, n)

        def tiles(b):
            return slice(TB * b, TB * b + TB)

        max_rows = bank(7).bitcast(BF16)[0:6 * (NH // 4), 0:L]

        def ffn_input(p, b):
            return (xT[:, 0, :], xT[:, 1, :], xE[:, 0:L], xT[:, 0, :])[b] if p else h2T[:, b, :]

        def o_bank(b, qt):
            return 6 if b == NB - 1 and qt % 2 else 7

        def tiles_of(h):
            return slice(2 * TB * h, 2 * TB * h + 2 * TB)

        def mamba_in(h, c):
            return h2T[:, HB + c, :] if h else xT[:, c, :]

        loads = [(w1c[:, :], rms1_w.rearrange("(p o) -> p o", o=1)),
                 (w2c[:, :], rms2_w.rearrange("(p o) -> p o", o=1)),
                 (ipw[:, :], in_proj_w), (dtw[0:RK, :], dt_proj_w), (rw[:, :], router_w),
                 (convw[:, :, :], conv_w.rearrange("(e p) o k -> p e (o k)", p=P)),
                 (aneg[:, :, :], A_log.rearrange("(e p) n -> p e n", p=P)),
                 (opw[:, :, :], out_proj_w.rearrange("(e p) d -> p e d", p=P))]
        loads += [(dst[:, e:e + 1], src[e * P:e * P + P].rearrange("(p o) -> p o", o=1))
                  for e in range(CT) for dst, src in ((convb, conv_b), (dtb, dt_proj_b), (dsk, D_skip))]
        loads.append((xpw[:, :, :], x_proj_w.rearrange("(e p) n -> p e n", p=P)))

        def turn(rows, cols=P):
            turn.n += 1
            return ps[0:rows, (turn.n - 1) % 4, 0:cols]

        turn.n = 0
        prep = []
        for src, dst in ((0, wgT), (1, wuT), (2, None)):
            for t in range(HT):
                cs = slice(t * P, t * P + P)
                prep.append((turn(P), wflt[:, src, cs], ident[:], True,
                             wdT[:, t, :] if dst is None else dst[:, cs], 0))
        n0 = len(prep)
        prep += [(turn(QL), auq[:, 0:QL], ident[:], True, auqT[0:QL, :], 0),
                 (turn(P), ao[:, :], ident[:], True, aoT[:, :], 0),
                 (turn(P), adq[0:QL, :], auqT[0:QL, :], False, wqq[:], n0 + 1),
                 (turn(P), auqT[0:QL, :], adq[0:QL, :], False, aqqT[:, :], n0 + 1),
                 (turn(KVL), auk[:, 0:KVL], aqqT[:, :], False, akT[0:KVL, :], n0 + 4),
                 (turn(KVL), auv[:, 0:KVL], aoT[:, :], False, av[0:KVL, :], n0 + 2),
                 (turn(P), adkv[0:KVL, :], akT[0:KVL, :], False, mT[:], n0 + 5),
                 (turn(P), adkv[0:KVL, :], av[0:KVL, :], False, vx[:], n0 + 6)]
        NPREP = len(prep)

        turns = (((0, 0, 0), (0, 2, P)), ((1, 0, 0), (1, 2, P)), ((0, 1, 0), (1, 1, 2 * P)), ((0, 3, 0),), ((1, 3, 0),))
        TURNS = len(turns)

        PAIRS, UNITS, LAG = NH // 2, (NH // 4) * TB, 2
        HP = PAIRS // 2
        uses = {"qk": "qk_rest", "o_turn": "o_add"}
        PATTERN = (("maxima", 0, "use", "maxima", 1, "maxima", "values", "short"),
                   (0, "use", "maxima", 1, "maxima", "values", "short"))
        steps, later, use = [], [], []
        for a in range(NB * PAIRS + HP + LAG):
            b, j = divmod(a, PAIRS)
            for n in range(1, NB):
                if a == max(0, PAIRS * n - 10):
                    later += [("norm", n), None, ("normalise", n), ("turn", n), ("qk", n, 0), ("qk", n, 1), ("vals", n)]
            turn_n = 0
            for i in range(2):
                c = 2 * (a - HP - LAG) + i
                unit = 0 <= c < NB * UNITS
                for part in PATTERN[i]:
                    if part == "maxima":
                        if b < NB:
                            steps.append(("maxima", b, j, turn_n))
                        turn_n += 1
                    elif part in (0, 1):
                        if unit:
                            steps.append(("scores", c, part))
                    elif part == "values":
                        if 0 < c <= NB * UNITS:
                            steps.append(("values", c - 1))
                            if c % UNITS == 0:
                                o = c // UNITS - 1
                                later = [("o_turn", o, qt) for qt in range(TB)] + later
                                if o < NB - 1:
                                    later += [("f_norm", 1, o), ("f_normalise", 1, o), ("f_turn", 1, o)]
                    elif part == "use":
                        steps += use
                        use = []
                    elif later:
                        short = later.pop(0)
                        if short:
                            steps.append(short)
                            if short[0] in uses:
                                use = [(uses[short[0]],) + short[1:]]
            if b < NB and j % HP == HP - 1:
                steps.append(("split_max", b, j // HP))
                later = [None, ("place_max", b, j // HP)] + later
        steps.append(("values", NB * UNITS - 1))
        steps += use
        last = NB - 1
        in_moe = {(NB + 1, 2): [("f_norm", 0, 0)], (NB + 1, 3): [("f_normalise", 0, 0)], (NB + 2, 1): [("f_turn", 0, 0)],
                  (NB + 2, 2): [("f_norm", 0, 1)], (NB + 2, 3): [("f_normalise", 0, 1)], (NB + 3, 1): [("f_turn", 0, 1)],
                  (NB + 3, 2): [("f_norm", 0, 2)], (NB + 3, 3): [("f_normalise", 0, 2)]}
        before = [[("f_turn", 0, 2), ("f_norm", 0, 3)], [("o_turn", last, 0), ("o_turn", last, 1)] + later]
        in_ffn = [{(0, 0): [("f_normalise", 0, 3)], (0, 2): [("f_turn", 0, 3)], (1, 1): [("norm", 0)],
                   (1, 2): [("normalise", 0)], (2, 0): [("turn", 0)], (2, 1): [("qk", 0, 0), ("qk_rest", 0, 0)],
                   (2, 2): [("qk", 0, 1), ("qk_rest", 0, 1)], (3, 0): [("vals", 0)]},
                  {(0, 0): [("o_add", last, 0), ("o_turn", last, 2), ("o_add", last, 1)],
                   (0, 1): [("o_turn", last, 3), ("o_add", last, 2)], (0, 2): [("o_add", last, 3), ("f_norm", 1, 3)],
                   (1, 0): [("f_normalise", 1, 3)], (1, 1): [("f_turn", 1, 3)]}]
        whole = [event for events in in_moe.values() for event in events]
        for p in range(2):
            whole += before[p] + [event for events in in_ffn[p].values() for event in events] + (steps if p == 0 else [])

        def attend(parts, events):
            for name, *args in events:
                if name in parts:
                    parts[name](*args)

        @block.sync
        def _(sp):
            sp.sem_inc(s_dbx, 4)
            sp.sem_inc(s_scan, 4)
            sp.sem_inc(s_ys, 4)
            sp.sem_inc(s_hc, 2)
            sp.sem_inc(s_hm, 2)
            sp.sem_inc(s_dn, 8)
            sp.sem_inc(s_acc, 2)
            for b in range(NB):
                sp.dma_start(x[:, tiles(b), :], xd[b]).then_inc(s_x[b], 16)
            sp.wait_ge(s_w, 16 * len(loads))
            for dst, src in (
                (wint[:, 0, :].rearrange("p (t d) -> p t d", t=HT), w_gate.rearrange("(t p) d -> p t d", p=P)),
                (wint[:, 1, :].rearrange("p (t d) -> p t d", t=HT), w_up.rearrange("(t p) d -> p t d", p=P)),
                (wint[:, 2, :], w_down),
                (adq[0:QL, :], W_dq), (auq[:, 0:QL], W_uq), (adkv[0:KVL, :], W_dkv),
                (auk[:, 0:KVL], W_uk), (auv[:, 0:KVL], W_uv), (ao[:, :], W_o),
            ):
                sp.dma_start(dst, src).then_inc(s_aw, 16)
            with sp.Fori(0, NE // 2) as pair:
                e0 = pair * 2
                for k in range(2):
                    sp.wait_ge(s_dn, e0 * 4 + 4 * (k + 1))
                    e = e0 + k
                    for i, w in enumerate((Wg, Wu)):
                        sp.dma_start(moew[:, k, i, :],
                                     w[bass.ds(e, 1), :, :].rearrange("e p f -> (e p) f")).then_inc(s_mw[k], 16)
                    sp.dma_start(moew[:, k, 2, :].rearrange("p (t d) -> p t d", t=FT),
                                 Wd[bass.ds(e, 1), :, :].rearrange("e (t p) d -> p (e t) d", p=P)).then_inc(s_mw[k], 16)
            sp.wait_ge(s_pad, 3)
            for g in range(SL):
                for r in range(2):
                    sp.dma_start(kz[64 * r + QR:64 * r + MR, g, r, :, :],
                                 onesr[0:3, :].unsqueeze(1).to_broadcast([3, PAIRS, L])).then_inc(s_ones, 16)
            sp.wait_ge(s_acc, 2 + NE * NB)

            def place_zeros(b):
                for r in range(2):
                    sp.dma_start(qq[64 * r + QR:64 * r + 64, b % SL, :, :],
                                 zeror[0:64 - QR, :].unsqueeze(1).to_broadcast([64 - QR, PAIRS, L])
                                 ).then_inc(s_qz[b], 16)

            def place(b, w, parts):
                g = b % SL
                for n, part in enumerate(((0, 0, 1, 0, 2, 1, 1), (0, 1, 0, 2, 0, 1, 2))[w]):
                    if part in parts:
                        for r in range(2):
                            rows = slice(64 * r + HS * n, 64 * r + HS * n + HS)
                            sp.dma_start(kz[rows, g, r, :, :] if w else qq[rows, g, :, :],
                                         qp[64 * r:64 * r + 64, w, part, :]).then_inc(s_qk[b][w], 16)

            def place_first(b, w):
                if b >= SL:
                    sp.wait_ge(s_s2, 2 * UNITS * (b - SL + 1))
                if w == 0 and b:
                    place_zeros(b)
                sp.wait_ge(s_qh, 2 * b + w + 1)
                place(b, w, (0,))

            def place_rest(b, w):
                sp.wait_ge(s_qp, 2 * (2 * b + w) + 2)
                place(b, w, (1, 2))

            place_zeros(0)
            attend(dict(qk=place_first, qk_rest=place_rest), whole)
            for b in range(NB):
                sp.wait_ge(s_fa, NB + b + 1)
                sp.dma_start(od[b], x[:, tiles(b), :]).then_inc(s_out, 16)
            sp.wait_ge(s_out, 16 * NB)

        @block.gpsimd
        def _(pool):
            G = nc.gpsimd
            ch = Chain(pool, s_pch)
            G.memset(ident[:], 0.0)
            G.memset(selr[:, :], 0.0)
            G.memset(cmask[:], 0.0)
            G.memset(kmask[:], 0.0)
            ch.link(G.memset(neghalf[:], -0.5))
            G.affine_select(out=ident[:], in_=ident[:], compare_op=ALU.not_equal, fill=1.0, base=0,
                            pattern=[[-1, P]], channel_multiplier=1).then_inc(s_const, 1)
            G.affine_select(out=cmask[:, L - P:L], in_=cmask[:, L - P:L], compare_op=ALU.is_ge, fill=NEG,
                            base=0, pattern=[[-1, P]], channel_multiplier=1)
            G.affine_select(out=kmask[:], in_=kmask[:], compare_op=ALU.is_ge, fill=NEG,
                            base=0, pattern=[[1, P]], channel_multiplier=-1)
            G.iota(iota8[:], pattern=[[1, NE]], base=0, channel_multiplier=0,
                   allow_small_or_imprecise_dtypes=True)
            for q in range(3):
                ch.link(G.affine_select(out=selr[:, :], in_=selr[:, :], compare_op=ALU.not_equal, fill=1.0,
                                        base=-2 * NS * q, pattern=[[-1, 2 * NS]], channel_multiplier=1))
            pool.sem_inc(s_const, 1)

            asked = [0]

            def powers(col, width):
                asked[0] += 1
                pool.wait_ge(s_var, asked[0])
                G.tensor_tensor(small[:, 2, col:col + width], small[:, 1, col:col + width],
                                neghalf[:, col:col + width], ALU.pow).then_inc(s_rstd, 1)

            for h in range(HB):
                powers(2 * TB * h, 2 * TB)
                powers(2 * TB * h, 2 * TB)
            pool.wait_ge(s_aw, 16 * 9)
            G.tensor_copy(wflt[:, :, :], wint[:, :, :]).then_inc(s_wflt, 1)
            for h in range(HB):
                pool.wait_ge(s_dl, HB * h + 1)
                G.tensor_tensor(dx[:, :, 0:L], delta[:, :, 0:L], xc[:, :, 0:L], ALU.mult).then_inc(s_dx, 1)
                pool.wait_ge(s_dx, HB * h + HB)
                with pool.Fori(0, NS // 2) as pair:
                    n0 = pair * 2
                    for k in range(2):
                        n = n0 + (h * NS + k)
                        pool.wait_ge(s_bs, n + 1)
                        for e in range(CT):
                            pool.wait_ge(s_scan, 2 * n + e + 1)
                            G.tensor_tensor(dBx[:, k, e, :], dx[:, e, :], bs[:, k, :],
                                            ALU.mult).then_inc(s_dbx, 1)
                powers(2 * TB * h, 2 * TB)

            pool.wait_ge(s_op, NB)
            pool.wait_ge(s_wpc, NPREP)
            pool.wait_ge(s_wt, 1)
            ch.link(G.memset(vv[:, :, :, :, :].rearrange("p b t h w -> p (b t h) w"), 0.0))
            G.memset(vv[:, :, :, :, :].rearrange("p b t h w -> p (b t h) w")[:, :, HS:HS + 1],
                     1.0).then_inc(s_pad, 1)
            G.memset(onesr[:, :], 1.0)
            G.memset(zeror[:, :], 0.0).then_inc(s_pad, 1)
            G.memset(kz[:, :, :, :, :].rearrange("p g r j l -> p (g r j l)").bitcast(F32), 0.0).then_inc(s_pad, 1)

            def norm(b):
                powers(TB * b, TB)


            def add_output(b, qt):
                pool.wait_ge(s_yn, b * TB + qt + 1)
                G.tensor_tensor(x[:, TB * b + qt, :], x[:, TB * b + qt, :], yn[:, qt, :], ALU.add).then_inc(s_ya, 1)

            def split_qk(b, w):
                n = 2 * b + w
                pool.wait_ge(s_qr, n + 1)
                if b:
                    pool.wait_ge(s_qk[b - 1][w], 16 * 14)
                G.tensor_copy(qp[:, w, 1, :], qr[:, w, :]).then_inc(s_qp, 1)
                pool.wait_ge(s_qp, 2 * n + 1)
                G.tensor_tensor(qp[:, w, 2, :], qr[:, w, :], qp[:, w, 1, :], ALU.subtract).then_inc(s_qp, 1)

            def split_max(b, q):
                k, n = b % 2, 2 * b + q
                pool.wait_ge(s_mx, (2 * b + q + 1) * HP * TURNS)
                wait(pool, s_mt, n - 3)
                js = slice(HP * q, HP * q + HP)
                src, rest = nm[:, k, :, :, js], nr[:, k, :, :, js]
                first, second, third = (m3[:, k, q, :, :, c, :] for c in range(3))
                ch.link(G.tensor_copy(first, src))
                ch.link(G.tensor_tensor(rest, src, first, ALU.subtract))
                ch.link(G.tensor_copy(second, rest))
                G.tensor_tensor(third, rest, second, ALU.subtract).then_inc(s_m3, 1)

            attend(dict(norm=norm, f_norm=lambda p, b: norm(b), qk_rest=split_qk, split_max=split_max,
                        o_add=add_output), whole)

        @block.scalar
        def _(act):
            S = nc.scalar
            ch = Chain(act, s_ach)
            for dst, src in loads:
                act.dma_start(dst, src).then_inc(s_w, 16)
            S.preload_act_table(ACT.Exp)
            act.wait_ge(s_w, 16 * len(loads))
            S.activation(aneg[:, :, :], aneg[:, :, :], ACT.Exp).then_inc(s_aexp, 1)

            def mamba_input(h, c, k):
                act.wait_ge(s_tr, HB * h + c + 1)
                S.activation(mamba_in(h, c), bank(k), ACT.Copy, scale=w1c[:, 0:1]).then_inc(s_xT, 1)

            for c in range(HB):
                mamba_input(0, c, c)

            def moe_input(h):
                for c in range(HB):
                    b = HB * h + c
                    act.wait_ge(s_tr2, b + 1)
                    S.activation(h2T[:, b, :], bank(4 + c), ACT.Copy, scale=w2c[:, 0:1]).then_inc(s_h2T, 1)

            def logits(h):
                act.wait_ge(s_rt, h + 1)
                S.copy(wtok[:, tiles_of(h), :],
                       ps[:, 7 * h, 0:2 * TB * NE].rearrange("p (t e) -> p t e", e=NE)).then_inc(s_rx, 1)

            for h in range(HB):
                if h:
                    act.wait_ge(s_op, HB * h)
                for c in range(HB):
                    b = HB * h + c
                    banks = ((2, 3, 4, 5), (6, 7, 0, 1))[c]
                    for e in range(CT):
                        act.wait_ge(s_ip, 4 * b + e + 1)
                        S.copy(xip[:, c, e, 4:4 + L], bank(banks[e])).then_inc(s_xi, 1)
                    for e in range(CT):
                        act.wait_ge(s_ip, 4 * b + 2 + e + 1)
                        S.activation(zs[:, e, c * L:c * L + L], bank(banks[2 + e]), ACT.Silu).then_inc(s_zs, 1)
                for c in range(HB):
                    b = HB * h + c
                    for e, (done, src) in enumerate(((s_cv, bank((2, 6)[c])), (s_cd, v[:, c, 1, :]))):
                        act.wait_ge(done, b + 1)
                        S.activation(xc[:, e, c * L:c * L + L], src, ACT.Silu,
                                     bias=convb[:, e:e + 1]).then_inc(s_xc, 1)
                    if c == 0:
                        if h:
                            moe_input(h - 1)
                        else:
                            for k in range(HB):
                                mamba_input(1, k, 4 + k)
                if h:
                    logits(h - 1)
                for c in range(HB):
                    b = HB * h + c
                    act.wait_ge(s_pj, b + 1)
                    S.copy(dts[0:RK, c, :], ps[0:RK, (4, 0)[c], :]).then_inc(s_dts, 1)
                S.preload_act_table_set("natural_log_exp_and_others")
                for c in range(HB):
                    b = HB * h + c
                    act.wait_ge(s_v, b + 1)
                    ch.link(S.activation(u[:, c, :, :], u[:, c, :, :], ACT.Exp))
                    S.activation(u[:, c, :, :], u[:, c, :, :], ACT.Ln, bias=1.0).then_inc(s_u, 1)
                with act.Fori(0, NS // 2) as pair:
                    n0 = pair * 2
                    for k in range(2):
                        n = n0 + (h * NS + k)
                        act.wait_ge(s_bps, n + 1)
                        act.wait_ge(s_dbx, 2 * n + 2)
                        S.copy(bs[:, k, :].rearrange("p (c l) -> p c l", c=HB), bank(6, 2)).then_inc(s_bs, 1)
                        for e in range(CT):
                            act.wait_ge(s_scan, 2 * n + e + 1)
                            if k == e == 0:
                                act.wait_ge(s_dl, HB * h + HB)
                            S.activation(dA[:, k, e, :].rearrange("p (c l) -> p c l", c=HB)[:, :, 1:L],
                                         delta[:, e, :].rearrange("p (c l) -> p c l", c=HB)[:, :, 1:L],
                                         ACT.Exp, scale=aneg[:, e, bass.ds(n0 + k, 1)]).then_inc(s_da, 1)
            for n, (src, _, _, _, dst, _) in enumerate(prep):
                act.wait_ge(s_wp, n + 1)
                if n in (NPREP - 2, NPREP - 6):
                    S.activation(dst.rearrange("p (r d j) -> p j r d", r=2, d=HS),
                                 src.rearrange("p (j r d) -> p j r d", r=2, d=HS), ACT.Copy,
                                 scale=QS if n == NPREP - 2 else 1.0).then_inc(s_wpc, 1)
                else:
                    S.copy(dst, src).then_inc(s_wpc, 1)
            moe_input(HB - 1)
            logits(HB - 1)
            act.wait_ge(s_rs2, 1)
            S.activation(wtok[:, :, :], wtok[:, :, :], ACT.Exp).then_inc(s_re, 1)

            S.preload_act_table(ACT.Silu)
            def turn(b):
                act.wait_ge(s_at, b + 1)
                wait(act, s_av, b)
                S.copy(xA[:, 0:L], bank(7)).then_inc(s_axT, 1)

            def first_part(b, w):
                act.wait_ge(s_aq, 2 * b + w + 1)
                if b:
                    act.wait_ge(s_qk[b - 1][w], 16 * 14)
                S.copy(qp[:, w, 0, :], bank(7)).then_inc(s_qh, 1)

            def vals(b):
                act.wait_ge(s_av, b + 1)
                act.wait_ge(s_pad, 3)
                S.copy(vv[:, b, :, :, 0:HS], bank(7).rearrange("p (t h d) -> p t h d", t=TB, d=HS)).then_inc(s_vv, 1)

            def place_max(b, q):
                n = 2 * b + q
                act.wait_ge(s_mt, n + 1)
                if b:
                    act.wait_ge(s_mp[b - 1][q], 32)
                S.copy(mrow[0:6 * HP, q, :], max_rows).then_inc(s_mr, 1)
                act.wait_ge(s_mr, n + 1)
                for r in range(2):
                    act.dma_start(qq[64 * r + QR:64 * r + MR, b % SL, HP * q:HP * q + HP, :],
                                  mrow[3 * HP * r:3 * HP * (r + 1), q, :]).then_inc(s_mp[b][q], 16)

            def exps(c, q):
                kt = c % TB
                if q == 0:
                    wait(act, s_pv, c - 1)
                act.wait_ge(s_s2, 2 * c + q + 1)
                S.activation(pt[:, c % 2, 2 * q:2 * q + 2, kt * P:L], ps[:, 2 * q:2 * q + 2, kt * P:L],
                             ACT.Exp).then_inc(s_ex, 1)

            def outputs(c):
                if c % TB == TB - 1:
                    b, n = c // UNITS, c // TB
                    act.wait_ge(s_pv, c + 1)
                    wait(act, s_ott, b * TB)
                    S.copy(ot[:, n % 4, :], bank(6)).then_inc(s_ot, 1)

            def f_turn(p, b):
                act.wait_ge(s_ft, p * NB + b + 1)
                S.copy(ffn_input(p, b), bank(6 + p)).then_inc(s_fxT, 1)

            parts = dict(f_turn=f_turn, turn=turn, qk=first_part, vals=vals, place_max=place_max, scores=exps, values=outputs)

            def experts(e0, more):
                for j in range(2 * NB):
                    for f in range(FT):
                        m = e0 * (NB * FT) + (j * FT + f)
                        act.wait_ge(s_g, m + 1)
                        act.wait_ge(s_hm, m + 1)
                        S.activation(sg[:, f % 2, :], bank(f % 2), ACT.Silu).then_inc(s_sg, 1)
                        if not more and (j, f) in in_moe:
                            attend(parts, in_moe[j, f])

            with act.Fori(0, NE // 2 - 1) as pair:
                experts(pair * 2, True)
            experts(NE - 2, False)

            def ffn(p):
                attend(parts, before[p])
                for b in range(NB):
                    for f in range(HT):
                        m = (p * NB + b) * HT + f
                        act.wait_ge(s_fg, m + 1)
                        wait(act, s_fh, m - 1)
                        S.activation(fsg[:, m % 2, :], bank(m % 2), ACT.Silu, scale=DQ).then_inc(s_fs, 1)
                        attend(parts, in_ffn[p].get((b, f), []))

            ffn(0)

            S.preload_act_table(ACT.Exp)
            act.wait_ge(s_pad, 3)
            attend(parts, steps)
            ffn(1)

        @block.vector
        def _(dve):
            V = nc.vector
            ch = Chain(dve, s_dch)
            count = {"var": 0}

            def moments(src, b, n=TB):
                t0 = TB * b
                for j in range(n):
                    last = V.bn_stats(stats[:, t0 + j, :], src[:, t0 + j, :])
                ch.link(last)
                for j in range(n):
                    last = V.bn_aggr(mv[:, t0 + j, :], stats[:, t0 + j, :])
                ch.link(last)

            def power(n):
                count["var"] += 1
                n.then_inc(s_var, 1)
                dve.wait_ge(s_rstd, count["var"])

            def normalise(dst, src, t, rcol):
                return V.tensor_scalar(dst, src, mv[:, t, 0:1], rcol, ALU.subtract, ALU.mult)

            for c in range(HB):
                V.memset(xip[:, c, :, 0:4], 0.0)

            def input_norm(h):
                sl = tiles_of(h)
                for c in range(HB):
                    dve.wait_ge(s_x[HB * h + c], 16)
                moments(x, HB * h, 2 * TB)
                power(V.tensor_scalar(small[:, 1, sl], mv[:, sl, 1], EPS, None, ALU.add))
                ch.link(V.tensor_tensor(small[:, 3, sl], small[:, 2, sl], small[:, 2, sl], ALU.mult))
                ch.link(V.tensor_tensor(small[:, 3, sl], small[:, 3, sl], mv[:, sl, 1], ALU.mult))
                V.tensor_copy(small[:, 0, sl], small[:, 2, sl])
                ch.link(V.tensor_scalar(small[:, 1, sl], small[:, 3, sl], EPS, None, ALU.add))
                count["var"] += 1
                dve.sem_inc(s_var, 1)
                for t in range(2 * TB * h, 2 * TB * h + 2 * TB):
                    last = normalise(r[:, t, :], x[:, t, :], t, small[:, 0, t:t + 1])
                ch.link(last)
                dve.wait_ge(s_rstd, count["var"])
                for c in range(HB):
                    b = HB * h + c
                    if h:
                        dve.wait_ge(s_tr, b - 1)
                    for j in range(TB):
                        t = TB * b + j
                        last = V.tensor_scalar(nb[:, c, j, :], r[:, t, :], small[:, 2, t:t + 1], None, ALU.mult)
                    last.then_inc(s_nb, 1)

            input_norm(0)
            dve.wait_ge(s_const, 2)
            dve.wait_ge(s_w, 16 * len(loads))
            dve.wait_ge(s_aexp, 1)
            V.tensor_scalar(aneg[:, :, :], aneg[:, :, :], -1.0, None, ALU.mult)
            V.tensor_copy(identb[:], ident[:])
            V.tensor_copy(sel[:, :, :], selr[:, :].unsqueeze(2).to_broadcast([P, 2 * NS, P]))
            for e in range(CT):
                if e == 0:
                    for k in range(DC):
                        V.tensor_scalar(convd[:, k, :], ident[:], convw[:, e, k:k + 1], None, ALU.mult)
                last = V.tensor_scalar(dskd[:, e, :], ident[:], dsk[:, e:e + 1], None, ALU.mult)
            last.then_inc(s_dconst, 1)
            def split_input(b):
                dve.wait_ge(s_h2T, b + 1)
                ch.link(V.tensor_copy(x_hi[:, b, :], h2T[:, b, :]))
                V.tensor_tensor(x_lo[:, b, :], h2T[:, b, :], x_hi[:, b, :].bitcast(F32),
                                ALU.subtract).then_inc(s_hs, 1)

            def split_expert(e, k):
                dve.wait_ge(s_mw[k], (e - k) * 24 + 48)
                w, hi, lo = (a[:, k, 0:2, :].rearrange("p w f -> p (w f)") for a in (moew, w_hi, w_lo))
                V.tensor_copy(hi, w).then_inc(s_wh, 1)
                dve.wait_ge(s_wh, e + 1)
                V.tensor_tensor(lo, w, hi.bitcast(F32), ALU.subtract).then_inc(s_ws, 1)

            input_norm(1)

            for h in range(HB):
                for c in range(HB):
                    b = HB * h + c
                    dve.wait_ge(s_xi, 2 * b + 2)
                    acc = v[:, c, 1, :]
                    V.tensor_scalar(acc, xip[:, c, 1, 1:1 + L], convw[:, 1, 0:1], None, ALU.mult).then_inc(s_cc, 1)
                    for k in range(1, DC):
                        dve.wait_ge(s_cc, (DC - 1) * b + k)
                        V.scalar_tensor_tensor(acc, xip[:, c, 1, 1 + k:1 + k + L], convw[:, 1, k:k + 1], acc,
                                               ALU.mult, ALU.add).then_inc(s_cd if k == DC - 1 else s_cc, 1)
                for c in range(HB):
                    b = HB * h + c
                    cs = slice(c * L, c * L + L)
                    rows = slice(RK, RK + 2 * NS)
                    src = ps[rows, (4, 0)[c], :]
                    dve.wait_ge(s_pj, b + 1)
                    ch.link(V.tensor_copy(bcp[rows, c, 0, :], src))
                    ch.link(V.tensor_tensor(bcr[rows, c, :], src, bcp[rows, c, 0, :], ALU.subtract))
                    V.tensor_copy(bc3[0:2 * NS, cs], bcp[rows, c, 0, :])
                    ch.link(V.tensor_copy(bcp[rows, c, 1, :], bcr[rows, c, :]))
                    V.tensor_copy(bc3[2 * NS:4 * NS, cs], bcp[rows, c, 1, :])
                    V.tensor_tensor(bc3[rows, cs], bcr[rows, c, :], bcp[rows, c, 1, :],
                                    ALU.subtract).then_inc(s_bc3, 1)
                for c in range(HB):
                    b = HB * h + c
                    for e in range(CT):
                        dve.wait_ge(s_dtp, 2 * b + e + 1)
                        last = V.tensor_scalar(v[:, c, e, :], bank((2, 6)[c] + e), dtb[:, e:e + 1], None, ALU.add)
                    ch.link(last)
                    V.scalar_tensor_tensor(u[:, c, :, :], v[:, c, :, :], -1.0, v[:, c, :, :],
                                           ALU.mult, ALU.min).then_inc(s_v, 1)
                for c in range(HB):
                    b = HB * h + c
                    dve.wait_ge(s_u, b + 1)
                    V.scalar_tensor_tensor(delta[:, :, c * L:c * L + L], v[:, c, :, :], 0.0, u[:, c, :, :],
                                           ALU.max, ALU.add).then_inc(s_dl, 1)
                dve.wait_ge(s_dl, HB * h + HB)
                V.tensor_tensor(dx[:, :, L:HL], delta[:, :, L:HL], xc[:, :, L:HL], ALU.mult).then_inc(s_dx, 1)
                for k in range(2):
                    last = V.memset(dA[:, k, :, :].rearrange("p e (c l) -> p (e c) l", c=HB)[:, :, 0:1], 0.0)
                ch.link(last)
                with dve.Fori(0, NS // 2) as pair:
                    n0 = pair * 2
                    for k in range(2):
                        n = n0 + (h * NS + k)
                        for e in range(CT):
                            dve.wait_ge(s_da, 2 * n + e + 1)
                            dve.wait_ge(s_dbx, 2 * n + e + 5)
                            dve.wait_ge(s_hc, 2 * n + e + 1)
                            V.tensor_tensor_scan(hst[:, e, :], dA[:, k, e, :], dBx[:, k, e, :], 0.0,
                                                 ALU.mult, ALU.add).then_inc(s_scan, 1)
                        dve.wait_ge(s_cps, n + 1)
                        for e in range(CT):
                            dve.wait_ge(s_scan, 2 * n + e + 5)
                            dve.wait_ge(s_ys, 2 * n + e + 1)
                            V.tensor_tensor(hC[:, k, e, :].rearrange("p (c l) -> p c l", c=HB),
                                            hst[:, e, :].rearrange("p (c l) -> p c l", c=HB),
                                            bank(4, 2), ALU.mult).then_inc(s_hc, 1)
                if h == HB - 1:
                    split_expert(0, 0)
                for e in range(CT):
                    dve.wait_ge(s_ys, 2 * NS * (h + 1) + e + 3)
                    V.tensor_tensor(zs[:, e, :].rearrange("p (c l) -> p c l", c=HB), bank(2 * e, 2),
                                    zs[:, e, :].rearrange("p (c l) -> p c l", c=HB), ALU.mult).then_inc(s_yg, 1)
                for c in range(HB):
                    b = HB * h + c
                    dve.wait_ge(s_op, b + 1)
                    V.tensor_tensor(r[:, tiles(b), :], bank(4 + c).rearrange("p (j d) -> p j d", j=TB),
                                    r[:, tiles(b), :], ALU.add).then_inc(s_r, 1)
                dve.wait_ge(s_r, HB * h + HB)
                sl = tiles_of(h)
                moments(r, HB * h, 2 * TB)
                ch.link(V.tensor_tensor(small[:, 3, sl], mv[:, sl, 0], mv[:, sl, 0], ALU.mult))
                ch.link(V.tensor_tensor(small[:, 3, sl], small[:, 3, sl], mv[:, sl, 1], ALU.add))
                power(V.tensor_scalar(small[:, 1, sl], small[:, 3, sl], EPS, None, ALU.add))
                for c in range(HB):
                    for j in range(TB):
                        t = TB * (HB * h + c) + j
                        last = V.tensor_scalar(nb[:, c, j, :], r[:, t, :], small[:, 2, t:t + 1], None, ALU.mult)
                    last.then_inc(s_h2, 1)
            split_input(0)
            split_input(1)
            dve.wait_ge(s_rx, HB)
            ch.link(V.tensor_reduce(m8[:, :], wtok[:, :, :], AX, ALU.max))
            V.tensor_tensor(wtok[:, :, :], wtok[:, :, :], m8[:, :].unsqueeze(2).to_broadcast([P, NT, NE]),
                            ALU.subtract).then_inc(s_rs2, 1)
            split_input(2)
            dve.wait_ge(s_re, 1)
            ch.link(V.tensor_reduce(m8[:, :], wtok[:, :, :], AX, ALU.add))
            ch.link(V.reciprocal(m8[:, :], m8[:, :]))
            ch.link(V.tensor_tensor(wtok[:, :, :], wtok[:, :, :], m8[:, :].unsqueeze(2).to_broadcast([P, NT, NE]),
                                    ALU.mult))
            for t in range(NT):
                last = V.max(rmax[:, t, :], wtok[:, t, :])
            ch.link(last)
            for t in range(NT):
                last = V.max_index(ridx[:, t, :], rmax[:, t, :], wtok[:, t, :])
            ch.link(last)
            ch.link(V.tensor_copy(rmax[:, :, 0:2], ridx[:, :, 0:2]))
            io = iota8[:, :].unsqueeze(1).to_broadcast([P, NT, NE])
            V.tensor_tensor(req[:, 0], io, rmax[:, :, 0:1].to_broadcast([P, NT, NE]), ALU.is_equal)
            ch.link(V.tensor_tensor(req[:, 1], io, rmax[:, :, 1:2].to_broadcast([P, NT, NE]), ALU.is_equal))
            ch.link(V.tensor_tensor(req[:, 0], req[:, 0], req[:, 1], ALU.add))
            V.tensor_tensor(wtok[:, :, :], wtok[:, :, :], req[:, 0], ALU.mult).then_inc(s_wt, 1)

            split_input(3)
            dve.wait_ge(s_wt, 1)

            def experts(e0, more):
                def hidden(j, f):
                    m = e0 * (NB * FT) + (j * FT + f)
                    dve.wait_ge(s_sg, m + 1)
                    dve.wait_ge(s_u2, m + 1)
                    if f == 0:
                        dve.wait_ge(s_dn, e0 * NB + j + 7)
                    V.tensor_tensor(hh[:, j % 2, f, :], sg[:, f % 2, :], bank(2 + f % 2), ALU.mult).then_inc(s_hm, 1)

                def add(j):
                    b = j % NB
                    dve.wait_ge(s_dn, e0 * NB + j + 9)
                    for t in range(TB):
                        last = V.scalar_tensor_tensor(r[:, TB * b + t, :], ps[:, 4 + j % 2, t * P:t * P + P],
                                                      wtok[:, TB * b + t, bass.ds(e0 + j // NB, 1)],
                                                      r[:, TB * b + t, :], ALU.mult, ALU.add)
                    last.then_inc(s_acc, 1)

                for j in range(2 * NB):
                    for f in range(FT):
                        hidden(j, f)
                        if f == 1 and j:
                            add(j - 1)
                        if not more and (j, f) in in_moe:
                            attend(parts, in_moe[j, f])
                    if j % NB == 1:
                        if j < NB:
                            split_expert(e0 + 1, 1)
                        elif more:
                            split_expert(e0 + 2, 0)
                add(2 * NB - 1)


            ln_n = [0]

            def layernorm_start(b):
                sl = slice(TB * b, TB * b + TB)
                moments(x, b)
                count["var"] += 1
                V.tensor_scalar(small[:, 1, sl], mv[:, sl, 1], EPS, None, ALU.add).then_inc(s_var, 1)

            def layernorm_end(b, k, done):
                dve.wait_ge(s_rstd, count["var"])
                for j in range(TB):
                    t = TB * b + j
                    last = normalise(nb[:, k, j, :], x[:, t, :], t, small[:, 2, t:t + 1])
                last.then_inc(done, 1)

            turned = [(s_tr2, NB)]

            def norm(b):
                dve.wait_ge(s_fa, b + 1)
                layernorm_start(b)

            def f_norm(p, b):
                if p == 0:
                    dve.wait_ge(s_acc, 2 + (NE - 1) * NB + b + 1)
                    ch.link(V.tensor_tensor(x[:, tiles(b), :], x[:, tiles(b), :], r[:, tiles(b), :], ALU.add))
                else:
                    dve.wait_ge(s_ya, TB * (b + 1))
                layernorm_start(b)

            def normalise_block(b):
                dve.wait_ge(*turned[0])
                layernorm_end(b, b % 2, s_an)
                turned[0] = (s_at, b + 1)

            def f_normalise(p, b):
                dve.wait_ge(*turned[0])
                layernorm_end(b, b % 2, s_fn)
                turned[0] = (s_ft, p * NB + b + 1)

            def rest_part(b, w):
                dve.wait_ge(s_qh, 2 * b + w + 1)
                wait(dve, s_qp, 2 * (2 * b + w - 2) + 2)
                V.tensor_tensor(qr[:, w, :], bank(7), qp[:, w, 0, :], ALU.subtract).then_inc(s_qr, 1)

            def maxima(b, j, n):
                m = (b * PAIRS + j) * TURNS + n
                dve.wait_ge(s_s1, m + 1)
                if b >= 2 and j == n == 0:
                    dve.wait_ge(s_m3, 2 * b - 2)
                wait(dve, s_mx, m - 1)
                for r, qt, col in turns[n]:
                    w = (qt + 1) * P
                    last = V.tensor_tensor_reduce(out=junk[:, m % 2, col:col + w], in0=ps[:, 4 + m % 2, col:col + w],
                                                  in1=cmask[:, L - w:L], scale=-1.0, scalar=3.0e38,
                                                  op0=ALU.add, op1=ALU.min,
                                                  accum_out=nm[:, b % 2, qt, r, j:j + 1])
                last.then_inc(s_mx, 1)

            def finish(b, qt):
                n = b * TB + qt + 1
                dve.wait_ge(s_ott, n)
                o = bank(o_bank(b, qt)).rearrange("p (h w) -> p h w", w=32)
                V.reciprocal(rs[:, qt, :], o[:, :, HS]).then_inc(s_rs, 1)
                dve.wait_ge(s_rs, n)
                wait(dve, s_ya, n - TB)
                V.tensor_tensor(yn[:, qt, :].rearrange("p (h d) -> p h d", d=HS), o[:, :, 0:HS],
                                rs[:, qt, :].unsqueeze(2).to_broadcast([P, NH, HS]), ALU.mult).then_inc(s_yn, 1)

            parts = dict(norm=norm, normalise=normalise_block, f_norm=f_norm, f_normalise=f_normalise, qk_rest=rest_part, maxima=maxima, o_add=finish)

            with dve.Fori(0, NE // 2 - 1) as pair:
                experts(pair * 2, True)
            experts(NE - 2, False)

            def ffn(p):
                def hid(b, f):
                    m = (p * NB + b) * HT + f
                    dve.wait_ge(s_fs, m + 1)
                    dve.wait_ge(s_fu, m + 1)
                    if f == 0:
                        wait(dve, s_fd, p * NB + b - 1)
                    V.tensor_tensor(fhh[:, b % 2, f, :], fsg[:, m % 2, :], bank(2 + m % 2), ALU.mult).then_inc(s_fh, 1)

                def add(b):
                    q = p * NB + b
                    dve.wait_ge(s_fd, q + 1)
                    V.scalar_tensor_tensor(x[:, tiles(b), :], bank(4 + b % 2).rearrange("p (j d) -> p j d", j=TB),
                                           DQ * DQ, x[:, tiles(b), :], ALU.mult, ALU.add).then_inc(s_fa, 1)

                attend(parts, before[p])
                for b in range(NB):
                    for f in range(HT):
                        hid(b, f)
                        if f == 1 and b:
                            add(b - 1)
                        attend(parts, in_ffn[p].get((b, f), []))
                add(NB - 1)

            ffn(0)

            dve.wait_ge(s_fa, NB)
            attend(parts, steps)
            ffn(1)

        @block.tensor
        def _(pe):
            T = nc.tensor

            def mm(o, l, rr, start=True, stop=True):
                return T.matmul(o, l, rr, start=start, stop=stop)

            pe.wait_ge(s_const, 2)

            def turn_input(h, c, k):
                pe.wait_ge(s_nb, HB * h + c + 1)
                for j in range(TB):
                    last = T.transpose(ps[:, k, j * P:j * P + P], nb[:, c, j, :], ident[:])
                last.then_inc(s_tr, 1)

            for c in range(HB):
                turn_input(0, c, c)

            def prepare():
                pe.wait_ge(s_wflt, 1)
                pe.wait_ge(s_aw, 16 * 9)
                for n, (o, l, rr, turned, _, need) in enumerate(prep):
                    wait(pe, s_wpc, max(need, n - 3))
                    (T.transpose(o, l, rr) if turned else mm(o, l, rr)).then_inc(s_wp, 1)
                pe.wait_ge(s_wpc, NPREP)

            def turn_h2(h):
                for c in range(HB):
                    b = HB * h + c
                    pe.wait_ge(s_h2, b + 1)
                    for j in range(TB):
                        last = T.transpose(ps[:, 4 + c, j * P:j * P + P], nb[:, c, j, :], ident[:])
                    last.then_inc(s_tr2, 1)

            def router(h):
                pe.wait_ge(s_h2T, HB * h + HB)
                for c in range(HB):
                    for j in range(TB):
                        t = c * TB + j
                        last = mm(ps[:, 7 * h, t * NE:t * NE + NE], h2T[:, HB * h + c, j * P:j * P + P], rw[:])
                last.then_inc(s_rt, 1)

            pe.wait_ge(s_w, 16 * len(loads))
            pe.wait_ge(s_dconst, 1)
            for h in range(HB):
                if h:
                    pe.wait_ge(s_r, HB * h)
                pe.wait_ge(s_xT, HB * h + HB)
                for c in range(HB):
                    banks = ((2, 3, 4, 5), (6, 7, 0, 1))[c]
                    for m in range(4):
                        mm(bank(banks[m]), ipw[:, m * P:m * P + P], mamba_in(h, c)).then_inc(s_ip, 1)
                for c in range(HB):
                    b = HB * h + c
                    pe.wait_ge(s_xi, 2 * b + 2)
                    for k in range(DC):
                        last = mm(bank((2, 6)[c]), convd[:, k, :], xip[:, c, 0, 1 + k:1 + k + L],
                                  start=(k == 0), stop=(k == DC - 1))
                    last.then_inc(s_cv, 1)
                    if c == 0:
                        pe.wait_ge(s_zs, 2 * b + 2)
                        if h:
                            turn_h2(h - 1)
                        else:
                            for k in range(HB):
                                turn_input(1, k, 4 + k)
                if h == 0:
                    pe.wait_ge(s_xT, NB)
                if h:
                    pe.wait_ge(s_zs, 2 * HB * (h + 1))
                    router(h - 1)
                for c in range(HB):
                    b = HB * h + c
                    pe.wait_ge(s_zs, 2 * b + 2)
                    pe.wait_ge(s_xc, 2 * b + 2)
                    if h and c:
                        pe.wait_ge(s_rx, h)
                    for e in range(CT):
                        last = mm(ps[0:RK + 2 * NS, (4, 0)[c], :], xpw[:, e, :], xc[:, e, c * L:c * L + L],
                                  start=(e == 0), stop=(e == CT - 1))
                    last.then_inc(s_pj, 1)
                for c in range(HB):
                    b = HB * h + c
                    pe.wait_ge(s_dts, b + 1)
                    for e in range(CT):
                        mm(bank((2, 6)[c] + e), dtw[0:RK, e * P:e * P + P], dts[0:RK, c, :]).then_inc(s_dtp, 1)
                pe.wait_ge(s_v, HB * h + HB)
                pe.wait_ge(s_bc3, HB * h + HB)
                def ysum(k, e, stop):
                    for c in range(HB):
                        last = mm(bank(2 * e + c), ident[:], hC[:, k, e, c * L:c * L + L], start=False, stop=stop)
                    last.then_inc(s_ys, 1)

                def row(n):
                    return sel[0:96, bass.ds(n, 1), :].rearrange("p o q -> p (o q)")

                def spread_b(n):
                    pe.wait_ge(s_bs, n + h * NS)
                    for c in range(HB):
                        last = mm(bank(6 + c), row(n), bc3[0:96, c * L:c * L + L])
                    last.then_inc(s_bps, 1)

                def state(n, k):
                    gn = n + h * NS
                    pe.wait_ge(s_hc, 2 * gn + 2)
                    for c in range(HB):
                        last = mm(bank(4 + c), row(n + NS), bc3[0:96, c * L:c * L + L])
                    last.then_inc(s_cps, 1)
                    for e in range(CT):
                        ysum(1 - k, e, False)

                for bk, r0, done in ((6, 0, s_bps), (4, NS, s_cps)):
                    for c in range(HB):
                        last = mm(bank(bk + c), sel[0:96, r0, :], bc3[0:96, c * L:c * L + L])
                    last.then_inc(done, 1)
                for e in range(CT):
                    for c in range(HB):
                        mm(bank(2 * e + c), dskd[:, e, :], xc[:, e, c * L:c * L + L], stop=False)
                spread_b(1)
                spread_b(2)
                state(1, 1)
                with pe.Fori(1, NS // 2 - 1) as pair:
                    for k in range(2):
                        spread_b(pair * 2 + k + 1)
                        state(pair * 2 + k, k)
                spread_b(NS - 1)
                state(NS - 2, 0)
                state(NS - 1, 1)
                pe.wait_ge(s_hc, 2 * NS * (h + 1) + 2)
                for e in range(CT):
                    ysum(1, e, True)
                pe.wait_ge(s_yg, 2 * h + 2)
                for c in range(HB):
                    for j in range(TB):
                        for e in range(CT):
                            last = mm(ps[:, 4 + c, j * P:j * P + P], zs[:, e, c * L + j * P:c * L + j * P + P],
                                      opw[:, e, :], start=(e == 0), stop=(e == CT - 1))
                    last.then_inc(s_op, 1)
            prepare()
            pe.wait_ge(s_r, NB)
            turn_h2(HB - 1)
            router(HB - 1)

            def experts(e0, more):
                def gate_up(j, f):
                    k, b = j // NB, j % NB
                    m = e0 * (NB * FT) + (j * FT + f)
                    fs = slice(f * P, f * P + P)
                    if k == f == 0:
                        pe.wait_ge(s_hs, b + 1)
                    pe.wait_ge(s_hm, m + 1)
                    for i, done in enumerate((s_g, s_u2)):
                        o = bank(2 * i + f % 2)
                        mm(o, w_hi[:, k, i, fs], x_hi[:, b, :], True, False)
                        mm(o, w_hi[:, k, i, fs], x_lo[:, b, :], False, False)
                        mm(o, w_lo[:, k, i, fs], x_hi[:, b, :], False, True).then_inc(done, 1)

                def down(j):
                    k = j // NB
                    pe.wait_ge(s_hm, e0 * (NB * FT) + (j * FT + FT + 2))
                    pe.wait_ge(s_acc, e0 * NB + j + 1)
                    for t in range(TB):
                        for f in range(FT):
                            last = mm(ps[:, 4 + j % 2, t * P:t * P + P], hh[:, j % 2, f, t * P:t * P + P],
                                      moew[:, k, 2, f * P:f * P + P], start=(f == 0), stop=(f == FT - 1))
                    last.then_inc(s_dn, 1)

                for j in range(2 * NB):
                    if j % NB == 0:
                        pe.wait_ge(s_ws, e0 + (j // NB + 1))
                    for f in range(FT):
                        gate_up(j, f)
                        if f == 0 and j:
                            down(j - 1)
                        if not more and (j, f) in in_moe:
                            attend(parts, in_moe[j, f])
                down(2 * NB - 1)

            bank7_read = [[]]

            def bank7(reader, count):
                for s, n in bank7_read[0]:
                    pe.wait_ge(s, n)
                bank7_read[0] = list(zip(reader, count))

            def turn(b):
                pe.wait_ge(s_an, b + 1)
                bank7((s_axT,), (b + 1,))
                for j in range(TB):
                    last = T.transpose(ps[:, 7, j * P:j * P + P], nb[:, b % 2, j, :], ident[:])
                last.then_inc(s_at, 1)

            def qk(b, w):
                bank7((s_qh, s_qr), (2 * b + w + 1,) * 2)
                pe.wait_ge(s_axT, b + 1)
                mm(bank(7), (wqq, mT)[w][:], xA[:, 0:L]).then_inc(s_aq, 1)

            def vals(b):
                bank7((s_vv,), (b + 1,))
                for j in range(TB):
                    last = mm(ps[:, 7, j * P:j * P + P], xA[:, j * P:j * P + P], vx[:])
                last.then_inc(s_av, 1)

            def maxima(b, j, n):
                if j == n == 0:
                    for w in range(2):
                        pe.wait_ge(s_qk[b][w], 16 * 14)
                    pe.wait_ge(s_qz[b], 32)
                m = (b * PAIRS + j) * TURNS + n
                wait(pe, s_mx, m - 1)
                for r, qt, col in turns[n]:
                    w = (qt + 1) * P
                    last = mm(ps[:, 4 + m % 2, col:col + w], qq[:, b % SL, j, qt * P:qt * P + P],
                              kz[:, b % SL, r, j, 0:w])
                last.then_inc(s_s1, 1)

            def place_max(b, q):
                n = 2 * b + q
                pe.wait_ge(s_m3, n + 1)
                bank7((s_mr,), (n + 1,))
                for qt in range(TB):
                    last = T.transpose(max_rows[:, qt * P:qt * P + P],
                                       m3[:, b % 2, q, qt, :, :, :].rearrange("p r c j -> p (r c j)"), identb[:])
                last.then_inc(s_mt, 1)

            def scores(c, q):
                b, u, kt = c // UNITS, c // TB % 4, c % TB
                if c % (UNITS // 2) == 0 and q == 0:
                    pe.wait_ge(s_mp[b][u // 2], 32)
                wait(pe, s_ex, 2 * (c - 1) + q + 1)
                for r in range(2):
                    mm(ps[:, 2 * q + r, kt * P:L], kz[:, b % SL, r, 2 * u + q, kt * P:kt * P + P],
                       qq[:, b % SL, 2 * u + q, kt * P:L], stop=False)
                for r in range(2):
                    last = mm(ps[:, 2 * q + r, kt * P:kt * P + P], identb[:], kmask[:], start=False)
                last.then_inc(s_s2, 1)

            def values(c):
                b, u, kt = c // UNITS, c // TB % 4, c % TB
                pe.wait_ge(s_ex, 2 * c + 2)
                if kt == 0:
                    wait(pe, s_ot, c // TB)
                for g in range(4):
                    last = mm(ps[32 * g:32 * g + 32, 6, kt * P:L], vv[:, b, kt, 4 * u + g, :],
                              pt[:, c % 2, g, kt * P:L], start=(kt == 0), stop=(kt == TB - 1))
                last.then_inc(s_pv, 1)

            def finish(b, qt):
                pe.wait_ge(s_ot, 4 * (b + 1))
                if o_bank(b, qt) == 7:
                    bank7((s_yn,), (b * TB + qt + 1,))
                elif qt > 1:
                    pe.wait_ge(s_yn, b * TB + qt - 1)
                for u in range(4):
                    last = T.transpose(ps[:, o_bank(b, qt), u * P:u * P + P], ot[:, u, qt * P:qt * P + P], ident[:])
                last.then_inc(s_ott, 1)

            def f_turn(p, b):
                pe.wait_ge(s_fn, p * NB + b + 1)
                if p:
                    bank7((s_fxT,), (p * NB + b + 1,))
                else:
                    wait(pe, s_fxT, b)
                for j in range(TB):
                    last = T.transpose(ps[:, 6 + p, j * P:j * P + P], nb[:, b % 2, j, :], ident[:])
                last.then_inc(s_ft, 1)

            parts = dict(f_turn=f_turn, turn=turn, qk=qk, vals=vals, maxima=maxima, place_max=place_max, scores=scores,
                         values=values, o_turn=finish)

            with pe.Fori(0, NE // 2 - 1) as pair:
                experts(pair * 2, True)
            experts(NE - 2, False)
            pe.wait_ge(s_hm, 2 + NE * NB * FT)

            def ffn(p):
                def gate_up(b, f):
                    m = (p * NB + b) * HT + f
                    wait(pe, s_fh, m - 1)
                    mm(bank(m % 2), wgT[:, f * P:f * P + P], ffn_input(p, b)).then_inc(s_fg, 1)
                    mm(bank(2 + m % 2), wuT[:, f * P:f * P + P], ffn_input(p, b)).then_inc(s_fu, 1)

                def down(b):
                    q = p * NB + b
                    pe.wait_ge(s_fh, q * HT + HT)
                    if q == 0:
                        pe.wait_ge(s_acc, 2 + NE * NB)
                    wait(pe, s_fa, q - 1)
                    for t in range(TB):
                        for f in range(HT):
                            last = mm(ps[:, 4 + b % 2, t * P:t * P + P], fhh[:, b % 2, f, t * P:t * P + P],
                                      wdT[:, f, :], start=(f == 0), stop=(f == HT - 1))
                    last.then_inc(s_fd, 1)

                attend(parts, before[p])
                for b in range(NB):
                    pe.wait_ge(s_fxT, p * NB + b + 1)
                    for f in range(HT):
                        gate_up(b, f)
                        if f == 0 and b:
                            down(b - 1)
                        attend(parts, in_ffn[p].get((b, f), []))
                down(NB - 1)

            ffn(0)

            pe.wait_ge(s_fa, NB)
            pe.wait_ge(s_pad, 3)
            pe.wait_ge(s_ones, 16 * 2 * SL)
            attend(parts, steps)
            ffn(1)


_INS = ["hidden_states", "rms1_w", "rms2_w", "in_proj_w", "conv_w", "conv_b", "x_proj_w", "dt_proj_w",
        "dt_proj_b", "A_log", "D_skip", "out_proj_w", "router_w", "Wg", "Wu", "Wd"]
_INS = ["L0_attn_a_" + n for n in _INS] + ["L0_attn_b_" + n for n in
                                           ("W_dq", "W_uq", "W_dkv", "W_uk", "W_uv", "W_o")]
_INS += ["L0_ffn_" + n for n in ("w_gate", "w_up", "w_down")]
_SHAPE = (4, 512, 128)


def kernel(**inputs):
    import numpy as _np
    import concourse.bacc as _bacc
    from concourse import mybir as _mybir
    from concourse.bass_utils import run_bass_kernel_spmd as _run

    nc = _bacc.Bacc("TRN2", target_bir_lowering=False, num_devices=1)
    arrays, args = {}, []
    for name in _INS:
        a = _np.ascontiguousarray(inputs[name])
        arrays[f"in_{name}"] = a
        args.append(nc.dram_tensor(f"in_{name}", a.shape, _mybir.dt.from_np(a.dtype), kind="ExternalInput").ap())
    out = nc.dram_tensor("out_0", _SHAPE, _mybir.dt.float32, kind="ExternalOutput").ap()
    build(nc, *args, out)
    r = _run(nc, [arrays], core_ids=[0])
    return r.results[0]["out_0"]
```
